# Optimizing a Trainium2 kernel written in Bass

```python
import numpy as np
import jax
import jax.numpy as jnp

def _softmax(x, axis=-1):
    return jax.nn.softmax(x, axis=axis)

def _gelu(x):
    return jax.nn.gelu(x, approximate=True)

def _silu(x):
    return jax.nn.silu(x)

def _sigmoid(x):
    return jax.nn.sigmoid(x)

def _layernorm(x, axis=-1, eps=1e-05):
    m = jnp.mean(x, axis=axis, keepdims=True)
    v = jnp.var(x, axis=axis, keepdims=True)
    return (x - m) / jnp.sqrt(v + eps)

def _scatter_add(tgt, idx, src, axis=0):
    return tgt.at[idx].add(src)

def _segment_sum(src, seg, n):
    return jax.ops.segment_sum(src, seg, n)
kernel_name = 'mk_gnn_resnorm_d4_gnn_r64_58393f'

def setup_inputs(seed: int=0):
    np.random.seed(seed)
    _w = jnp.asarray

    def _rec_inputs():
        import jax
        import jax.numpy as jnp
        _gk = jax.random.key(seed)
        x = -0.0005121 + 1.001 * jax.random.normal(jax.random.fold_in(_gk, 1), (100000, 64), jnp.float32)
        src = jax.random.randint(jax.random.fold_in(_gk, 2), (25000,), 0, 100000, jnp.int32)
        dst = jnp.minimum((100000 * jax.random.uniform(jax.random.fold_in(_gk, 3), (25000,)) ** 2.0).astype(jnp.int32), 99999)
        _o = jnp.argsort(dst, stable=True)
        src = src[_o]
        dst = dst[_o]
        edge_attr_64 = 4.59472e-05 + 1.00006 * jax.random.normal(jax.random.fold_in(_gk, 12), (25000, 64), jnp.float32)
        return (x, src, dst, edge_attr_64)
    x, src, dst, edge_attr_64 = _rec_inputs()

    def _L0_gnn_setup():
        import jax, jax.numpy as jnp
        import numpy as np
        N_NODES = 50000
        N_EDGES = 12500
        HID = 64
        ALPHA = 0.5
        EPS = 0.1
        key = jax.random.key(seed)
        k1, k2, k3, k4 = jax.random.split(key, 4)
        h = jax.random.normal(k1, (N_NODES, HID), dtype=jnp.float32)
        gate_w = jax.random.normal(k2, (2 * HID, 1), dtype=jnp.float32) * 0.05
        gate_b = jnp.zeros((1,), dtype=jnp.float32)
        src = jax.random.randint(k3, (N_EDGES,), 0, N_NODES, dtype=jnp.int64 if jax.config.jax_enable_x64 else jnp.int32)
        dst = jax.random.randint(k4, (N_EDGES,), 0, N_NODES, dtype=jnp.int64 if jax.config.jax_enable_x64 else jnp.int32)
        return {'h': h, 'gate_w': gate_w, 'gate_b': gate_b, 'src': src, 'dst': dst}
    _L0_gnn_all = _L0_gnn_setup()
    _L0_gnn_in = {k: v for k, v in _L0_gnn_all.items() if k in ('gate_w', 'gate_b')}
    del _L0_gnn_all

    def _L1_gnn_setup():
        import jax, jax.numpy as jnp
        import numpy as np
        N_NODES = 50000
        N_EDGES = 12500

        def gat_layer(x, src, dst, W, a_s, a_d, b, concat):
            N = x.shape[0]
            H, C = a_s.shape
            h = (x @ W).reshape(N, H, C)
            alpha_s = jnp.einsum('nhc,hc->nh', h, a_s)
            alpha_d = jnp.einsum('nhc,hc->nh', h, a_d)
            logits = jax.nn.leaky_relu(alpha_s[src] + alpha_d[dst], 0.2)
            m = jax.ops.segment_max(logits, dst, num_segments=N)
            e = jnp.exp(logits - m[dst])
            s = jax.ops.segment_sum(e, dst, num_segments=N)
            a = e / s[dst]
            out = jax.ops.segment_sum(h[src] * a[:, :, None], dst, num_segments=N)
            out = out.reshape(N, H * C) if concat else out.mean(axis=1)
            return out + b
        key = jax.random.key(seed)
        ks = jax.random.split(key, 10)
        in_c, hid, heads, out_c = (64, 64, 2, 64)
        x = jax.random.normal(ks[0], (N_NODES, in_c), dtype=jnp.float32)
        edge_index = jax.random.randint(ks[1], (2, N_EDGES), 0, N_NODES, dtype=jnp.int64)
        sc = lambda f: 1.0 / np.sqrt(f)
        W1 = jax.random.normal(ks[2], (in_c, heads * hid), dtype=jnp.float32) * sc(in_c)
        as1 = jax.random.normal(ks[3], (heads, hid), dtype=jnp.float32) * sc(hid)
        ad1 = jax.random.normal(ks[4], (heads, hid), dtype=jnp.float32) * sc(hid)
        b1 = jnp.zeros((heads * hid,), dtype=jnp.float32)
        W2 = jax.random.normal(ks[5], (heads * hid, heads * out_c), dtype=jnp.float32) * sc(heads * hid)
        as2 = jax.random.normal(ks[6], (heads, out_c), dtype=jnp.float32) * sc(out_c)
        ad2 = jax.random.normal(ks[7], (heads, out_c), dtype=jnp.float32) * sc(out_c)
        b2 = jnp.zeros((out_c,), dtype=jnp.float32)
        return {'x': x, 'edge_index': edge_index, 'W1': W1, 'as1': as1, 'ad1': ad1, 'b1': b1, 'W2': W2, 'as2': as2, 'ad2': ad2, 'b2': b2}
    _L1_gnn_all = _L1_gnn_setup()
    _L1_gnn_in = {k: v for k, v in _L1_gnn_all.items() if k in ('W1', 'as1', 'ad1', 'b1', 'W2', 'as2', 'ad2', 'b2')}
    del _L1_gnn_all

    def _L2_gnn_setup():
        import jax, jax.numpy as jnp
        import numpy as np
        N_NODES = 50000
        N_EDGES = 12500
        FEAT_DIM = 64
        key = jax.random.key(seed)
        k1, k2, k3 = jax.random.split(key, 3)
        x = jax.random.normal(k1, (N_NODES, FEAT_DIM), dtype=jnp.float32)
        beta = jnp.ones((1,), dtype=jnp.float32)
        row_index = jnp.sort(jax.random.randint(k2, (N_EDGES,), 0, N_NODES, dtype=jnp.int32))
        col_index = jax.random.randint(k3, (N_EDGES,), 0, N_NODES, dtype=jnp.int32)
        return {'x': x, 'beta': beta, 'row_index': row_index, 'col_index': col_index}
    _L2_gnn_all = _L2_gnn_setup()
    _L2_gnn_in = {k: v for k, v in _L2_gnn_all.items() if k in ('beta',)}
    del _L2_gnn_all

    def _L3_gnn_setup():
        import jax, jax.numpy as jnp
        import numpy as np
        N_NODES = 100000
        N_EDGES = 1250000
        D = 64
        key = jax.random.key(seed)
        ks = jax.random.split(key, 8)
        x = jax.random.normal(ks[0], (N_NODES, D), dtype=jnp.float32)
        edge_index = jax.random.randint(ks[1], (2, N_EDGES), 0, N_NODES, dtype=jnp.int64)
        edge_attr = jax.random.normal(ks[2], (N_EDGES, D), dtype=jnp.float32)
        s = 1.0 / np.sqrt(D)
        Wl = jax.random.uniform(ks[3], (D, D), jnp.float32, -s, s)
        bl = jax.random.uniform(ks[4], (D,), jnp.float32, -s, s)
        Wn = jax.random.uniform(ks[5], (D, D), jnp.float32, -s, s)
        bn = jax.random.uniform(ks[6], (D,), jnp.float32, -s, s)
        return {'x': x, 'edge_index': edge_index, 'edge_attr': edge_attr, 'Wl': Wl, 'bl': bl, 'Wn': Wn, 'bn': bn}
    _L3_gnn_all = _L3_gnn_setup()
    _L3_gnn_in = {k: v for k, v in _L3_gnn_all.items() if k in ('Wl', 'bl', 'Wn', 'bn')}
    del _L3_gnn_all
    return {'x': x, 'src': src, 'dst': dst, 'edge_attr_64': edge_attr_64, 'L0_gnn_gate_w': _L0_gnn_in['gate_w'], 'L0_gnn_gate_b': _L0_gnn_in['gate_b'], 'L1_gnn_W1': _L1_gnn_in['W1'], 'L1_gnn_as1': _L1_gnn_in['as1'], 'L1_gnn_ad1': _L1_gnn_in['ad1'], 'L1_gnn_b1': _L1_gnn_in['b1'], 'L1_gnn_W2': _L1_gnn_in['W2'], 'L1_gnn_as2': _L1_gnn_in['as2'], 'L1_gnn_ad2': _L1_gnn_in['ad2'], 'L1_gnn_b2': _L1_gnn_in['b2'], 'L2_gnn_beta': _L2_gnn_in['beta'], 'L3_gnn_Wl': _L3_gnn_in['Wl'], 'L3_gnn_bl': _L3_gnn_in['bl'], 'L3_gnn_Wn': _L3_gnn_in['Wn'], 'L3_gnn_bn': _L3_gnn_in['bn']}

def reference(x, src, dst, edge_attr_64, L0_gnn_gate_w, L0_gnn_gate_b, L1_gnn_W1, L1_gnn_as1, L1_gnn_ad1, L1_gnn_b1, L1_gnn_W2, L1_gnn_as2, L1_gnn_ad2, L1_gnn_b2, L2_gnn_beta, L3_gnn_Wl, L3_gnn_bl, L3_gnn_Wn, L3_gnn_bn):
    import jax
    import jax.numpy as jnp

    def _L0_gnn_ref(h, gate_w, gate_b, src, dst):
        import jax, jax.numpy as jnp
        import numpy as np
        N_NODES = 50000
        N_EDGES = 12500
        HID = 64
        ALPHA = 0.5
        EPS = 0.1
        n_nodes = h.shape[0]
        n_edges = src.shape[0]
        deg = jax.ops.segment_sum(jnp.ones((n_edges,), h.dtype), dst, num_segments=n_nodes)
        norm = jnp.clip(deg, 1.0, None) ** (-0.5)
        b_node = jnp.zeros((n_nodes,), h.dtype)
        w_dst = gate_w[:h.shape[1], 0]
        w_src = gate_w[h.shape[1]:, 0]
        g = jnp.tanh(h[dst] @ w_dst + h[src] @ w_src + gate_b[0])
        e = g * (norm[dst] * norm[src] * ALPHA + (EPS - ALPHA) * b_node[dst] * b_node[src])
        z = jax.ops.segment_sum(h[src] * e[:, None], dst, num_segments=n_nodes)
        return z

    def _L1_gnn_ref(x, edge_index, W1, as1, ad1, b1, W2, as2, ad2, b2):
        import jax, jax.numpy as jnp
        import numpy as np
        N_NODES = 50000
        N_EDGES = 12500

        def gat_layer(x, src, dst, W, a_s, a_d, b, concat):
            N = x.shape[0]
            H, C = a_s.shape
            h = (x @ W).reshape(N, H, C)
            alpha_s = jnp.einsum('nhc,hc->nh', h, a_s)
            alpha_d = jnp.einsum('nhc,hc->nh', h, a_d)
            logits = jax.nn.leaky_relu(alpha_s[src] + alpha_d[dst], 0.2)
            m = jax.ops.segment_max(logits, dst, num_segments=N)
            e = jnp.exp(logits - m[dst])
            s = jax.ops.segment_sum(e, dst, num_segments=N)
            a = e / s[dst]
            out = jax.ops.segment_sum(h[src] * a[:, :, None], dst, num_segments=N)
            out = out.reshape(N, H * C) if concat else out.mean(axis=1)
            return out + b
        N = x.shape[0]
        loops = jnp.arange(N, dtype=edge_index.dtype)
        src = jnp.concatenate([edge_index[0], loops])
        dst = jnp.concatenate([edge_index[1], loops])
        h = gat_layer(x, src, dst, W1, as1, ad1, b1, concat=True)
        out = gat_layer(h, src, dst, W2, as2, ad2, b2, concat=False)
        return out

    def _L2_gnn_ref(x, beta, row_index, col_index):
        import jax, jax.numpy as jnp
        import numpy as np
        N_NODES = 50000
        N_EDGES = 12500
        FEAT_DIM = 64
        'AGNN layer: SDDMM edge attention (beta * cosine similarity) over the\n            sparse graph, per-row softmax, then sparse neighbor aggregation.\n            Equivalent math to mygraph.SDDMM + mygraph.agnn_udf (select_id == 5).\n            x: [N, D]; row_index/col_index: [E] edge endpoints (row = destination).\n            '
        N = x.shape[0]
        eps = 1e-08
        xn = x * jax.lax.rsqrt(jnp.sum(x * x, axis=-1, keepdims=True) + eps)
        att = beta[0] * jnp.sum(xn[row_index] * xn[col_index], axis=-1)
        m = jax.ops.segment_max(att, row_index, num_segments=N)
        m = jnp.where(jnp.isfinite(m), m, 0.0)
        e = jnp.exp(att - m[row_index])
        denom = jax.ops.segment_sum(e, row_index, num_segments=N)
        alpha = e / jnp.maximum(denom[row_index], 1e-16)
        out = jax.ops.segment_sum(alpha[:, None] * x[col_index], row_index, num_segments=N)
        return out

    def _L3_gnn_ref(x, edge_index, edge_attr, Wl, bl, Wn, bn):
        import jax, jax.numpy as jnp
        import numpy as np
        N_NODES = 100000
        N_EDGES = 1250000
        D = 64
        src = edge_index[0]
        dst = edge_index[1]
        e_proj = edge_attr @ Wl + bl
        msg = jax.nn.relu(x[src] + e_proj)
        agg = jax.ops.segment_sum(msg, dst, num_segments=x.shape[0])
        return (x + agg) @ Wn + bn
    edge_index = jnp.stack([src, dst])
    x = _layernorm(x + _L0_gnn_ref(x, L0_gnn_gate_w, L0_gnn_gate_b, src, dst), axis=-1)
    x = _layernorm(x + _L1_gnn_ref(x, edge_index, L1_gnn_W1, L1_gnn_as1, L1_gnn_ad1, L1_gnn_b1, L1_gnn_W2, L1_gnn_as2, L1_gnn_ad2, L1_gnn_b2), axis=-1)
    x = _layernorm(x + _L2_gnn_ref(x, L2_gnn_beta, src, dst), axis=-1)
    x = _layernorm(x + _L3_gnn_ref(x, edge_index, edge_attr_64, L3_gnn_Wl, L3_gnn_bl, L3_gnn_Wn, L3_gnn_bn), axis=-1)
    return x

_drawn_inputs = setup_inputs


def setup_inputs(seed=0):
    import zlib

    import numpy as np

    out = dict(_drawn_inputs(seed))
    spreads = {'L1_gnn_b1': (0.0, 0.1), 'L1_gnn_b2': (0.0, 0.1)}
    factors = {'L1_gnn_ad1': 3.495, 'L1_gnn_ad2': 11.552, 'L3_gnn_bl': 5.354}
    for name, (base, spread) in spreads.items():
        noise = np.random.default_rng([zlib.crc32(name.encode()), seed]).standard_normal(out[name].shape)
        drawn = base * np.exp(spread * noise) if base else spread * noise
        out[name] = jnp.asarray(drawn.astype(out[name].dtype))
    for name, factor in factors.items():
        out[name] = (out[name] * factor).astype(out[name].dtype)
    return out
```

```python
from contextlib import ExitStack

import concourse.bass as bass
from concourse import mybir

F32 = mybir.dt.float32
I32 = mybir.dt.int32
ALU = mybir.AluOpType
ACT = mybir.ActivationFunctionType
AX = mybir.AxisListType.X

NODES, EDGES, D, H = 100000, 25000, 64, 2
P = 125
NJ = NODES // P
J = EDGES // P
NC = 8
EC = 4
U = 2
EPS = 1e-5
W1ROW, W2ROW = D + 4, 2 * D + 4
SORT = 32768
FAR = 1 << 20
LOW = -1e38



class Chain:

    def __init__(self, eng, sem):
        self.eng, self.sem, self.base, self.n = eng, sem, 0, 0

    def link(self, ins):
        self.n += 1
        ins.then_inc(self.sem, 1)
        self.eng.wait_ge(self.sem, self.base + self.n)


def pairs(eng, chunks, body, chain=None):
    before = chain.n if chain else 0
    body(0, range(2))
    per = chain.n - before if chain else 0
    with eng.Fori(1, chunks // 2) as i:
        if chain:
            total = chain.n
            chain.base, chain.n = (i - 1) * per + total, 0
        body(i, range(2))
        if chain:
            assert chain.n == per
    if chain:
        chain.base, chain.n = 0, total + (chunks // 2 - 1) * per
    if chunks % 2:
        body(chunks // 2, range(1))


def turn(i, rounds, r, u, us):
    return i * 2 * rounds + r * len(us) + u + 1


def build(nc, x, src, dst, edge_attr, gate_w, gate_b, W1, as1, ad1, b1, W2, as2, ad2, b2, beta, Wl, bl, Wn, bn, out):
    ctx = ExitStack()
    with ctx:
        def sb(name, shape, dt=F32):
            return ctx.enter_context(nc.sbuf_tensor(name, shape, dt))

        def sem(name):
            return ctx.enter_context(nc.semaphore(name))

        def sems(names):
            return [sem(n) for n in names.split()]

        ident = sb("ident", [128, 128])
        ones = sb("ones", [1, 128])
        eps = sb("eps", [128, 1])
        eps2 = sb("eps2", [128, 1])
        eps8 = sb("eps8", [128, 1])
        w1_dup = sb("w1_dup", [128, 128])
        w1_heads = sb("w1_heads", [128, 128])
        w1_t = sb("w1_t", [128, 128])
        w2_ext = sb("w2_ext", [128, 132])
        w2_mean = sb("w2_mean", [128, D])
        wa = sb("wa", [128, 4])
        wa_pair = sb("wa_pair", [128, 8])
        att1 = sb("att1", [128, 4, D])
        att2 = sb("att2", [128, 4, D])
        att_tmp = sb("att_tmp", [128, 4, D])
        gat_pair = sb("gat_pair", [128, 128])
        wn_pair = sb("wn_pair", [128, 128])
        wn_diag = sb("wn_diag", [128, 128])
        wl_diag = sb("wl_diag", [128, 128])
        wn_dup = sb("wn_dup", [128, D])
        mix = sb("mix", [128, D])
        row_mean = sb("row_mean", [128, 1])
        b1_col = sb("b1_col", [128, 1])
        b2_row = sb("b2_row", [1, D])
        b2_all = sb("b2_all", [P, D])
        bn_row = sb("bn_row", [1, D])
        bn_all = sb("bn_all", [P, D])
        bl_all = sb("bl_all", [P, D])
        gat_bias = sb("gat_bias", [1, NC, D])
        wn_bias = sb("wn_bias", [1, NC, D])
        gw = sb("gw", [P, 2, D])
        gb = sb("gb", [P, 1])
        beta_all = sb("beta_all", [P, 1])

        bank = [ctx.enter_context(nc.psum_tensor(f"bank{i}", [128, 512], F32)) for i in range(8)]

        s_v, s_a, s_g = sems("s_v s_a s_g")
        v = Chain(nc.vector, s_v)
        pool = Chain(nc.gpsimd, s_g)

        X1 = nc.dram_tensor("x1_rows", [NODES, W1ROW], F32).ap()
        H2 = nc.dram_tensor("h2_rows", [NODES, W2ROW], F32).ap()
        X2 = nc.dram_tensor("x2_rows", [NODES, D], F32).ap()
        X3 = nc.dram_tensor("x3_rows", [NODES, D], F32).ap()
        NORM = nc.dram_tensor("norm_rows", [NODES, 1], F32).ap()
        E1 = nc.dram_tensor("x1_edge_rows", [EDGES, W1ROW], F32).ap()
        E2 = nc.dram_tensor("h2_edge_rows", [EDGES, W2ROW], F32).ap()
        SORTED = nc.dram_tensor("sorted_pairs", [2, SORT], I32).ap()

        s_zero, s_const, s_w, s_wd, s_w1t, s_w1sb, s_mixp, s_mixv = sems("s_zero s_const s_w s_wd s_w1t s_w1sb s_mixp s_mixv")
        loads = [
            (w1_dup[0:D, :], W1), (w1_dup[D:128, :], W1),
            (w2_ext[:, 0:128], W2), (wn_dup[0:D, :], Wn), (wn_dup[D:128, :], Wn),
            (att1[:, 0:2, :], as1.unsqueeze(0).to_broadcast([128, H, D])),
            (att1[:, 2:4, :], ad1.unsqueeze(0).to_broadcast([128, H, D])),
            (att2[:, 0:2, :], as2.unsqueeze(0).to_broadcast([128, H, D])),
            (att2[:, 2:4, :], ad2.unsqueeze(0).to_broadcast([128, H, D])),
            (b1_col[:, :], b1.unsqueeze(1)), (b2_row[:, :], b2.unsqueeze(0)), (bn_row[:, :], bn.unsqueeze(0)),
            (b2_all[:, :], b2.unsqueeze(0).to_broadcast([P, D])), (bn_all[:, :], bn.unsqueeze(0).to_broadcast([P, D])),
            (bl_all[:, :], bl.unsqueeze(0).to_broadcast([P, D])),
            (gw[:, :, :], gate_w.rearrange("(s f) o -> o s f", s=2).to_broadcast([P, 2, D])),
            (gb[:, :], gate_b.unsqueeze(0).to_broadcast([P, 1])),
            (beta_all[:, :], beta.unsqueeze(0).to_broadcast([P, 1])),
        ]
        with nc.Block() as block:
            @block.sync
            def _(sp):
                for to, frm in loads:
                    sp.dma_start(to, frm).then_inc(s_w, 16)
                sp.wait_ge(s_zero, 1)
                for h in range(2):
                    half = slice(h * D, h * D + D)
                    sp.dma_start(w1_heads[half, half], W1[:, half]).then_inc(s_wd, 16)
                    sp.dma_start(wl_diag[half, half], Wl).then_inc(s_wd, 16)
                    sp.dma_start(wn_diag[half, half], Wn).then_inc(s_wd, 16)
                sp.wait_ge(s_wd, 96)

            @block.gpsimd
            def _(g):
                pool.link(g.memset(ident[:, :], 0.0))
                pool.link(g.affine_select(out=ident[:, :], in_=ident[:, :], compare_op=ALU.not_equal, fill=1.0,
                                          base=0, pattern=[[-1, 128]], channel_multiplier=1))
                g.memset(eps[:, :], EPS)
                g.memset(eps2[:, :], EPS * EPS)
                g.memset(eps8[:, :], 1e-8)
                g.memset(ones[:, :], 1.0).then_inc(s_const, 1)

            @block.vector
            def _(dve):
                for t in (w1_heads, wl_diag, wn_diag, gat_pair, wa_pair):
                    dve.memset(t[:, :], 0.0)
                dve.memset(wn_pair[:, :], 0.0).then_inc(s_zero, 1)
                dve.wait_ge(s_w, 16 * len(loads))
                for k in range(4):
                    part = slice((k % H) * D, (k % H) * D + D)
                    v.link(dve.tensor_tensor(att_tmp[:, k, :], w1_dup[:, part], att1[:, k, :], ALU.mult))
                v.link(dve.tensor_reduce(wa[:, :], att_tmp[:, :, :], AX, ALU.add))
                for h in range(2):
                    half = slice(h * D, h * D + D)
                    dve.tensor_copy(wa_pair[half, 4 * h:4 * h + 4], wa[half, :])
                for k in range(4):
                    part = slice((k % H) * D, (k % H) * D + D)
                    v.link(dve.tensor_tensor(att_tmp[:, k, :], w2_ext[:, part], att2[:, k, :], ALU.mult))
                v.link(dve.tensor_reduce(w2_ext[:, 128:132], att_tmp[:, :, :], AX, ALU.add))
                v.link(dve.tensor_tensor(w2_mean[:, :], w2_ext[:, 0:D], w2_ext[:, D:128], ALU.add))
                v.link(dve.tensor_scalar(w2_mean[:, :], w2_mean[:, :], 0.5, None, ALU.mult))
                dve.wait_ge(s_w1t, 1)
                for h in range(2):
                    last = dve.tensor_copy(w1_t[:, h * D:h * D + D], bank[0][:, 0:D])
                last.then_inc(s_w1sb, 1)
                dve.wait_ge(s_mixp, 1)

                def centre(rows, m):
                    v.link(dve.tensor_reduce(row_mean[0:rows, :], m, AX, ALU.add))
                    v.link(dve.tensor_scalar(row_mean[0:rows, :], row_mean[0:rows, :], 1.0 / D, None, ALU.mult))
                    v.link(dve.tensor_scalar(m, m, row_mean[0:rows, :], None, ALU.subtract))

                for pair, w in ((gat_pair, bank[1][:, 0:D]), (wn_pair, wn_dup[:, :])):
                    for h in range(2):
                        half = slice(h * D, h * D + D)
                        v.link(dve.tensor_tensor(mix[half, :], ident[half, half], w[half, :], ALU.add))
                    centre(128, mix[:, :])
                    for h in range(2):
                        half = slice(h * D, h * D + D)
                        v.link(dve.tensor_copy(pair[half, half], mix[half, :]))
                v.link(dve.tensor_tensor(mix[0:1, :], bank[2][0:1, 0:D], b2_row[:, :], ALU.add))
                centre(1, mix[0:1, :])
                v.link(dve.tensor_copy(gat_bias[:, :, :], mix[0:1, :].unsqueeze(1).to_broadcast([1, NC, D])))
                centre(1, bn_row[:, :])
                v.link(dve.tensor_copy(wn_bias[:, :, :], bn_row[:, :].unsqueeze(1).to_broadcast([1, NC, D])))

            @block.tensor
            def _(pe):
                pe.wait_ge(s_w, 16 * len(loads))
                pe.wait_ge(s_const, 1)
                pe.transpose(bank[0][:, 0:D], w1_dup[0:D, :], ident[0:D, 0:D]).then_inc(s_w1t, 1)
                pe.wait_ge(s_w1sb, 1)
                pe.matmul(bank[1][:, 0:D], w1_t[:, :], w2_mean[:, :], start=True, stop=True)
                pe.matmul(bank[2][0:1, 0:D], b1_col[:, :], w2_mean[:, :], start=True, stop=True).then_inc(s_mixp, 1)


        def rowbuf(name, width, n=U):
            return [sb(f"{name}{u}", [P, NC, width]) for u in range(n)]

        n_in, n_c, n_sq, n_out = rowbuf("n_in", D), rowbuf("n_c", D), rowbuf("n_sq", D), rowbuf("n_out", D)
        r_x1, r_h2, r_x2 = rowbuf("r_x1", W1ROW), rowbuf("r_h2", W2ROW), rowbuf("r_x2", D)
        n_t = [sb(f"n_t{u}", [128, NC // 2 * P]) for u in range(U)]
        o1_t = sb("o1_t", [128, 2, NC // 2 * P])
        n_mean, n_var, n_sd, n_r = ([sb(f"n_{n}{u}", [P, NC]) for u in range(U)] for n in ("mean", "var", "sd", "r"))
        n_sd2, n_r2 = ([sb(f"n_{n}{u}", [P, NC]) for u in range(U)] for n in ("sd2", "r2"))
        s_nin, s_nst, s_x1st, s_h2st, s_x2st, s_x3st = ([sem(f"{n}{u}") for u in range(U)] for n in
            ("s_nin", "s_nst", "s_x1st", "s_h2st", "s_x2st", "s_x3st"))
        s_nc, s_nq, s_nx, s_nt, s_nts, s_nm, s_no, s_nv, s_nd = sems("s_nc s_nq s_nx s_nt s_nts s_nm s_no s_nv s_nd")
        s_o1, s_o1s, s_h2, s_h2s, s_x1r, s_x2r = sems("s_o1 s_o1s s_h2 s_h2s s_x1r s_x2r")
        NCH = NJ // NC

        def nodes_of(t):
            return t.rearrange("(p j) f -> p (j f)", p=P)

        def flat(t):
            return t.rearrange("p c f -> p (c f)")

        def h2_slot(c):
            return bank[4 + c // 3][0:P, c % 3 * W2ROW:c % 3 * W2ROW + W2ROW]

        att_psum = bank[6][0:P, 2 * W2ROW:2 * W2ROW + 4 * NC]

        def nodes_sp(sp):
            def load(k, u):
                sp.dma_start(flat(n_in[u][:, :, :]), nodes_of(x)[:, bass.ds(k * NC * D, NC * D)]).then_inc(s_nin[u], 16)

            for u in range(U):
                load(u, u)

            def store(i, u, to, frm, width, done):
                sp.dma_start(nodes_of(to)[:, bass.ds((2 * i + u) * NC * width, NC * width)], flat(frm[u][:, :, :])).then_inc(done[u], 16)

            def body(i, us, load_next=True):
                for u in us:
                    sp.wait_ge(s_x1r, turn(i, 1, 0, u, us))
                    store(i, u, X1, r_x1, W1ROW, s_x1st)
                    if load_next:
                        load(2 * i + 2 + u, u)
                for u in us:
                    sp.wait_ge(s_h2s, turn(i, 1, 0, u, us))
                    store(i, u, H2, r_h2, W2ROW, s_h2st)
                for u in us:
                    sp.wait_ge(s_x2r, turn(i, 1, 0, u, us))
                    store(i, u, X2, r_x2, D, s_x2st)
                for u in us:
                    sp.wait_ge(s_nx, turn(i, 2, 1, u, us))
                    store(i, u, X3, n_c, D, s_x3st)
                for u in us:
                    sp.wait_ge(s_no, turn(i, 1, 0, u, us))
                    store(i, u, out, n_out, D, s_nst)
            with nc.sync.Fori(0, NCH // 2 - 1) as i:
                body(i, range(2))
            body(NCH // 2 - 1, range(2), False)
            for u in range(U):
                for s in (s_nst, s_x1st, s_h2st, s_x2st, s_x3st):
                    sp.wait_ge(s[u], 16 * (NCH // 2))

        def wide(t, width=D):
            return t.unsqueeze(2).to_broadcast([P, t.shape[1], width])

        def nodes_dve(dve):
            def body(i, us):
                first = isinstance(i, int) and i == 0
                for u in us:
                    dve.wait_ge(s_nin[u], 16 * i + 16)
                    v.link(dve.tensor_reduce(n_mean[u][:, :], n_in[u][:, :, :], AX, ALU.add))
                    v.link(dve.tensor_scalar(n_mean[u][:, :], n_mean[u][:, :], -1.0 / D, None, ALU.mult))
                    if not first:
                        dve.wait_ge(s_x3st[u], 16 * i)
                    dve.tensor_tensor(n_c[u][:, :, :], n_in[u][:, :, :], wide(n_mean[u][:, :]), ALU.add).then_inc(s_nc, 1)
                for r in range(3):
                    for u in us:
                        dve.wait_ge(s_nq, turn(i, 3, r, u, us))
                        dve.tensor_reduce(n_var[u][:, :], n_sq[u][:, :, :], AX, ALU.add).then_inc(s_nv, 1)
                    for u in us:
                        dve.wait_ge(s_nd, turn(i, 3, r, u, us))
                        v.link(dve.reciprocal(n_r[u][:, :], n_sd[u][:, :]))
                        if r == 0:
                            if not first:
                                dve.wait_ge(s_x1st[u], 16 * i)
                            v.link(dve.tensor_tensor(n_c[u][:, :, :], n_c[u][:, :, :], wide(n_r[u][:, :]), ALU.mult))
                            dve.tensor_copy(r_x1[u][:, :, 0:D], n_c[u][:, :, :]).then_inc(s_nx, 1)
                        else:
                            y = bank[7][0:P, :].rearrange("p (c f) -> p c f", f=D) if u == 0 else bank[3][0:P, :].rearrange("p (c f) -> p c f", f=D)
                            if r == 2:
                                if not first:
                                    dve.wait_ge(s_nst[u], 16 * i)
                                dve.tensor_tensor(n_out[u][:, :, :], y, wide(n_r[u][:, :]), ALU.mult).then_inc(s_no, 1)
                            else:
                                v.link(dve.reciprocal(n_r2[u][:, :], n_sd2[u][:, :]))
                                if not first:
                                    dve.wait_ge(s_x2st[u], 16 * i)
                                dve.tensor_tensor(r_x2[u][:, :, :], y, wide(n_r2[u][:, :]), ALU.mult).then_inc(s_x2r, 1)
                                dve.tensor_tensor(n_c[u][:, :, :], y, wide(n_r[u][:, :]), ALU.mult).then_inc(s_nx, 1)
            pairs(nc.vector, NCH, body, v)

        def nodes_act(act):
            def body(i, us):
                first = isinstance(i, int) and i == 0
                for r in range(3):
                    for u in us:
                        if r:
                            act.wait_ge(s_nm, turn(i, 2, r - 1, u, us))
                        else:
                            act.wait_ge(s_nc, turn(i, 1, 0, u, us))
                        frm = flat(n_c[u][:, :, :]) if r == 0 else bank[7 if u == 0 else 3][0:P, :]
                        nc.scalar.activation(flat(n_sq[u][:, :, :]), frm, ACT.Square, scale=D ** -0.5).then_inc(s_nq, 1)
                    for u in us:
                        act.wait_ge(s_nv, turn(i, 3, r, u, us))
                        if r == 1:
                            nc.scalar.activation(n_sd2[u][:, :], n_var[u][:, :], ACT.Sqrt, bias=eps[0:P, :])
                        nc.scalar.activation(n_sd[u][:, :], n_var[u][:, :], ACT.Sqrt, bias=(eps2 if r == 1 else eps)[0:P, :],
                                             scale=1.0 + EPS if r == 1 else 1.0).then_inc(s_nd, 1)
                    if r < 2:
                        for u in us:
                            act.wait_ge(s_nt, turn(i, 2, r, u, us))
                            nc.scalar.copy(n_t[u][:, :], bank[u][:, 0:NC // 2 * P]).then_inc(s_nts, 1)
                    if r == 0:
                        for u in us:
                            act.wait_ge(s_o1, turn(i, 1, 0, u, us))
                            nc.scalar.activation(o1_t[:, 0, :], bank[2][:, 0:NC // 2 * P], ACT.Identity, bias=b1_col[:, :])
                            nc.scalar.activation(o1_t[:, 1, :], bank[3][:, 0:NC // 2 * P], ACT.Identity, bias=b1_col[:, :]).then_inc(s_o1s, 1)
                            act.wait_ge(s_h2, turn(i, 1, 0, u, us))
                            if not first:
                                act.wait_ge(s_h2st[u], 16 * i)
                            for b, cols in enumerate((3, 3, 2)):
                                ins = nc.scalar.copy(flat(r_h2[u][:, 3 * b:3 * b + cols, :]), bank[4 + b][0:P, 0:cols * W2ROW])
                            ins.then_inc(s_h2s, 1)
                            if not first:
                                act.wait_ge(s_x1st[u], 16 * i)
                            nc.scalar.copy(r_x1[u][:, :, D:W1ROW], att_psum.rearrange("p (c a) -> p c a", a=4)).then_inc(s_x1r, 1)
            pairs(nc.scalar, NCH, body)

        def nodes_pe(pe):
            def body(i, us):
                first = isinstance(i, int) and i == 0
                for r, (w, bias) in enumerate(((gat_pair, gat_bias), (wn_pair, wn_bias))):
                    for u in us:
                        pe.wait_ge(s_nx, turn(i, 2, r, u, us))
                        for c in range(NC // 2):
                            last = pe.transpose(bank[u][:, c * P:(c + 1) * P], flat(n_c[u][:, 2 * c:2 * c + 2, :]), ident[0:P, 0:P])
                        last.then_inc(s_nt, 1)
                    if r == 0:
                        for u in us:
                            pe.wait_ge(s_nts, turn(i, 2, r, u, us))
                            if u == 0 and not first:
                                pe.wait_ge(s_no, 2 * i)
                            if u == 1:
                                pe.wait_ge(s_o1s, turn(i, 1, 0, 0, us))
                            for h in range(2):
                                half = slice(h * D, h * D + D)
                                last = pe.matmul(bank[2 + h][:, 0:NC // 2 * P], w1_dup[half, :], n_t[u][half, :], start=True, stop=True)
                            last.then_inc(s_o1, 1)
                            pe.wait_ge(s_o1s, turn(i, 1, 0, u, us))
                            if u or not first:
                                pe.wait_ge(s_h2s, 2 * i + u)
                                pe.wait_ge(s_x1r, 2 * i + u)
                            for c in range(NC):
                                pe.matmul(h2_slot(c), o1_t[:, c % 2, c // 2 * P:c // 2 * P + P], w2_ext[:, :], start=True, stop=True)
                            for c in range(NC // 2):
                                last = pe.matmul(att_psum[:, 8 * c:8 * c + 8], n_t[u][:, c * P:c * P + P], wa_pair[:, :], start=True, stop=True)
                            last.then_inc(s_h2, 1)
                    for u in us:
                        if r == 1:
                            pe.wait_ge(s_nts, turn(i, 2, r, u, us))
                        y = bank[7 if u == 0 else 3]
                        pe.matmul(y[0:P, :], ones[0:1, 0:P], flat(bias[:, :, :]), start=True, stop=False)
                        for c in range(NC // 2):
                            last = pe.matmul(y[0:P, c * 128:(c + 1) * 128], n_t[u][:, c * P:(c + 1) * P], w[:, :],
                                             start=False, stop=c == NC // 2 - 1)
                        last.then_inc(s_nm, 1)
            pairs(nc.tensor, NCH, body)

        def plane(name, dt=F32):
            return sb(name, [P, J], dt)

        A = sb("edge_rows", [P, 2 * J * (D + 2)])

        def rows_of(at, width):
            return A[:, at:at + J * width].rearrange("p (j w) -> p j w", w=width)

        src_i, dst_i, scat_i, src_scat_i = plane("src_i", I32), plane("dst_i", I32), plane("scat_i", I32), plane("src_scat_i", I32)
        key, key_prev, key_next = plane("key"), plane("key_prev"), plane("key_next")
        key_i, prev_i, next_i = plane("key_i", I32), plane("prev_i", I32), plane("next_i", I32)
        cont, last, more = plane("cont"), plane("last"), plane("more")
        reach_f, reach_r = plane("reach_f"), plane("reach_r")
        pen_f, pen_reach = plane("pen_f"), plane("pen_reach")
        norm_d, norm_s = plane("norm_d"), plane("norm_s")
        heads = [plane(f"head{h}") for h in range(2)]
        tops = [plane(f"top{h}") for h in range(2)]
        dens = [plane(f"den{h}") for h in range(2)]
        selfs = [plane(f"self{h}") for h in range(2)]
        own4 = sb("own4", [P, J, 4])
        pass_f_t, pen_f_t, pass_r_t = (sb(n, [128, P]) for n in ("pass_f_t", "pen_f_t", "pass_r_t"))
        cross_in = sb("cross_in", [128, 128])
        crossed = sb("crossed", [128, P + 1])
        carry_in = sb("carry_in", [P, D])
        e_dup = [sb(f"e_dup{u}", [P, NC, 2, D]) for u in range(U)]
        s_tin, s_tout = sems("s_tin s_tout")
        crossings = {"dve": 0, "pe": 0}

        def edges_of(t):
            return t.rearrange("(p j) -> p j", p=P)

        def transpose_dve(dve, ins):
            ins.then_inc(s_tin, 1)
            crossings["dve"] += 1
            dve.wait_ge(s_tout, crossings["dve"])

        def transpose_pe(pe, frm, rows, cols):
            crossings["pe"] += 1
            pe.wait_ge(s_tin, crossings["pe"])
            pe.transpose(bank[0][0:cols, 0:rows], frm, ident[0:rows, 0:rows]).then_inc(s_tout, 1)

        def segments_dve(dve):
            dve.tensor_tensor(cont[:, :], key[:, :], key_prev[:, :], ALU.is_equal)
            dve.tensor_tensor(last[:, :], key[:, :], key_next[:, :], ALU.not_equal)
            v.link(dve.tensor_tensor(more[:, :], key[:, :], key_next[:, :], ALU.is_equal))
            dve.tensor_scalar(pen_f[:, :], cont[:, :], 1.0, -LOW, ALU.subtract, ALU.mult)
            dve.tensor_tensor_scan(reach_f[:, :], cont[:, :], cont[:, :], 1.0, ALU.mult, ALU.mult)
            v.link(dve.tensor_tensor_scan(reach_r[:, ::-1], more[:, ::-1], more[:, ::-1], 1.0, ALU.mult, ALU.mult))
            dve.tensor_scalar(pen_reach[:, :], reach_f[:, :], 1.0, -LOW, ALU.subtract, ALU.mult)
            transpose_dve(dve, dve.tensor_copy(cross_in[0:P, :], reach_f[:, J - 1:J].to_broadcast([P, 128])))
            v.link(dve.tensor_copy(pass_f_t[:, :], bank[0][:, 0:P]))
            dve.tensor_scalar(pen_f_t[:, :], pass_f_t[:, :], 1.0, -LOW, ALU.subtract, ALU.mult)
            transpose_dve(dve, dve.tensor_copy(cross_in[0:P, :], reach_r[:, 0:1].to_broadcast([P, 128])))
            v.link(dve.tensor_copy(pass_r_t[:, :], bank[0][:, 0:P]))

        def segments_pe(pe):
            for _ in range(2):
                transpose_pe(pe, cross_in[0:P, :], P, 128)

        def carry_dve(dve, ends, n, kind):
            transpose_dve(dve, dve.tensor_copy(cross_in[0:P, 0:n], ends))
            if kind == "hold":
                v.link(dve.memset(crossed[0:n, P:P + 1], 0.0))
                transpose_dve(dve, dve.tensor_tensor_scan(crossed[0:n, P - 1::-1], pass_r_t[0:n, ::-1], bank[0][0:n, P - 1::-1], 0.0, ALU.mult, ALU.add))
            else:
                first = LOW if kind == "max" else 0.0
                v.link(dve.memset(crossed[0:n, 0:1], first))
                transpose_dve(dve, dve.tensor_tensor_scan(
                    crossed[0:n, 1:P + 1], (pen_f_t if kind == "max" else pass_f_t)[0:n, :], bank[0][0:n, 0:P], first,
                    ALU.add if kind == "max" else ALU.mult, ALU.max if kind == "max" else ALU.add))
            v.link(dve.tensor_copy(carry_in[:, 0:n], bank[0][0:P, 0:n]))

        def carry_pe(pe, n, kind):
            transpose_pe(pe, cross_in[0:P, 0:n], P, n)
            transpose_pe(pe, crossed[0:n, 1:P + 1] if kind == "hold" else crossed[0:n, 0:P], n, P)

        def over_segments(dve, kind, ws):
            if kind == "hold":
                for w in ws:
                    done = dve.tensor_tensor(w, w, last[:, :], ALU.mult)
                v.link(done)
                for w in ws:
                    done = dve.tensor_tensor_scan(w[:, ::-1], more[:, ::-1], w[:, ::-1], 0.0, ALU.mult, ALU.add)
            elif kind == "max":
                for w in ws:
                    done = dve.tensor_tensor_scan(w, pen_f[:, :], w, LOW, ALU.add, ALU.max)
            else:
                for w in ws:
                    done = dve.tensor_tensor_scan(w, cont[:, :], w, 0.0, ALU.mult, ALU.add)
            v.link(done)
            at = 0 if kind == "hold" else J - 1
            for w in ws:
                carry_dve(dve, w[:, at:at + 1], 1, kind)
                if kind == "max":
                    done = dve.scalar_tensor_tensor(w, pen_reach[:, :], carry_in[:, 0:1], w, ALU.add, ALU.max)
                else:
                    reach = reach_r if kind == "hold" else reach_f
                    done = dve.scalar_tensor_tensor(w, reach[:, :], carry_in[:, 0:1], w, ALU.mult, ALU.add)
                v.link(done)

        def over_segments_pe(pe, kind, n):
            for _ in range(n):
                carry_pe(pe, 1, kind)

        def rows_over_segments(dve, kind, rows):
            if kind == "hold":
                v.link(dve.tensor_tensor(rows[:, :, 0:D], rows[:, :, 0:D], last[:, :].unsqueeze(2).to_broadcast([P, J, D]), ALU.mult))
            for f in range(D):
                if kind == "hold":
                    done = dve.tensor_tensor_scan(rows[:, ::-1, f], more[:, ::-1], rows[:, ::-1, f], 0.0, ALU.mult, ALU.add)
                else:
                    done = dve.tensor_tensor_scan(rows[:, :, f], cont[:, :], rows[:, :, f], 0.0, ALU.mult, ALU.add)
            v.link(done)
            at = 0 if kind == "hold" else J - 1
            carry_dve(dve, rows[:, at, 0:D], D, kind)
            reach = reach_r if kind == "hold" else reach_f
            for f in range(D):
                done = dve.scalar_tensor_tensor(rows[:, :, f], reach[:, :], carry_in[:, f:f + 1], rows[:, :, f], ALU.mult, ALU.add)
            v.link(done)

        def gather(g, to, table, idx, done):
            for j in range(J):
                g.indirect_dma_start(out=to[:, j, :] if len(to.shape) == 3 else to[:, j:j + 1], out_offset=None, in_=table,
                                     in_offset=bass.IndirectOffsetOnAxis(ap=idx[:, j:j + 1], axis=0),
                                     bounds_check=NODES - 1, oob_is_err=False).then_inc(done, 16)

        def scatter(g, table, frm, idx, cols, done):
            for j in range(cols):
                g.indirect_dma_start(out=table, out_offset=bass.IndirectOffsetOnAxis(ap=idx[:, j:j + 1], axis=0),
                                     in_=frm[:, j, :] if len(frm.shape) == 3 else frm[:, j:j + 1], in_offset=None,
                                     bounds_check=NODES - 1, oob_is_err=False).then_inc(done, 16)

        ALL = 16 * J


        SF, SLOT_BITS = SORT // 128, SORT.bit_length() - 1
        F_BITS = SF.bit_length() - 1
        k_srt = [sb(f"k_srt{n}", [128, SF]) for n in range(2)]
        d_srt = [sb(f"d_srt{n}", [128, SF]) for n in range(2)]
        s_srt = sb("s_srt", [128, SF])
        gray_i, bits_i = sb("gray_i", [128, SF], I32), sb("bits_i", [128, SF], I32)
        ki_srt, di_srt = sb("ki_srt", [128, SF], I32), sb("di_srt", [128, SF], I32)
        s_sl, s_sio, s_sfill, s_sst, s_sorted = sems("s_sl s_sio s_sfill s_sst s_sorted")
        s_stin, s_stout = sems("s_stin s_stout")
        FULL = EDGES // SF

        def sort_steps():
            for merge in range(1, SLOT_BITS + 1):
                yield "direct", merge
                if merge > F_BITS:
                    yield "turn", 0
                    for bit in range(merge - 1, F_BITS - 1, -1):
                        yield "exchange", bit - F_BITS
                    yield "turn", 0
                for bit in range(min(merge, F_BITS) - 1, -1, -1):
                    yield "exchange", bit

        STEPS = list(sort_steps())

        def sort_sp(sp):
            sp.wait_ge(s_sfill, 1)
            for to, frm in ((ki_srt, src), (di_srt, dst)):
                sp.dma_start(to[0:FULL, :], frm[0:FULL * SF].rearrange("(p f) -> p f", f=SF)).then_inc(s_sl, 16)
                sp.dma_start(to[FULL:FULL + 1, 0:EDGES - FULL * SF], frm[FULL * SF:EDGES].unsqueeze(0)).then_inc(s_sl, 16)

        def sort_store_sp(sp):
            sp.wait_ge(s_sorted, 1)
            for n, frm in enumerate((ki_srt, di_srt)):
                sp.dma_start(SORTED[n].rearrange("(p f) -> p f", f=SF), frm[:, :]).then_inc(s_sst, 16)
            sp.wait_ge(s_sst, 32)

        def sort_fill_dve(dve):
            dve.memset(di_srt[:, :], 0)
            dve.memset(ki_srt[:, :], FAR).then_inc(s_sfill, 1)

        def sort_dve(dve):
            dve.wait_ge(s_sio, 1)
            v.link(dve.tensor_single_scalar(bits_i[:, :], gray_i[:, :], 1, ALU.logical_shift_right))
            v.link(dve.tensor_tensor(gray_i[:, :], gray_i[:, :], bits_i[:, :], ALU.bitwise_xor))
            dve.wait_ge(s_sl, 64)
            dve.tensor_copy(d_srt[0][:, :], di_srt[:, :])
            v.link(dve.tensor_copy(k_srt[0][:, :], ki_srt[:, :]))
            now, turns = 0, 0
            for n, (what, bit) in enumerate(STEPS):
                hand_over = n + 1 < len(STEPS) and STEPS[n + 1][0] == "turn"
                k0, k1, d0, d1 = (t[:, :] for t in (k_srt[now], k_srt[1 - now], d_srt[now], d_srt[1 - now]))
                if what == "direct":
                    if bit == 1:
                        v.link(dve.tensor_scalar(bits_i[:, :], bits_i[:, :], 1, None, ALU.bitwise_and))
                    else:
                        v.link(dve.tensor_scalar(bits_i[:, :], gray_i[:, :], bit - 1, 1, ALU.logical_shift_right, ALU.bitwise_and))
                    v.link(dve.tensor_scalar(s_srt[:, :], bits_i[:, :], -2.0, 1.0, ALU.mult, ALU.add))
                    done = dve.tensor_tensor(k0, k0, s_srt[:, :], ALU.mult)
                elif what == "turn":
                    turns += 1
                    dve.wait_ge(s_stout, turns)
                    dve.tensor_copy(k1, bank[0][:, 0:SF])
                    done = dve.tensor_copy(d1, bank[0][:, SF:2 * SF])
                    now = 1 - now
                else:
                    k0, k1, d0, d1 = (t.rearrange("p (n two d) -> p n two d", two=2, d=1 << bit) for t in (k0, k1, d0, d1))
                    swap = s_srt[:, 0:SF // 2].rearrange("p (n d) -> p n d", d=1 << bit)
                    diff = s_srt[:, SF // 2:SF].rearrange("p (n d) -> p n d", d=1 << bit)
                    dve.tensor_tensor(swap, k0[:, :, 0], k0[:, :, 1], ALU.is_gt)
                    v.link(dve.tensor_tensor(diff, d0[:, :, 1], d0[:, :, 0], ALU.subtract))
                    v.link(dve.tensor_tensor(diff, diff, swap, ALU.mult))
                    dve.tensor_tensor(k1[:, :, 0], k0[:, :, 0], k0[:, :, 1], ALU.min)
                    dve.tensor_tensor(k1[:, :, 1], k0[:, :, 0], k0[:, :, 1], ALU.max)
                    dve.tensor_tensor(d1[:, :, 0], d0[:, :, 0], diff, ALU.add)
                    done = dve.tensor_tensor(d1[:, :, 1], d0[:, :, 1], diff, ALU.subtract)
                    now = 1 - now
                if hand_over:
                    done.then_inc(s_stin, 1)
                else:
                    v.link(done)
            dve.tensor_copy(ki_srt[:, :], k_srt[now][:, :])
            dve.tensor_copy(di_srt[:, :], d_srt[now][:, :]).then_inc(s_sorted, 1)

        def sort_pe(pe):
            now, turns = 0, 0
            for what, _ in STEPS:
                if what == "turn":
                    turns += 1
                    pe.wait_ge(s_stin, turns)
                    for h in range(SF // 128):
                        part = slice(h * 128, h * 128 + 128)
                        pe.transpose(bank[0][:, part], k_srt[now][:, part], ident[:, :])
                        ins = pe.transpose(bank[0][:, SF + h * 128:SF + h * 128 + 128], d_srt[now][:, part], ident[:, :])
                    ins.then_inc(s_stout, 1)
                if what != "direct":
                    now = 1 - now
        s_idx, s_pre, s_deg, s_sd, s_ninit, s_fill = sems("s_idx s_pre s_deg s_sd s_ninit s_fill")
        xs, xd = rows_of(0, D), rows_of(J * D, D)
        fill = e_dup[0][:, :, :, :].rearrange("p c h f -> p (c h f)")[:, 0:NJ]

        def load_order(sp, keys, done):
            sp.dma_start(key_i[:, :], edges_of(keys)).then_inc(done, 16)
            sp.dma_start(prev_i[1:P, :], keys[J - 1:EDGES - 1].rearrange("(p j) -> p j", j=J)).then_inc(done, 16)
            sp.dma_start(prev_i[0:1, 1:J], keys[0:J - 1].unsqueeze(0)).then_inc(done, 16)
            sp.dma_start(next_i[0:P - 1, :], keys[1:EDGES - J + 1].rearrange("(p j) -> p j", j=J)).then_inc(done, 16)
            sp.dma_start(next_i[P - 1:P, 0:J - 1], keys[EDGES - J + 1:EDGES].unsqueeze(0)).then_inc(done, 16)

        def order_dve(dve):
            dve.tensor_copy(key[:, :], key_i[:, :])
            dve.tensor_copy(key_prev[:, :], prev_i[:, :])
            v.link(dve.tensor_copy(key_next[:, :], next_i[:, :]))
            segments_dve(dve)

        def last_only(dve, to, tmp):
            v.link(dve.tensor_scalar(tmp, more[:, :], float(FAR), None, ALU.mult))
            v.link(dve.tensor_tensor(tmp, key[:, :], tmp, ALU.add))
            v.link(dve.tensor_copy(to, tmp))

        with nc.Block() as block:
            @block.sync
            def _(sp):
                sp.wait_ge(s_pre, 1)
                load_order(sp, dst, s_idx)
                sp.dma_start(src_i[:, :], edges_of(src)).then_inc(s_idx, 16)
                sp.dma_start(dst_i[:, :], edges_of(dst)).then_inc(s_idx, 16)
                sp.wait_ge(s_fill, 1)
                sp.dma_start(NORM.rearrange("(p j) o -> p (j o)", p=P), fill).then_inc(s_ninit, 16)
                sp.wait_ge(s_ninit, 16)

            @block.vector
            def _(dve):
                dve.memset(prev_i[:, :], -1)
                dve.memset(next_i[:, :], -1).then_inc(s_pre, 1)
                dve.memset(fill, 1.0).then_inc(s_fill, 1)
                v.link(dve.memset(norm_d[:, :], 1.0))
                dve.wait_ge(s_idx, 7 * 16)
                order_dve(dve)
                over_segments(dve, "sum", [norm_d[:, :]])
                v.link(dve.tensor_scalar(norm_d[:, :], norm_d[:, :], 1.0, None, ALU.max))
                dve.tensor_copy(norm_s[:, :], norm_d[:, :]).then_inc(s_deg, 1)
                dve.wait_ge(s_sd, 1)
                v.link(dve.reciprocal(norm_d[:, :], norm_s[:, :]))
                over_segments(dve, "hold", [norm_d[:, :]])
                last_only(dve, scat_i[:, :], heads[0][:, :])

            @block.scalar
            def _(act):
                act.wait_ge(s_deg, 1)
                nc.scalar.activation(norm_s[:, :], norm_s[:, :], ACT.Sqrt).then_inc(s_sd, 1)

            @block.tensor
            def _(pe):
                segments_pe(pe)
                over_segments_pe(pe, "sum", 1)
                over_segments_pe(pe, "hold", 1)

        s_gx, s_gn, s_sn = sems("s_gx s_gn s_sn")
        with nc.Block() as block:
            @block.gpsimd
            def _(g):
                g.iota(gray_i[:, :], pattern=[[1, SF]], base=0, channel_multiplier=SF).then_inc(s_sio, 1)
                scatter(g, NORM, norm_d, scat_i, J, s_sn)
                gather(g, xs, x, src_i, s_gx)
                gather(g, xd, x, dst_i, s_gx)
                g.wait_ge(s_sn, ALL)
                gather(g, norm_s, NORM, src_i, s_gn)
                g.wait_ge(s_gx, 2 * ALL)
                g.wait_ge(s_gn, ALL)

            @block.sync
            def _(sp):
                sort_sp(sp)
                nodes_sp(sp)
                sort_store_sp(sp)

            @block.vector
            def _(dve):
                sort_fill_dve(dve)
                nodes_dve(dve)
                sort_dve(dve)

            @block.scalar
            def _(act):
                nodes_act(act)

            @block.tensor
            def _(pe):
                nodes_pe(pe)
                sort_pe(pe)

        ECH = J // NC

        def phase(name, names, double=""):
            made = {n: sem(f"s_{name}_{n}") for n in names.split()}
            made.update({n: [sem(f"s_{name}_{n}{u}") for u in range(U)] for n in double.split()})
            return type(name, (), made)

        def chunk(t, i, u):
            return t[:, bass.ds((2 * i + u) * NC, NC)] if len(t.shape) == 2 else t[:, bass.ds((2 * i + u) * NC, NC), :]

        def tall(row):
            return row[:, :].unsqueeze(1).to_broadcast([P, NC, D])

        def edge_rows(t, i, u, width):
            return t.rearrange("(p j) f -> p (j f)", p=P)[:, bass.ds((2 * i + u) * NC * width, NC * width)]

        def is_first(i):
            return isinstance(i, int) and i == 0

        def centre_dve(dve, s, i, us):
            for u in us:
                v.link(dve.tensor_reduce(n_mean[u][:, :], n_in[u][:, :, :], AX, ALU.add))
                v.link(dve.tensor_scalar(n_mean[u][:, :], n_mean[u][:, :], -1.0 / D, None, ALU.mult))
                dve.tensor_tensor(n_c[u][:, :, :], n_in[u][:, :, :], wide(n_mean[u][:, :]), ALU.add).then_inc(s.centred, 1)

        def deviation_dve(dve, s, i, us, r=0, rounds=1):
            for u in us:
                dve.wait_ge(s.squares, turn(i, rounds, r, u, us))
                dve.tensor_reduce(n_var[u][:, :], n_sq[u][:, :, :], AX, ALU.add).then_inc(s.var, 1)

        def inverse_dve(dve, s, i, us, u, r=0, rounds=1):
            dve.wait_ge(s.dev, turn(i, rounds, r, u, us))
            v.link(dve.reciprocal(n_r[u][:, :], n_sd[u][:, :]))

        def deviation_act(act, s, i, us, r=0, rounds=1, frm=None, twice=False):
            for u in us:
                if frm is None:
                    act.wait_ge(s.centred, turn(i, 1, 0, u, us))
                nc.scalar.activation(flat(n_sq[u][:, :, :]), flat(n_c[u][:, :, :]) if frm is None else frm(u), ACT.Square,
                                     scale=D ** -0.5).then_inc(s.squares, 1)
            for u in us:
                act.wait_ge(s.var, turn(i, rounds, r, u, us))
                if twice:
                    nc.scalar.activation(n_sd2[u][:, :], n_var[u][:, :], ACT.Sqrt, bias=eps2[0:P, :], scale=1.0 + EPS)
                nc.scalar.activation(n_sd[u][:, :], n_var[u][:, :], ACT.Sqrt, bias=eps[0:P, :]).then_inc(s.dev, 1)

        def transpose_pairs(pe, frm, to):
            for c in range(NC // 2):
                done = pe.transpose(to[:, c * P:(c + 1) * P], flat(frm[:, 2 * c:2 * c + 2, :]), ident[0:P, 0:P])
            return done

        def product_pairs(pe, u, w, to):
            for c in range(NC // 2):
                done = pe.matmul(to[0:P, c * 128:(c + 1) * 128], n_t[u][:, c * P:(c + 1) * P], w[:, :], start=True, stop=True)
            return done

        def cols3(t):
            return t.rearrange("p (c f) -> p c f", f=D)

        def scatter_pass(s, parts):
            def program(g):
                def body(i, us):
                    for rows_ready, table, rows, idx, done in parts:
                        for u in us:
                            g.wait_ge(rows_ready, turn(i, 1, 0, u, us))
                            scatter(g, table, rows[u], idx[:, (2 * i + u) * NC:(2 * i + u + 1) * NC], NC, done[u])
                for i in range((ECH + 1) // 2):
                    body(i, range(min(U, ECH - 2 * i)))
                for _, _, _, _, done in parts:
                    for u in range(U):
                        g.wait_ge(done[u], 16 * NC * ((ECH + 1 - u) // 2))
            return program

        s0 = phase("gate", "tanh_in tanh centred squares var dev x1 turned turned_sb terms row", "stored scattered")
        with nc.Block() as block:
            @block.vector
            def _(dve):
                start = v.n
                with nc.vector.Fori(0, ECH) as i:
                    v.base, v.n = i * 2 + start, 0
                    for w, rows in enumerate((xd, xs)):
                        done = dve.tensor_tensor(n_sq[w][:, :, :], rows[:, bass.ds(i * NC, NC), :], gw[:, w, :].unsqueeze(1).to_broadcast([P, NC, D]), ALU.mult)
                    v.link(done)
                    for w in range(2):
                        done = dve.tensor_reduce(heads[w][:, bass.ds(i * NC, NC)], n_sq[w][:, :, :], AX, ALU.add)
                    v.link(done)
                v.base, v.n = 0, start + 2 * ECH
                dve.tensor_tensor(heads[0][:, :], heads[0][:, :], heads[1][:, :], ALU.add).then_inc(s0.tanh_in, 1)
                dve.wait_ge(s0.tanh, 1)
                v.link(dve.scalar_tensor_tensor(heads[0][:, :], heads[0][:, :], 0.5, norm_d[:, :], ALU.mult, ALU.mult))
                v.link(dve.tensor_tensor(heads[0][:, :], heads[0][:, :], norm_s[:, :], ALU.mult))
                v.link(dve.tensor_tensor(xs, xs, wide(heads[0][:, :]), ALU.mult))
                rows_over_segments(dve, "sum", xs)

                def body(i, us):
                    for u in us:
                        v.link(dve.tensor_tensor(n_in[u][:, :, :], chunk(xs, i, u), chunk(xd, i, u), ALU.add))
                        if not is_first(i):
                            dve.wait_ge(s0.turned, 2 * i - 1 + u)
                    centre_dve(dve, s0, i, us)
                    deviation_dve(dve, s0, i, us)
                    for u in us:
                        inverse_dve(dve, s0, i, us, u)
                        if not is_first(i):
                            dve.wait_ge(s0.stored[u], 16 * i)
                            dve.wait_ge(s0.scattered[u], 16 * NC * i)
                        v.link(dve.tensor_tensor(n_c[u][:, :, :], n_c[u][:, :, :], wide(n_r[u][:, :]), ALU.mult))
                        dve.tensor_copy(r_x1[u][:, :, 0:D], n_c[u][:, :, :]).then_inc(s0.x1, 1)
                pairs(nc.vector, ECH, body, v)

            @block.scalar
            def _(act):
                act.wait_ge(s0.tanh_in, 1)
                nc.scalar.activation(heads[0][:, :], heads[0][:, :], ACT.Tanh, bias=gb[:, :]).then_inc(s0.tanh, 1)

                def body(i, us):
                    deviation_act(act, s0, i, us)
                    for u in us:
                        act.wait_ge(s0.turned, turn(i, 1, 0, u, us))
                        nc.scalar.copy(n_t[u][:, :], bank[u][:, 0:NC // 2 * P]).then_inc(s0.turned_sb, 1)
                    for u in us:
                        act.wait_ge(s0.terms, turn(i, 1, 0, u, us))
                        terms = bank[2 + u][0:P, 0:4 * NC].rearrange("p (c a) -> p c a", a=4)
                        nc.scalar.copy(chunk(own4[:, :, :], i, u), terms)
                        nc.scalar.copy(r_x1[u][:, :, D:W1ROW], terms).then_inc(s0.row, 1)
                pairs(nc.scalar, ECH, body)

            @block.tensor
            def _(pe):
                carry_pe(pe, D, "sum")

                def body(i, us):
                    for u in us:
                        pe.wait_ge(s0.x1, turn(i, 1, 0, u, us))
                        transpose_pairs(pe, n_c[u], bank[u]).then_inc(s0.turned, 1)
                    for u in us:
                        pe.wait_ge(s0.turned_sb, turn(i, 1, 0, u, us))
                        if not is_first(i):
                            pe.wait_ge(s0.row, 2 * i - 1 + u)
                        for c in range(NC // 2):
                            done = pe.matmul(bank[2 + u][0:P, 8 * c:8 * c + 8], n_t[u][:, c * P:c * P + P], wa_pair[:, :], start=True, stop=True)
                        done.then_inc(s0.terms, 1)
                pairs(nc.tensor, ECH, body)

            def store_pass(sp, s, table, rows, width):
                def body(i, us):
                    for u in us:
                        sp.wait_ge(s.row, turn(i, 1, 0, u, us))
                        sp.dma_start(edge_rows(table, i, u, width), flat(rows[u][:, :, :])).then_inc(s.stored[u], 16)
                pairs(nc.sync, ECH, body)
                for u in range(U):
                    sp.wait_ge(s.stored[u], 16 * ((ECH + 1 - u) // 2))

            @block.sync
            def _(sp):
                store_pass(sp, s0, E1, r_x1, W1ROW)

            @block.gpsimd
            def _(g):
                scatter_pass(s0, [(s0.row, X1, r_x1, scat_i, s0.scattered)])(g)

        def attention_dve(dve, s, rows, at):
            for h in range(H):
                dve.tensor_copy(dens[h][:, :], own4[:, :, 2 + h])
                v.link(dve.tensor_tensor(selfs[h][:, :], own4[:, :, h], own4[:, :, 2 + h], ALU.add))
            for h in range(H):
                v.link(dve.scalar_tensor_tensor(selfs[h][:, :], selfs[h][:, :], 0.2, selfs[h][:, :], ALU.mult, ALU.max))
            over_segments(dve, "hold", [d[:, :] for d in dens])
            for h in range(H):
                v.link(dve.tensor_tensor(heads[h][:, :], rows[:, :, at + h], dens[h][:, :], ALU.add))
                v.link(dve.scalar_tensor_tensor(heads[h][:, :], heads[h][:, :], 0.2, heads[h][:, :], ALU.mult, ALU.max))
                v.link(dve.tensor_copy(tops[h][:, :], heads[h][:, :]))
            over_segments(dve, "max", [t[:, :] for t in tops])
            for h in range(H):
                v.link(dve.tensor_tensor(tops[h][:, :], tops[h][:, :], selfs[h][:, :], ALU.max))
            over_segments(dve, "hold", [t[:, :] for t in tops])
            for h in range(H):
                dve.tensor_tensor(heads[h][:, :], heads[h][:, :], tops[h][:, :], ALU.subtract)
                v.link(dve.tensor_tensor(selfs[h][:, :], selfs[h][:, :], tops[h][:, :], ALU.subtract))
                done = dve.tensor_scalar(selfs[h][:, :], selfs[h][:, :], 0.0, None, ALU.min)
            done.then_inc(s.logits, 1)
            dve.wait_ge(s.exps, 1)
            for h in range(H):
                v.link(dve.tensor_copy(dens[h][:, :], heads[h][:, :]))
            over_segments(dve, "sum", [d[:, :] for d in dens])
            for h in range(H):
                v.link(dve.tensor_tensor(dens[h][:, :], dens[h][:, :], selfs[h][:, :], ALU.add))
                v.link(dve.tensor_scalar(dens[h][:, :], dens[h][:, :], 0.5, None, ALU.max))
                v.link(dve.reciprocal(dens[h][:, :], dens[h][:, :]))

        def attention_act(act, s):
            act.wait_ge(s.logits, 1)
            for t in (*heads, *selfs):
                done = nc.scalar.activation(t[:, :], t[:, :], ACT.Exp)
            done.then_inc(s.exps, 1)

        def attention_pe(pe):
            over_segments_pe(pe, "hold", 2)
            over_segments_pe(pe, "max", 2)
            over_segments_pe(pe, "hold", 2)
            over_segments_pe(pe, "sum", 2)

        s1 = phase("att1", "gathered logits exps x turned turned_sb o1 o1_sb h2 row", "loaded stored scattered")
        xa, vb = rows_of(0, W1ROW), rows_of(J * W1ROW, D)
        with nc.Block() as block:
            @block.gpsimd
            def _(g):
                gather(g, xa, X1, src_i, s1.gathered)
                scatter_pass(s1, [(s1.row, H2, r_h2, scat_i, s1.scattered)])(g)

            @block.vector
            def _(dve):
                dve.wait_ge(s1.gathered, ALL)
                attention_dve(dve, s1, xa, D)
                dve.tensor_tensor(vb, xa[:, :, 0:D], wide(heads[1][:, :]), ALU.mult)
                v.link(dve.tensor_tensor(xa[:, :, 0:D], xa[:, :, 0:D], wide(heads[0][:, :]), ALU.mult))
                sums = (xa[:, :, 0:D], vb)
                for rows in sums:
                    rows_over_segments(dve, "sum", rows)

                def body(i, us):
                    for u in us:
                        dve.wait_ge(s1.loaded[u], 16 * i + 16)
                        if not is_first(i):
                            dve.wait_ge(s1.turned, 2 * i - 1 + u)
                        for h in range(H):
                            tmp = (n_sq, n_in)[h][u][:, :, :]
                            v.link(dve.tensor_tensor(tmp, r_x1[u][:, :, 0:D], wide(chunk(selfs[h], i, u)), ALU.mult))
                            v.link(dve.tensor_tensor(tmp, tmp, chunk(sums[h], i, u), ALU.add))
                            done = dve.tensor_tensor(e_dup[u][:, :, h, :], tmp, wide(chunk(dens[h], i, u)), ALU.mult)
                        done.then_inc(s1.x, 1)
                pairs(nc.vector, ECH, body, v)

            @block.tensor
            def _(pe):
                attention_pe(pe)
                for _ in range(H):
                    carry_pe(pe, D, "sum")

                def body(i, us):
                    for u in us:
                        pe.wait_ge(s1.x, turn(i, 1, 0, u, us))
                        for c in range(NC):
                            done = pe.transpose(bank[c // 4][:, c % 4 * P:(c % 4 + 1) * P], e_dup[u][:, c, :, :].rearrange("p h f -> p (h f)"), ident[0:P, 0:P])
                        done.then_inc(s1.turned, 1)
                        pe.wait_ge(s1.turned_sb, turn(i, 1, 0, u, us))
                        for half in range(2):
                            done = pe.matmul(bank[2 + half][:, 0:NC // 2 * P], w1_heads[:, :], n_t[half][:, :], start=True, stop=True)
                        done.then_inc(s1.o1, 1)
                        pe.wait_ge(s1.o1_sb, turn(i, 1, 0, u, us))
                        if u or not is_first(i):
                            pe.wait_ge(s1.row, 2 * i + u)
                        for c in range(NC):
                            done = pe.matmul(h2_slot(c), o1_t[:, c // 4, c % 4 * P:c % 4 * P + P], w2_ext[:, :], start=True, stop=True)
                        done.then_inc(s1.h2, 1)
                pairs(nc.tensor, ECH, body)

            @block.scalar
            def _(act):
                attention_act(act, s1)

                def body(i, us):
                    for u in us:
                        act.wait_ge(s1.turned, turn(i, 1, 0, u, us))
                        nc.scalar.copy(n_t[0][:, :], bank[0][:, 0:NC // 2 * P])
                        nc.scalar.copy(n_t[1][:, :], bank[1][:, 0:NC // 2 * P]).then_inc(s1.turned_sb, 1)
                        act.wait_ge(s1.o1, turn(i, 1, 0, u, us))
                        for half in range(2):
                            done = nc.scalar.activation(o1_t[:, half, :], bank[2 + half][:, 0:NC // 2 * P], ACT.Identity, bias=b1_col[:, :])
                        done.then_inc(s1.o1_sb, 1)
                        act.wait_ge(s1.h2, turn(i, 1, 0, u, us))
                        if not is_first(i):
                            act.wait_ge(s1.stored[u], 16 * i)
                            act.wait_ge(s1.scattered[u], 16 * NC * i)
                        for b, cols in enumerate((3, 3, 2)):
                            at = bank[4 + b][0:P, 0:cols * W2ROW]
                            nc.scalar.copy(own4[:, bass.ds((2 * i + u) * NC + 3 * b, cols), :], at.rearrange("p (c w) -> p c w", w=W2ROW)[:, :, 2 * D:W2ROW])
                            done = nc.scalar.copy(flat(r_h2[u][:, 3 * b:3 * b + cols, :]), at)
                        done.then_inc(s1.row, 1)
                pairs(nc.scalar, ECH, body)

            @block.sync
            def _(sp):
                def load(i, u):
                    sp.dma_start(flat(r_x1[u][:, :, :]), edge_rows(E1, i, u, W1ROW)).then_inc(s1.loaded[u], 16)

                def body(i, us):
                    for u in us:
                        if not is_first(i):
                            sp.wait_ge(s1.x, 2 * i - 1 + u)
                        load(i, u)
                    for u in us:
                        sp.wait_ge(s1.row, turn(i, 1, 0, u, us))
                        sp.dma_start(edge_rows(E2, i, u, W2ROW), flat(r_h2[u][:, :, :])).then_inc(s1.stored[u], 16)
                pairs(nc.sync, ECH, body)
                for u in range(U):
                    sp.wait_ge(s1.stored[u], 16 * ((ECH + 1 - u) // 2))

        s2 = phase("att2", "gathered logits exps centred squares var dev row x3", "loaded scattered scattered3")
        ha = rows_of(0, W2ROW)
        with nc.Block() as block:
            @block.gpsimd
            def _(g):
                gather(g, ha, H2, src_i, s2.gathered)
                scatter_pass(s2, [(s2.row, X2, r_x2, scat_i, s2.scattered), (s2.x3, X3, n_out, scat_i, s2.scattered3)])(g)

            @block.vector
            def _(dve):
                dve.wait_ge(s2.gathered, ALL)
                attention_dve(dve, s2, ha, 2 * D)
                for h in range(H):
                    v.link(dve.scalar_tensor_tensor(selfs[h][:, :], selfs[h][:, :], 1.0 / H, dens[h][:, :], ALU.mult, ALU.mult))
                over_segments(dve, "hold", [d[:, :] for d in dens])
                for h in range(H):
                    v.link(dve.scalar_tensor_tensor(heads[h][:, :], heads[h][:, :], 1.0 / H, dens[h][:, :], ALU.mult, ALU.mult))
                for h in range(H):
                    part = ha[:, :, h * D:h * D + D]
                    v.link(dve.tensor_tensor(part, part, wide(heads[h][:, :]), ALU.mult))
                v.link(dve.tensor_tensor(ha[:, :, 0:D], ha[:, :, 0:D], ha[:, :, D:2 * D], ALU.add))
                rows_over_segments(dve, "sum", ha[:, :, 0:D])

                def body(i, us):
                    for u in us:
                        dve.wait_ge(s2.loaded[u], 32 * i + 32)
                        y = n_in[u][:, :, :]
                        v.link(dve.tensor_tensor(y, r_h2[u][:, :, 0:D], wide(chunk(selfs[0], i, u)), ALU.mult))
                        v.link(dve.tensor_tensor(n_c[u][:, :, :], r_h2[u][:, :, D:2 * D], wide(chunk(selfs[1], i, u)), ALU.mult))
                        v.link(dve.tensor_tensor(y, y, n_c[u][:, :, :], ALU.add))
                        v.link(dve.tensor_tensor(y, y, chunk(ha[:, :, 0:D], i, u), ALU.add))
                        v.link(dve.tensor_tensor(y, y, r_x1[u][:, :, 0:D], ALU.add))
                        v.link(dve.tensor_tensor(y, y, tall(b2_all), ALU.add))
                    centre_dve(dve, s2, i, us)
                    deviation_dve(dve, s2, i, us)
                    for u in us:
                        inverse_dve(dve, s2, i, us, u)
                        if not is_first(i):
                            dve.wait_ge(s2.scattered[u], 16 * NC * i)
                            dve.wait_ge(s2.scattered3[u], 16 * NC * i)
                        v.link(dve.reciprocal(n_r2[u][:, :], n_sd2[u][:, :]))
                        dve.tensor_tensor(r_x2[u][:, :, :], n_c[u][:, :, :], wide(n_r[u][:, :]), ALU.mult).then_inc(s2.row, 1)
                        dve.tensor_tensor(n_out[u][:, :, :], n_c[u][:, :, :], wide(n_r2[u][:, :]), ALU.mult).then_inc(s2.x3, 1)
                pairs(nc.vector, ECH, body, v)

            @block.tensor
            def _(pe):
                attention_pe(pe)
                over_segments_pe(pe, "hold", 2)
                carry_pe(pe, D, "sum")

            @block.scalar
            def _(act):
                attention_act(act, s2)
                pairs(nc.scalar, ECH, lambda i, us: deviation_act(act, s2, i, us, twice=True))

            @block.sync
            def _(sp):
                def body(i, us):
                    for u in us:
                        if not is_first(i):
                            sp.wait_ge(s2.centred, 2 * i - 1 + u)
                        sp.dma_start(flat(r_x1[u][:, :, :]), edge_rows(E1, i, u, W1ROW)).then_inc(s2.loaded[u], 16)
                        sp.dma_start(flat(r_h2[u][:, :, :]), edge_rows(E2, i, u, W2ROW)).then_inc(s2.loaded[u], 16)
                pairs(nc.sync, ECH, body)

        s3 = phase("cos", "ordered outside gathered norms roots logits exps centred squares var dev x3 turned turned_sb y row", "scattered scattered_out")
        xr, xc = rows_of(0, D), rows_of(J * D, D)
        col_i = norm_s[:, :].bitcast(I32)
        with nc.Block() as block:
            @block.sync
            def _(sp):
                sp.wait_ge(s3.outside, 1)
                load_order(sp, SORTED[0, 0:EDGES], s3.ordered)
                sp.dma_start(col_i, edges_of(SORTED[1, 0:EDGES])).then_inc(s3.ordered, 16)

            @block.gpsimd
            def _(g):
                g.wait_ge(s3.ordered, 6 * 16)
                gather(g, xr, X2, key_i, s3.gathered)
                gather(g, xc, X2, col_i, s3.gathered)
                scatter_pass(s3, [(s3.x3, X3, r_x2, src_scat_i, s3.scattered), (s3.row, out, n_out, src_scat_i, s3.scattered_out)])(g)

            @block.vector
            def _(dve):
                dve.memset(prev_i[:, :], -1)
                dve.memset(next_i[:, :], -1).then_inc(s3.outside, 1)
                dve.wait_ge(s3.ordered, 6 * 16)
                order_dve(dve)
                last_only(dve, src_scat_i[:, :], heads[0][:, :])
                dve.wait_ge(s3.gathered, 2 * ALL)
                start = v.n
                products = ((n_sq[0], xr, xr, tops[0]), (n_sq[1], xc, xc, tops[1]), (n_in[0], xr, xc, heads[0]))
                with nc.vector.Fori(0, ECH) as i:
                    v.base, v.n = i * 2 + start, 0
                    for tmp, a, b, _ in products:
                        done = dve.tensor_tensor(tmp[:, :, :], a[:, bass.ds(i * NC, NC), :], b[:, bass.ds(i * NC, NC), :], ALU.mult)
                    v.link(done)
                    for tmp, _, _, to in products:
                        done = dve.tensor_reduce(to[:, bass.ds(i * NC, NC)], tmp[:, :, :], AX, ALU.add)
                    v.link(done)
                v.base, v.n = 0, start + 2 * ECH
                dve.tensor_copy(dens[0][:, :], tops[0][:, :]).then_inc(s3.norms, 1)
                dve.wait_ge(s3.roots, 1)
                for t in tops:
                    v.link(dve.reciprocal(t[:, :], t[:, :]))
                    v.link(dve.tensor_tensor(heads[0][:, :], heads[0][:, :], t[:, :], ALU.mult))
                v.link(dve.tensor_scalar(heads[0][:, :], heads[0][:, :], beta_all[:, :], None, ALU.mult))
                v.link(dve.tensor_copy(tops[0][:, :], heads[0][:, :]))
                over_segments(dve, "max", [tops[0][:, :]])
                over_segments(dve, "hold", [tops[0][:, :]])
                dve.tensor_tensor(heads[0][:, :], heads[0][:, :], tops[0][:, :], ALU.subtract).then_inc(s3.logits, 1)
                dve.wait_ge(s3.exps, 1)
                v.link(dve.tensor_copy(dens[0][:, :], heads[0][:, :]))
                over_segments(dve, "sum", [dens[0][:, :]])
                v.link(dve.tensor_scalar(dens[0][:, :], dens[0][:, :], 1e-16, None, ALU.max))
                v.link(dve.reciprocal(dens[0][:, :], dens[0][:, :]))
                v.link(dve.tensor_tensor(xc, xc, wide(heads[0][:, :]), ALU.mult))
                rows_over_segments(dve, "sum", xc)

                def body(i, us):
                    for u in us:
                        v.link(dve.tensor_tensor(n_in[u][:, :, :], chunk(xc, i, u), wide(chunk(dens[0], i, u)), ALU.mult))
                        v.link(dve.tensor_tensor(n_in[u][:, :, :], n_in[u][:, :, :], chunk(xr, i, u), ALU.add))
                    centre_dve(dve, s3, i, us)
                    deviation_dve(dve, s3, i, us, 0, 2)
                    for u in us:
                        inverse_dve(dve, s3, i, us, u, 0, 2)
                        if not is_first(i):
                            dve.wait_ge(s3.scattered[u], 16 * NC * i)
                            dve.wait_ge(s3.scattered_out[u], 16 * NC * i)
                        dve.tensor_tensor(r_x2[u][:, :, :], n_c[u][:, :, :], wide(n_r[u][:, :]), ALU.mult).then_inc(s3.x3, 1)
                    deviation_dve(dve, s3, i, us, 1, 2)
                    for u in us:
                        inverse_dve(dve, s3, i, us, u, 1, 2)
                        dve.tensor_tensor(n_out[u][:, :, :], cols3(bank[2 + u][0:P, :]), wide(n_r[u][:, :]), ALU.mult).then_inc(s3.row, 1)
                pairs(nc.vector, ECH, body, v)

            @block.tensor
            def _(pe):
                segments_pe(pe)
                over_segments_pe(pe, "max", 1)
                over_segments_pe(pe, "hold", 1)
                over_segments_pe(pe, "sum", 1)
                carry_pe(pe, D, "sum")

                def body(i, us):
                    for u in us:
                        pe.wait_ge(s3.x3, turn(i, 1, 0, u, us))
                        transpose_pairs(pe, r_x2[u], bank[u]).then_inc(s3.turned, 1)
                    for u in us:
                        pe.wait_ge(s3.turned_sb, turn(i, 1, 0, u, us))
                        if not is_first(i):
                            pe.wait_ge(s3.row, 2 * i - 1 + u)
                        pe.matmul(bank[2 + u][0:P, :], ones[0:1, 0:P], flat(wn_bias[:, :, :]), start=True, stop=False)
                        for c in range(NC // 2):
                            done = pe.matmul(bank[2 + u][0:P, c * 128:(c + 1) * 128], n_t[u][:, c * P:(c + 1) * P], wn_pair[:, :],
                                             start=False, stop=c == NC // 2 - 1)
                        done.then_inc(s3.y, 1)
                pairs(nc.tensor, ECH, body)

            @block.scalar
            def _(act):
                act.wait_ge(s3.norms, 1)
                for t in tops:
                    done = nc.scalar.activation(t[:, :], t[:, :], ACT.Sqrt, bias=eps8[0:P, :])
                done.then_inc(s3.roots, 1)
                act.wait_ge(s3.logits, 1)
                nc.scalar.activation(heads[0][:, :], heads[0][:, :], ACT.Exp).then_inc(s3.exps, 1)

                def body(i, us):
                    deviation_act(act, s3, i, us, 0, 2)
                    for u in us:
                        act.wait_ge(s3.turned, turn(i, 1, 0, u, us))
                        nc.scalar.copy(n_t[u][:, :], bank[u][:, 0:NC // 2 * P]).then_inc(s3.turned_sb, 1)
                    for u in us:
                        act.wait_ge(s3.y, turn(i, 1, 0, u, us))
                    deviation_act(act, s3, i, us, 1, 2, lambda u: bank[2 + u][0:P, :])
                pairs(nc.scalar, ECH, body)

        s4 = phase("msg", "ordered outside gathered turned turned_sb proj msg sum_turned sum_turned_sb y x centred squares var dev row", "loaded scattered")
        with nc.Block() as block:
            @block.sync
            def _(sp):
                sp.wait_ge(s4.outside, 1)
                load_order(sp, dst, s4.ordered)

                def body(i, us):
                    for u in us:
                        if not is_first(i):
                            sp.wait_ge(s4.turned, 2 * i - 1 + u)
                        sp.dma_start(flat(n_in[u][:, :, :]), edge_rows(edge_attr, i, u, D)).then_inc(s4.loaded[u], 16)
                pairs(nc.sync, ECH, body)

            @block.gpsimd
            def _(g):
                gather(g, xs, X3, src_i, s4.gathered)
                gather(g, xd, X3, dst_i, s4.gathered)
                scatter_pass(s4, [(s4.row, out, n_out, scat_i, s4.scattered)])(g)

            @block.vector
            def _(dve):
                dve.memset(prev_i[:, :], -1)
                dve.memset(next_i[:, :], -1).then_inc(s4.outside, 1)
                dve.wait_ge(s4.ordered, 5 * 16)
                order_dve(dve)
                dve.wait_ge(s4.gathered, 2 * ALL)

                def message(i, us):
                    for u in us:
                        dve.wait_ge(s4.proj, turn(i, 1, 0, u, us))
                        v.link(dve.tensor_tensor(n_sq[u][:, :, :], cols3(bank[2 + u][0:P, :]), chunk(xs, i, u), ALU.add))
                        v.link(dve.tensor_tensor(n_sq[u][:, :, :], n_sq[u][:, :, :], tall(bl_all), ALU.add))
                        dve.tensor_scalar(chunk(xs, i, u), n_sq[u][:, :, :], 0.0, None, ALU.max).then_inc(s4.msg, 1)
                pairs(nc.vector, ECH, message, v)
                dve.wait_ge(s4.msg, ECH)
                rows_over_segments(dve, "sum", xs)

                def body(i, us):
                    for u in us:
                        dve.tensor_tensor(n_in[u][:, :, :], chunk(xs, i, u), chunk(xd, i, u), ALU.add).then_inc(s4.x, 1)
                    for u in us:
                        dve.wait_ge(s4.y, turn(i, 1, 0, u, us))
                        v.link(dve.tensor_tensor(n_in[u][:, :, :], cols3(bank[2 + u][0:P, :]), chunk(xd, i, u), ALU.add))
                        v.link(dve.tensor_tensor(n_in[u][:, :, :], n_in[u][:, :, :], tall(bn_all), ALU.add))
                    centre_dve(dve, s4, i, us)
                    deviation_dve(dve, s4, i, us)
                    for u in us:
                        inverse_dve(dve, s4, i, us, u)
                        if not is_first(i):
                            dve.wait_ge(s4.scattered[u], 16 * NC * i)
                        dve.tensor_tensor(n_out[u][:, :, :], n_c[u][:, :, :], wide(n_r[u][:, :]), ALU.mult).then_inc(s4.row, 1)
                pairs(nc.vector, ECH, body, v)

            @block.tensor
            def _(pe):
                segments_pe(pe)

                def project(i, us):
                    for u in us:
                        pe.wait_ge(s4.loaded[u], 16 * i + 16)
                        if not is_first(i):
                            pe.wait_ge(s4.turned_sb, 2 * i - 1 + u)
                        transpose_pairs(pe, n_in[u], bank[4 + u]).then_inc(s4.turned, 1)
                    for u in us:
                        pe.wait_ge(s4.turned_sb, turn(i, 1, 0, u, us))
                        if not is_first(i):
                            pe.wait_ge(s4.msg, 2 * i - 1 + u)
                        product_pairs(pe, u, wl_diag, bank[2 + u]).then_inc(s4.proj, 1)
                pairs(nc.tensor, ECH, project)
                carry_pe(pe, D, "sum")

                def body(i, us):
                    for u in us:
                        pe.wait_ge(s4.x, turn(i, 1, 0, u, us))
                        transpose_pairs(pe, n_in[u], bank[4 + u]).then_inc(s4.sum_turned, 1)
                    for u in us:
                        pe.wait_ge(s4.sum_turned_sb, turn(i, 1, 0, u, us))
                        product_pairs(pe, u, wn_diag, bank[2 + u]).then_inc(s4.y, 1)
                pairs(nc.tensor, ECH, body)

            @block.scalar
            def _(act):
                def project(i, us):
                    for u in us:
                        act.wait_ge(s4.turned, turn(i, 1, 0, u, us))
                        if not is_first(i):
                            act.wait_ge(s4.proj, 2 * i - 1 + u)
                        nc.scalar.copy(n_t[u][:, :], bank[4 + u][:, 0:NC // 2 * P]).then_inc(s4.turned_sb, 1)
                pairs(nc.scalar, ECH, project)

                def body(i, us):
                    for u in us:
                        act.wait_ge(s4.sum_turned, turn(i, 1, 0, u, us))
                        nc.scalar.copy(n_t[u][:, :], bank[4 + u][:, 0:NC // 2 * P]).then_inc(s4.sum_turned_sb, 1)
                    deviation_act(act, s4, i, us)
                pairs(nc.scalar, ECH, body)

_INS = ['x', 'src', 'dst', 'edge_attr_64', 'L0_gnn_gate_w', 'L0_gnn_gate_b', 'L1_gnn_W1', 'L1_gnn_as1', 'L1_gnn_ad1', 'L1_gnn_b1', 'L1_gnn_W2', 'L1_gnn_as2', 'L1_gnn_ad2', 'L1_gnn_b2', 'L2_gnn_beta', 'L3_gnn_Wl', 'L3_gnn_bl', 'L3_gnn_Wn', 'L3_gnn_bn']


def kernel(**inputs):
    import numpy as np
    import concourse.bacc as bacc
    from concourse import mybir
    from concourse.bass_utils import run_bass_kernel_spmd

    nc = bacc.Bacc("TRN2", target_bir_lowering=False, num_devices=1)
    arrays, args = {}, []
    for name in _INS:
        a = np.ascontiguousarray(inputs[name])
        arrays[f"in_{name}_dram"] = a
        args.append(nc.dram_tensor(f"in_{name}_dram", a.shape, mybir.dt.from_np(a.dtype), kind="ExternalInput").ap())
    out = nc.dram_tensor("out_dram", (100000, 64), mybir.dt.float32, kind="ExternalOutput").ap()
    build(nc, *args, out)
    r = run_bass_kernel_spmd(nc, [arrays], core_ids=[0])
    return r.results[0]["out_dram"]
```

```python
from contextlib import ExitStack

import concourse.bass as bass
from concourse import mybir

F32 = mybir.dt.float32
I32 = mybir.dt.int32
BF16 = mybir.dt.bfloat16
ALU = mybir.AluOpType
ACT = mybir.ActivationFunctionType
AX = mybir.AxisListType.X

NODES, EDGES, D, H = 100000, 25000, 64, 2
P = 125
NJ = NODES // P
J = EDGES // P
NC = 8
EC = 4
U = 2
EPS = 1e-5
GROUPS = 5
W1ROW, W2ROW = D + 5, 2 * D + 4
NW = W2ROW + 4 + D
SORT = 32768
FAR = 1 << 20
LOW = -1e38



class Chain:

    def __init__(self, eng, sem):
        self.eng, self.sem, self.base, self.n = eng, sem, 0, 0

    def link(self, ins):
        self.n += 1
        ins.then_inc(self.sem, 1)
        self.eng.wait_ge(self.sem, self.base + self.n)


def pairs(eng, chunks, body, chain=None):
    before = chain.n if chain else 0
    body(0, range(2))
    per = chain.n - before if chain else 0
    with eng.Fori(1, chunks // 2) as i:
        if chain:
            total = chain.n
            chain.base, chain.n = (i - 1) * per + total, 0
        body(i, range(2))
        if chain:
            assert chain.n == per
    if chain:
        chain.base, chain.n = 0, total + (chunks // 2 - 1) * per
    if chunks % 2:
        body(chunks // 2, range(1))


def turn(i, rounds, r, u, us):
    return i * 2 * rounds + r * len(us) + u + 1


def skewed(eng, pairs_n, body, chain=None):
    body(0, True, False)
    before = chain.n if chain else 0
    body(1, True, True)
    per = chain.n - before if chain else 0
    with eng.Fori(2, pairs_n) as i:
        if chain:
            total = chain.n
            chain.base, chain.n = (i - 2) * per + total, 0
        body(i, True, True)
        if chain:
            assert chain.n == per
    if chain:
        chain.base, chain.n = 0, total + (pairs_n - 2) * per
    body(pairs_n, False, True)


def build(nc, x, src, dst, edge_attr, gate_w, gate_b, W1, as1, ad1, b1, W2, as2, ad2, b2, beta, Wl, bl, Wn, bn, out):
    ctx = ExitStack()
    with ctx:
        def sb(name, shape, dt=F32):
            return ctx.enter_context(nc.sbuf_tensor(name, shape, dt))

        def sem(name):
            return ctx.enter_context(nc.semaphore(name))

        def sems(names):
            return [sem(n) for n in names.split()]

        ident = sb("ident", [128, 128])
        eps = sb("eps", [128, 1])
        eps8 = sb("eps8", [128, 1])
        w1_dup = sb("w1_dup", [128, 128])
        w1_heads = sb("w1_heads", [128, 128])
        w1_t = sb("w1_t", [128, D])
        w2_ext = sb("w2_ext", [128, 132])
        w2_mean = sb("w2_mean", [128, D])
        wa = sb("wa", [128, 4])
        node_w = sb("node_w", [D + 1, NW])
        out_w = sb("out_w", [D, D])
        wn_pair = sb("wn_pair", [128, 128])
        wn_bias = sb("wn_bias", [3, NC * D], BF16)
        wl_bias = sb("wl_bias", [3, NC * D], BF16)
        ones3 = sb("ones3", [3, 128], BF16)
        parts = [sb(f"bias_parts{n}", [1, 3, D], BF16) for n in range(2)]
        piece = sb("bias_part", [1, D], BF16)
        rest = sb("bias_rest", [1, D])
        wa_pair = sb("wa_pair", [128, 8])
        att1 = sb("att1", [128, 4, D])
        att2 = sb("att2", [128, 4, D])
        att_tmp = sb("att_tmp", [128, 4, D])
        wn_diag = sb("wn_diag", [128, 128])
        wl_diag = sb("wl_diag", [128, 128])
        bias_row = sb("bias_row", [1, NW])
        r_x1 = [sb(f"r_x1{u}", [P, NC, W1ROW]) for u in range(U)]
        x_t = [sb(f"x_t{u}", [D + 1, NC * P]) for u in range(U)]
        row_mean = sb("row_mean", [128, 1])
        b1_col = sb("b1_col", [128, 1])
        b2_row = sb("b2_row", [1, D])
        b2_all = sb("b2_all", [P, D])
        bn_row = sb("bn_row", [1, D])
        bn_all = sb("bn_all", [P, D])
        bl_row = sb("bl_row", [1, D])
        gw = sb("gw", [P, 2, D])
        gb = sb("gb", [P, 1])
        beta_all = sb("beta_all", [P, 1])

        banks = ctx.enter_context(nc.psum_tensor("banks", [128, 8, 512], F32))
        bank = [banks[:, i, :] for i in range(8)]

        s_v, s_a, s_g = sems("s_v s_a s_g")
        v = Chain(nc.vector, s_v)
        pool = Chain(nc.gpsimd, s_g)

        X1 = nc.dram_tensor("x1_rows", [NODES, W1ROW], F32).ap()
        H2 = nc.dram_tensor("h2_rows", [NODES, W2ROW], F32).ap()
        X2 = nc.dram_tensor("x2_rows", [NODES, D], F32).ap()
        X3 = nc.dram_tensor("x3_rows", [NODES, D], F32).ap()
        NORM = nc.dram_tensor("norm_rows", [NODES, 1], F32).ap()
        E1 = nc.dram_tensor("x1_edge_rows", [EDGES, W1ROW], F32).ap()
        E2 = nc.dram_tensor("h2_edge_rows", [EDGES, W2ROW], F32).ap()
        EP = nc.dram_tensor("edge_projections", [EDGES, D], F32).ap()
        SORTED = nc.dram_tensor("sorted_pairs", [2, SORT], I32).ap()

        s_zero, s_const, s_w, s_wd, s_w1t, s_w1sb, s_mixp, s_bias = sems("s_zero s_const s_w s_wd s_w1t s_w1sb s_mixp s_bias")
        loads = [
            (w1_dup[0:D, :], W1), (w1_dup[D:128, :], W1),
            (w2_ext[:, 0:128], W2), (out_w[0:D, :], Wn),
            (att1[:, 0:2, :], as1.unsqueeze(0).to_broadcast([128, H, D])),
            (att1[:, 2:4, :], ad1.unsqueeze(0).to_broadcast([128, H, D])),
            (att2[:, 0:2, :], as2.unsqueeze(0).to_broadcast([128, H, D])),
            (att2[:, 2:4, :], ad2.unsqueeze(0).to_broadcast([128, H, D])),
            (b1_col[:, :], b1.unsqueeze(1)), (b2_row[:, :], b2.unsqueeze(0)), (bn_row[:, :], bn.unsqueeze(0)),
            (b2_all[:, :], b2.unsqueeze(0).to_broadcast([P, D])), (bn_all[:, :], bn.unsqueeze(0).to_broadcast([P, D])),
            (bl_row[:, :], bl.unsqueeze(0)),
            (gw[:, :, :], gate_w.rearrange("(s f) o -> o s f", s=2).to_broadcast([P, 2, D])),
            (gb[:, :], gate_b.unsqueeze(0).to_broadcast([P, 1])),
            (beta_all[:, :], beta.unsqueeze(0).to_broadcast([P, 1])),
        ]
        with nc.Block() as block:
            @block.sync
            def _(sp):
                for to, frm in loads:
                    sp.dma_start(to, frm).then_inc(s_w, 16)
                sp.wait_ge(s_zero, 1)
                for h in range(2):
                    half = slice(h * D, h * D + D)
                    sp.dma_start(w1_heads[half, half], W1[:, half]).then_inc(s_wd, 16)
                    sp.dma_start(wl_diag[half, half], Wl).then_inc(s_wd, 16)
                    sp.dma_start(wn_diag[half, half], Wn).then_inc(s_wd, 16)
                sp.wait_ge(s_bias, 1)
                sp.dma_start(node_w[D:D + 1, :], bias_row[:, :]).then_inc(s_wd, 16)
                for h in range(2):
                    half = slice(h * D, h * D + D)
                    sp.dma_start(wn_pair[half, half], out_w[:, :]).then_inc(s_wd, 16)
                for to, frm in ((wn_bias, parts[0]), (wl_bias, parts[1])):
                    for k in range(3):
                        sp.dma_start(to[k:k + 1, :].rearrange("o (c f) -> o c f", f=D), frm[:, k].unsqueeze(1).to_broadcast([1, NC, D])).then_inc(s_wd, 16)
                sp.wait_ge(s_wd, 15 * 16)

            @block.gpsimd
            def _(g):
                pool.link(g.memset(ident[:, :], 0.0))
                pool.link(g.affine_select(out=ident[:, :], in_=ident[:, :], compare_op=ALU.not_equal, fill=1.0,
                                          base=0, pattern=[[-1, 128]], channel_multiplier=1))
                g.memset(eps[:, :], EPS)
                g.memset(eps8[:, :], 1e-8).then_inc(s_const, 1)

            @block.vector
            def _(dve):
                for t in (w1_heads, wl_diag, wa_pair, wn_pair):
                    dve.memset(t[:, :], 0.0)
                dve.memset(wn_diag[:, :], 0.0).then_inc(s_zero, 1)
                dve.wait_ge(s_w, 16 * len(loads))
                for k in range(4):
                    part = slice((k % H) * D, (k % H) * D + D)
                    v.link(dve.tensor_tensor(att_tmp[:, k, :], w1_dup[:, part], att1[:, k, :], ALU.mult))
                v.link(dve.tensor_reduce(wa[:, :], att_tmp[:, :, :], AX, ALU.add))
                for h in range(2):
                    half = slice(h * D, h * D + D)
                    dve.tensor_copy(wa_pair[half, 4 * h:4 * h + 4], wa[half, :])
                for k in range(4):
                    part = slice((k % H) * D, (k % H) * D + D)
                    v.link(dve.tensor_tensor(att_tmp[:, k, :], w2_ext[:, part], att2[:, k, :], ALU.mult))
                v.link(dve.tensor_reduce(w2_ext[:, 128:132], att_tmp[:, :, :], AX, ALU.add))
                v.link(dve.tensor_tensor(w2_mean[:, :], w2_ext[:, 0:D], w2_ext[:, D:128], ALU.add))
                v.link(dve.tensor_scalar(w2_mean[:, :], w2_mean[:, :], 0.5, None, ALU.mult))
                dve.wait_ge(s_w1t, 1)
                dve.tensor_copy(w1_t[:, :], bank[0][:, 0:D]).then_inc(s_w1sb, 1)
                dve.wait_ge(s_mixp, 1)

                def centre(rows, m):
                    v.link(dve.tensor_reduce(row_mean[0:rows, :], m, AX, ALU.add))
                    v.link(dve.tensor_scalar(row_mean[0:rows, :], row_mean[0:rows, :], 1.0 / D, None, ALU.mult))
                    v.link(dve.tensor_scalar(m, m, row_mean[0:rows, :], None, ALU.subtract))

                y_cols = slice(W2ROW + 4, NW)
                v.link(dve.tensor_copy(node_w[0:D, 0:W2ROW], bank[1][0:D, 0:W2ROW]))
                v.link(dve.tensor_copy(node_w[0:D, W2ROW:W2ROW + 4], wa[0:D, :]))
                v.link(dve.tensor_tensor(node_w[0:D, y_cols], bank[1][0:D, W2ROW:W2ROW + D], ident[0:D, 0:D], ALU.add))
                centre(D, node_w[0:D, y_cols])
                v.link(dve.tensor_tensor(out_w[0:D, :], out_w[0:D, :], ident[0:D, 0:D], ALU.add))
                centre(D, out_w[0:D, :])
                v.link(dve.memset(bias_row[:, :], 0.0))
                v.link(dve.tensor_copy(bias_row[:, 0:W2ROW], bank[2][0:1, 0:W2ROW]))
                v.link(dve.tensor_tensor(bias_row[:, y_cols], bank[2][0:1, W2ROW:W2ROW + D], b2_row[:, :], ALU.add))
                centre(1, bias_row[:, y_cols])
                centre(1, bn_row[:, :])
                v.link(dve.memset(ones3[:, :], 1.0))
                for row, to in ((bn_row, parts[0]), (bl_row, parts[1])):
                    v.link(dve.tensor_copy(rest[:, :], row[:, :]))
                    for k in range(3):
                        v.link(dve.tensor_copy(piece[:, :], rest[:, :]))
                        v.link(dve.tensor_copy(to[:, k], piece[:, :]))
                        v.link(dve.tensor_tensor(rest[:, :], rest[:, :], piece[:, :], ALU.subtract))
                for u in range(U):
                    done = dve.memset(r_x1[u][:, :, D:D + 1], 1.0)
                done.then_inc(s_bias, 1)

            @block.tensor
            def _(pe):
                pe.wait_ge(s_w, 16 * len(loads))
                pe.wait_ge(s_const, 1)
                pe.transpose(bank[0][:, 0:D], w1_dup[0:D, :], ident[0:D, 0:D]).then_inc(s_w1t, 1)
                pe.wait_ge(s_w1sb, 1)
                for rows, w in ((bank[1][0:D, :], w1_t[:, :]), (bank[2][0:1, :], b1_col[:, :])):
                    pe.matmul(rows[:, 0:W2ROW], w, w2_ext[:, :], start=True, stop=True)
                    done = pe.matmul(rows[:, W2ROW:W2ROW + D], w, w2_mean[:, :], start=True, stop=True)
                done.then_inc(s_mixp, 1)

        def rowbuf(name, width, n=U):
            return [sb(f"{name}{u}", [P, NC, width]) for u in range(n)]

        n_in, n_c, n_sq, n_out = rowbuf("n_in", D), rowbuf("n_c", D), rowbuf("n_sq", D), rowbuf("n_out", D)
        r_h2, r_x2 = rowbuf("r_h2", W2ROW), rowbuf("r_x2", D)
        r_x3 = r_x2
        n_t = [sb(f"n_t{u}", [128, NC // 2 * P]) for u in range(U)]
        o1_t = sb("o1_t", [128, 2, NC // 2 * P])
        n_mean, n_var, n_sd, n_r = ([sb(f"n_{n}{u}", [P, NC]) for u in range(U)] for n in ("mean", "var", "sd", "r"))
        n_var2, n_sd2, n_r2 = ([sb(f"n_{n}{u}", [P, NC]) for u in range(U)] for n in ("var2", "sd2", "r2"))
        e_dup = [sb(f"e_dup{u}", [P, NC, 2, D]) for u in range(U)]
        NCH = NJ // NC

        def phase(name, names, double=""):
            made = {n: sem(f"s_{name}_{n}") for n in names.split()}
            made.update({n: [sem(f"s_{name}_{n}{u}") for u in range(U)] for n in double.split()})
            return type(name, (), made)

        def flat(t):
            return t.rearrange("p c f -> p (c f)")

        def wide(t, width=D):
            return t.unsqueeze(2).to_broadcast([P, t.shape[1], width])

        def cols3(t):
            return t.rearrange("p (c f) -> p c f", f=D)

        def is_first(i):
            return isinstance(i, int) and i == 0

        def is_second(i):
            return isinstance(i, int) and i == 1

        def h2_slot(c):
            return bank[4 + c // 3][0:P, c % 3 * W2ROW:c % 3 * W2ROW + W2ROW]

        def node_rows(t, i, u, width):
            return t.rearrange("(p j) f -> p (j f)", p=P)[:, bass.ds((2 * i + u) * NC * width, NC * width)]

        def transposed_rows(pe, rows, u):
            for c in range(NC):
                done = pe.transpose(bank[4 + 2 * u + c // 4][0:D + 1, c % 4 * P:c % 4 * P + P], rows[:, c, :], ident[0:P, 0:P])
            return done

        def transposed_act(u):
            return nc.scalar.copy(x_t[u][:, :].rearrange("f (b n) -> f b n", b=2), banks[0:D + 1, 4 + 2 * u:6 + 2 * u, 0:NC // 2 * P])

        def add_bias(pe, to, bias):
            pe.matmul(to[0:P, :], ones3[:, 0:P], bias[:, :], start=True, stop=False)

        sn = phase("node", "centred squares squares2 var var2 dev dev2 x1 turned turned_sb product terms row x2", "loaded x1_out h2_out x2_out")
        product = [banks[0:P, 2 * h:2 * h + 2, 0:2 * NW].rearrange("p b (c w) -> p b c w", w=NW) for h in range(2)]
        NPAIRS = NCH // 2

        def half(t, h):
            return t[:, h * NC // 2:(h + 1) * NC // 2, :].rearrange("p (b c) w -> p b c w", c=2)

        def nodes_sp(sp):
            def load(i, u):
                sp.dma_start(flat(n_in[u][:, :, :]), node_rows(x, i, u, D)).then_inc(sn.loaded[u], 16)

            def store(i):
                for u in range(U):
                    sp.wait_ge(sn.terms, 4 * i + 2 * u + 2)
                    sp.dma_start(node_rows(X1, i, u, W1ROW), flat(r_x1[u][:, :, :])).then_inc(sn.x1_out[u], 16)
                    sp.wait_ge(sn.row, 4 * i + 2 * u + 2)
                    sp.dma_start(node_rows(H2, i, u, W2ROW), flat(r_h2[u][:, :, :])).then_inc(sn.h2_out[u], 16)
                for u in range(U):
                    sp.wait_ge(sn.x2, 2 * i + u + 1)
                    sp.dma_start(node_rows(X2, i, u, D), flat(r_x2[u][:, :, :])).then_inc(sn.x2_out[u], 16)

            for u in range(U):
                load(0, u)
            for u in range(U):
                sp.wait_ge(sn.centred, u + 1)
                load(1, u)
            with nc.sync.Fori(2, NPAIRS) as i:
                for u in range(U):
                    sp.wait_ge(sn.centred, 2 * i - 1 + u)
                    load(i, u)
                store(i - 2)
            for i in (NPAIRS - 2, NPAIRS - 1):
                store(i)
            for u in range(U):
                for s in (sn.x1_out, sn.h2_out, sn.x2_out):
                    sp.wait_ge(s[u], 16 * NPAIRS)

        def nodes_dve(dve):
            def body(i, a, b):
                if a:
                    for u in range(U):
                        dve.wait_ge(sn.loaded[u], 16 * i + 16)
                        v.link(dve.tensor_reduce(n_mean[u][:, :], n_in[u][:, :, :], AX, ALU.add))
                        v.link(dve.tensor_scalar(n_mean[u][:, :], n_mean[u][:, :], -1.0 / D, None, ALU.mult))
                        dve.tensor_tensor(n_c[u][:, :, :], n_in[u][:, :, :], wide(n_mean[u][:, :]), ALU.add).then_inc(sn.centred, 1)
                    for u in range(U):
                        dve.wait_ge(sn.squares, 2 * i + u + 1)
                        dve.tensor_reduce(n_var[u][:, :], n_sq[u][:, :, :], AX, ALU.add).then_inc(sn.var, 1)
                if b:
                    for u in range(U):
                        dve.wait_ge(sn.squares2, 4 * i - 2 + 2 * u)
                        dve.tensor_reduce(n_var2[u][:, :], n_out[u][:, :, :], AX, ALU.add).then_inc(sn.var2, 1)
                if a:
                    for u in range(U):
                        dve.wait_ge(sn.dev, 2 * i + u + 1)
                        v.link(dve.reciprocal(n_r[u][:, :], n_sd[u][:, :]))
                        if b:
                            dve.wait_ge(sn.x1_out[u], 16 * i)
                        dve.tensor_tensor(r_x1[u][:, :, 0:D], n_c[u][:, :, :], wide(n_r[u][:, :]), ALU.mult).then_inc(sn.x1, 1)
                if b:
                    for u in range(U):
                        dve.wait_ge(sn.dev2, 2 * i - 1 + u)
                        v.link(dve.reciprocal(n_r2[u][:, :], n_sd2[u][:, :]))
                        if not is_second(i):
                            dve.wait_ge(sn.x2_out[u], 16 * i - 16)
                        dve.wait_ge(sn.row, 4 * i - 2 + 2 * u)
                        dve.tensor_tensor(r_x2[u][:, :, :], e_dup[u][:, :, 0, :], wide(n_r2[u][:, :]), ALU.mult).then_inc(sn.x2, 1)
            skewed(nc.vector, NPAIRS, body, v)

        def nodes_act(act):
            def body(i, a, b):
                if a:
                    for u in range(U):
                        act.wait_ge(sn.centred, 2 * i + u + 1)
                        nc.scalar.activation(flat(n_sq[u][:, :, :]), flat(n_c[u][:, :, :]), ACT.Square, scale=D ** -0.5).then_inc(sn.squares, 1)
                if b:
                    for u in range(U):
                        for h in range(2):
                            act.wait_ge(sn.product, 4 * i - 3 + 2 * u + h)
                            y = product[h][:, :, :, W2ROW + 4:NW]
                            nc.scalar.copy(half(r_x1[u][:, :, D + 1:W1ROW], h), product[h][:, :, :, W2ROW:W2ROW + 4]).then_inc(sn.terms, 1)
                            nc.scalar.activation(half(n_out[u][:, :, :], h), y, ACT.Square, scale=D ** -0.5).then_inc(sn.squares2, 1)
                            if h == 0 and not is_second(i):
                                act.wait_ge(sn.x2, 2 * i - 3 + u)
                                act.wait_ge(sn.h2_out[u], 16 * i - 16)
                            nc.scalar.copy(half(e_dup[u][:, :, 0, :], h), y)
                            nc.scalar.copy(half(r_h2[u][:, :, :], h), product[h][:, :, :, 0:W2ROW]).then_inc(sn.row, 1)
                if a:
                    for u in range(U):
                        act.wait_ge(sn.var, 2 * i + u + 1)
                        nc.scalar.activation(n_sd[u][:, :], n_var[u][:, :], ACT.Sqrt, bias=eps[0:P, :]).then_inc(sn.dev, 1)
                if b:
                    for u in range(U):
                        act.wait_ge(sn.var2, 2 * i - 1 + u)
                        nc.scalar.activation(n_sd2[u][:, :], n_var2[u][:, :], ACT.Sqrt, bias=eps[0:P, :]).then_inc(sn.dev2, 1)
                if a:
                    for u in range(U):
                        act.wait_ge(sn.turned, 2 * i + u + 1)
                        transposed_act(u).then_inc(sn.turned_sb, 1)
            skewed(nc.scalar, NPAIRS, body)

        def nodes_pe(pe):
            def body(i, a, b):
                if b:
                    for u in range(U):
                        pe.wait_ge(sn.turned_sb, 2 * i - 1 + u)
                        for h in range(2):
                            if u or not is_second(i):
                                pe.wait_ge(sn.row, 4 * i - 5 + 2 * u + h)
                            for c in range(NC // 2):
                                at = (h * NC // 2 + c) * P
                                done = pe.matmul(product[h][:, c // 2, c % 2, :], x_t[u][:, at:at + P], node_w[:, :], start=True, stop=True)
                            done.then_inc(sn.product, 1)
                if a:
                    for u in range(U):
                        pe.wait_ge(sn.x1, 2 * i + u + 1)
                        transposed_rows(pe, r_x1[u][:, :, 0:D + 1], u).then_inc(sn.turned, 1)
            skewed(nc.tensor, NPAIRS, body)

        sx3 = phase("x3", "squares var dev x3", "loaded stored")

        def x3_sp(sp):
            def body(i, a, b):
                for u in range(U):
                    if a:
                        if b:
                            sp.wait_ge(sx3.x3, 2 * i - 1 + u)
                        sp.dma_start(flat(r_x2[u][:, :, :]), node_rows(X2, i, u, D)).then_inc(sx3.loaded[u], 16)
                    if b:
                        if not a:
                            sp.wait_ge(sx3.x3, 2 * i - 1 + u)
                        sp.dma_start(node_rows(X3, i - 1, u, D), flat(n_out[u][:, :, :])).then_inc(sx3.stored[u], 16)
            skewed(nc.sync, NPAIRS, body)

        def x3_stored(eng):
            for u in range(U):
                eng.wait_ge(sx3.stored[u], 16 * NPAIRS)

        def x3_dve(dve):
            def body(i, us):
                for u in us:
                    dve.wait_ge(sx3.squares, turn(i, 1, 0, u, us))
                    dve.tensor_reduce(n_var[u][:, :], n_sq[u][:, :, :], AX, ALU.add).then_inc(sx3.var, 1)
                for u in us:
                    dve.wait_ge(sx3.dev, turn(i, 1, 0, u, us))
                    v.link(dve.reciprocal(n_r[u][:, :], n_sd[u][:, :]))
                    if not is_first(i):
                        dve.wait_ge(sx3.stored[u], 16 * i)
                    dve.tensor_tensor(n_out[u][:, :, :], r_x2[u][:, :, :], wide(n_r[u][:, :]), ALU.mult).then_inc(sx3.x3, 1)
            pairs(nc.vector, NCH, body, v)

        def x3_act(act):
            def body(i, us):
                for u in us:
                    act.wait_ge(sx3.loaded[u], 16 * i + 16)
                    nc.scalar.activation(flat(n_sq[u][:, :, :]), flat(r_x2[u][:, :, :]), ACT.Square, scale=D ** -0.5).then_inc(sx3.squares, 1)
                for u in us:
                    act.wait_ge(sx3.var, turn(i, 1, 0, u, us))
                    nc.scalar.activation(n_sd[u][:, :], n_var[u][:, :], ACT.Sqrt, bias=eps[0:P, :]).then_inc(sx3.dev, 1)
            pairs(nc.scalar, NCH, body)

        so = phase("out", "turned turned_sb y squares var dev row", "loaded stored")

        def out_sp(sp):
            def load(i, u):
                sp.dma_start(flat(n_c[u][:, :, :]), node_rows(X3, i, u, D)).then_inc(so.loaded[u], 16)

            def store(i, u):
                sp.wait_ge(so.row, 2 * i + u + 1)
                sp.dma_start(node_rows(out, i, u, D), flat(n_out[u][:, :, :])).then_inc(so.stored[u], 16)

            for u in range(U):
                load(0, u)
            for u in range(U):
                sp.wait_ge(so.turned, u + 1)
                load(1, u)
            with nc.sync.Fori(2, NPAIRS) as i:
                for u in range(U):
                    sp.wait_ge(so.turned, 2 * i - 1 + u)
                    load(i, u)
                for u in range(U):
                    store(i - 2, u)
            for i in (NPAIRS - 2, NPAIRS - 1):
                for u in range(U):
                    store(i, u)

        def out_stored(eng):
            for u in range(U):
                eng.wait_ge(so.stored[u], 16 * NPAIRS)

        def out_pe(pe):
            def body(i, a, b):
                if b:
                    for u in range(U):
                        pe.wait_ge(so.turned_sb, 2 * i - 1 + u)
                        if not is_second(i):
                            pe.wait_ge(so.row, 2 * i - 3 + u)
                        add_bias(pe, bank[2 + u], wn_bias)
                        for c in range(NC // 2):
                            done = pe.matmul(bank[2 + u][0:P, c * 128:(c + 1) * 128], n_t[u][:, c * P:(c + 1) * P], wn_pair[:, :],
                                             start=False, stop=c == NC // 2 - 1)
                        done.then_inc(so.y, 1)
                if a:
                    for u in range(U):
                        pe.wait_ge(so.loaded[u], 16 * i + 16)
                        for c in range(NC // 2):
                            done = pe.transpose(bank[6 + u][:, c * P:(c + 1) * P], flat(n_c[u][:, 2 * c:2 * c + 2, :]), ident[0:P, 0:P])
                        done.then_inc(so.turned, 1)
            skewed(nc.tensor, NPAIRS, body)

        def out_act(act):
            def body(i, a, b):
                if a:
                    for u in range(U):
                        act.wait_ge(so.turned, 2 * i + u + 1)
                        nc.scalar.copy(n_t[u][:, :], bank[6 + u][:, 0:NC // 2 * P]).then_inc(so.turned_sb, 1)
                if b:
                    for u in range(U):
                        act.wait_ge(so.y, 2 * i - 1 + u)
                        nc.scalar.activation(flat(n_sq[u][:, :, :]), bank[2 + u][0:P, :], ACT.Square, scale=D ** -0.5).then_inc(so.squares, 1)
                    for u in range(U):
                        act.wait_ge(so.var, 2 * i - 1 + u)
                        nc.scalar.activation(n_sd[u][:, :], n_var[u][:, :], ACT.Sqrt, bias=eps[0:P, :]).then_inc(so.dev, 1)
            skewed(nc.scalar, NPAIRS, body)

        def out_dve(dve):
            def body(i, us):
                for u in us:
                    dve.wait_ge(so.squares, turn(i, 1, 0, u, us))
                    dve.tensor_reduce(n_var[u][:, :], n_sq[u][:, :, :], AX, ALU.add).then_inc(so.var, 1)
                for u in us:
                    dve.wait_ge(so.dev, turn(i, 1, 0, u, us))
                    v.link(dve.reciprocal(n_r[u][:, :], n_sd[u][:, :]))
                    if not is_first(i):
                        dve.wait_ge(so.stored[u], 16 * i)
                    dve.tensor_tensor(n_out[u][:, :, :], cols3(bank[2 + u][0:P, :]), wide(n_r[u][:, :]), ALU.mult).then_inc(so.row, 1)
            pairs(nc.vector, NCH, body, v)

        def plane(name, dt=F32):
            return sb(name, [P, J], dt)

        A = sb("edge_rows", [P, J * (W1ROW + D)])

        def rows_of(at, width):
            return A[:, at:at + J * width].rearrange("p (j w) -> p j w", w=width)

        src_i, dst_i, scat_i, src_scat_i = plane("src_i", I32), plane("dst_i", I32), plane("scat_i", I32), plane("src_scat_i", I32)
        key, key_prev, key_next = plane("key"), plane("key_prev"), plane("key_next")
        key_i, prev_i, next_i = plane("key_i", I32), plane("prev_i", I32), plane("next_i", I32)
        cont, last, more = plane("cont"), plane("last"), plane("more")
        reach_f, reach_r = plane("reach_f"), plane("reach_r")
        pen_f, pen_reach = plane("pen_f"), plane("pen_reach")
        norm_d, norm_s = plane("norm_d"), plane("norm_s")
        heads = [plane(f"head{h}") for h in range(2)]
        tops = [plane(f"top{h}") for h in range(2)]
        dens = [plane(f"den{h}") for h in range(2)]
        selfs = [plane(f"self{h}") for h in range(2)]
        own4 = sb("own4", [P, J, 4])
        pass_f_t, pen_f_t, pass_r_t = (sb(n, [128, P]) for n in ("pass_f_t", "pen_f_t", "pass_r_t"))
        cross_in = sb("cross_in", [128, 128])
        crossed = sb("crossed", [128, P + 1])
        carry_in = sb("carry_in", [P, 1])
        carry_rows = [sb(f"carry_rows{h}", [P, D]) for h in range(2)]
        s_tin, s_tout = sems("s_tin s_tout")
        crossings = {"dve": 0, "pe": 0}

        ECH = J // NC

        def chunk(t, i, u):
            return t[:, bass.ds((2 * i + u) * NC, NC)] if len(t.shape) == 2 else t[:, bass.ds((2 * i + u) * NC, NC), :]

        def tall(row):
            return row[:, :].unsqueeze(1).to_broadcast([P, NC, D])

        def dots_dve(dve, products, chunks):
            start = v.n
            with nc.vector.Fori(chunks[0], chunks[1]) as i:
                v.base, v.n = (i - chunks[0]) * 2 + start, 0
                for tmp, a, b, _ in products:
                    other = tall(b) if len(b.shape) == 2 else b[:, bass.ds(i * NC, NC), :]
                    done = dve.tensor_tensor(tmp[:, :, :], a[:, bass.ds(i * NC, NC), :], other, ALU.mult)
                v.link(done)
                for tmp, _, _, to in products:
                    done = dve.tensor_reduce(to[:, bass.ds(i * NC, NC)], tmp[:, :, :], AX, ALU.add)
                v.link(done)
            v.base, v.n = 0, start + 2 * (chunks[1] - chunks[0])

        def edges_of(t):
            return t.rearrange("(p j) -> p j", p=P)

        def transpose_dve(dve, ins):
            ins.then_inc(s_tin, 1)
            crossings["dve"] += 1
            dve.wait_ge(s_tout, crossings["dve"])

        def transpose_pe(pe, frm, rows, cols):
            crossings["pe"] += 1
            pe.wait_ge(s_tin, crossings["pe"])
            pe.transpose(bank[0][0:cols, 0:rows], frm, ident[0:rows, 0:rows]).then_inc(s_tout, 1)

        def segments_dve(dve):
            dve.tensor_tensor(cont[:, :], key[:, :], key_prev[:, :], ALU.is_equal)
            dve.tensor_tensor(last[:, :], key[:, :], key_next[:, :], ALU.not_equal)
            v.link(dve.tensor_tensor(more[:, :], key[:, :], key_next[:, :], ALU.is_equal))
            dve.tensor_scalar(pen_f[:, :], cont[:, :], 1.0, -LOW, ALU.subtract, ALU.mult)
            dve.tensor_tensor_scan(reach_f[:, :], cont[:, :], cont[:, :], 1.0, ALU.mult, ALU.mult)
            v.link(dve.tensor_tensor_scan(reach_r[:, ::-1], more[:, ::-1], more[:, ::-1], 1.0, ALU.mult, ALU.mult))
            dve.tensor_scalar(pen_reach[:, :], reach_f[:, :], 1.0, -LOW, ALU.subtract, ALU.mult)
            transpose_dve(dve, dve.tensor_copy(cross_in[0:P, :], reach_f[:, J - 1:J].to_broadcast([P, 128])))
            v.link(dve.tensor_copy(pass_f_t[:, :], bank[0][:, 0:P]))
            dve.tensor_scalar(pen_f_t[:, :], pass_f_t[:, :], 1.0, -LOW, ALU.subtract, ALU.mult)
            transpose_dve(dve, dve.tensor_copy(cross_in[0:P, :], reach_r[:, 0:1].to_broadcast([P, 128])))
            v.link(dve.tensor_copy(pass_r_t[:, :], bank[0][:, 0:P]))

        def segments_pe(pe):
            for _ in range(2):
                transpose_pe(pe, cross_in[0:P, :], P, 128)

        def carry_dve(dve, ends, n, kind, to):
            transpose_dve(dve, dve.tensor_copy(cross_in[0:P, 0:n], ends))
            if kind == "hold":
                v.link(dve.memset(crossed[0:n, P:P + 1], 0.0))
                transpose_dve(dve, dve.tensor_tensor_scan(crossed[0:n, P - 1::-1], pass_r_t[0:n, ::-1], bank[0][0:n, P - 1::-1], 0.0, ALU.mult, ALU.add))
            else:
                first = LOW if kind == "max" else 0.0
                v.link(dve.memset(crossed[0:n, 0:1], first))
                transpose_dve(dve, dve.tensor_tensor_scan(
                    crossed[0:n, 1:P + 1], (pen_f_t if kind == "max" else pass_f_t)[0:n, :], bank[0][0:n, 0:P], first,
                    ALU.add if kind == "max" else ALU.mult, ALU.max if kind == "max" else ALU.add))
            v.link(dve.tensor_copy(to, bank[0][0:P, 0:n]))

        def carry_pe(pe, n, kind):
            transpose_pe(pe, cross_in[0:P, 0:n], P, n)
            transpose_pe(pe, crossed[0:n, 1:P + 1] if kind == "hold" else crossed[0:n, 0:P], n, P)

        def over_segments(dve, kind, ws):
            if kind == "hold":
                for w in ws:
                    done = dve.tensor_tensor(w, w, last[:, :], ALU.mult)
                v.link(done)
                for w in ws:
                    done = dve.tensor_tensor_scan(w[:, ::-1], more[:, ::-1], w[:, ::-1], 0.0, ALU.mult, ALU.add)
            elif kind == "max":
                for w in ws:
                    done = dve.tensor_tensor_scan(w, pen_f[:, :], w, LOW, ALU.add, ALU.max)
            else:
                for w in ws:
                    done = dve.tensor_tensor_scan(w, cont[:, :], w, 0.0, ALU.mult, ALU.add)
            v.link(done)
            at = 0 if kind == "hold" else J - 1
            for w in ws:
                carry_dve(dve, w[:, at:at + 1], 1, kind, carry_in[:, :])
                if kind == "max":
                    done = dve.scalar_tensor_tensor(w, pen_reach[:, :], carry_in[:, 0:1], w, ALU.add, ALU.max)
                else:
                    reach = reach_r if kind == "hold" else reach_f
                    done = dve.scalar_tensor_tensor(w, reach[:, :], carry_in[:, 0:1], w, ALU.mult, ALU.add)
                v.link(done)

        def over_segments_pe(pe, kind, n):
            for _ in range(n):
                carry_pe(pe, 1, kind)

        def sum_rows_dve(dve, rows, carry):
            for f in range(D):
                done = dve.tensor_tensor_scan(rows[:, :, f], cont[:, :], rows[:, :, f], 0.0, ALU.mult, ALU.add)
            v.link(done)
            carry_dve(dve, rows[:, J - 1, :], D, "sum", carry[:, :])

        def add_carry(dve, to, rows, carry, i, u, tmp):
            v.link(dve.tensor_tensor(tmp, wide(chunk(reach_f, i, u)), tall(carry), ALU.mult))
            v.link(dve.tensor_tensor(to, chunk(rows, i, u), tmp, ALU.add))

        def gather(g, to, table, idx, done, cols=range(J)):
            for j in cols:
                g.indirect_dma_start(out=to[:, j, :] if len(to.shape) == 3 else to[:, j:j + 1], out_offset=None, in_=table,
                                     in_offset=bass.IndirectOffsetOnAxis(ap=idx[:, j:j + 1], axis=0),
                                     bounds_check=NODES - 1, oob_is_err=False).then_inc(done, 16)

        def scatter(g, table, frm, idx, cols, done):
            for j in range(cols):
                g.indirect_dma_start(out=table, out_offset=bass.IndirectOffsetOnAxis(ap=idx[:, j:j + 1], axis=0),
                                     in_=frm[:, j, :] if len(frm.shape) == 3 else frm[:, j:j + 1], in_offset=None,
                                     bounds_check=NODES - 1, oob_is_err=False).then_inc(done, 16)

        ALL = 16 * J


        SF, SLOT_BITS = SORT // 128, SORT.bit_length() - 1
        F_BITS = SF.bit_length() - 1
        k_srt = [n_t[n][:, 0:SF] for n in range(2)]
        d_srt = [o1_t[:, n, 0:SF] for n in range(2)]
        s_srt = sb("s_srt", [128, SF])
        gray_i, bits_i = sb("gray_i", [128, SF], I32), sb("bits_i", [128, SF], I32)
        ki_srt, di_srt = sb("ki_srt", [128, SF], I32), sb("di_srt", [128, SF], I32)
        s_sl, s_sio, s_sfill, s_sst, s_sorted = sems("s_sl s_sio s_sfill s_sst s_sorted")
        s_stin, s_stout = sems("s_stin s_stout")
        FULL = EDGES // SF

        def sort_steps():
            for merge in range(1, SLOT_BITS + 1):
                yield "direct", merge
                if merge > F_BITS:
                    yield "turn", 0
                    for bit in range(merge - 1, F_BITS - 1, -1):
                        yield "exchange", bit - F_BITS
                    yield "turn", 0
                for bit in range(min(merge, F_BITS) - 1, -1, -1):
                    yield "exchange", bit

        STEPS = list(sort_steps())

        def sort_sp(sp):
            sp.wait_ge(s_sfill, 1)
            for to, frm in ((ki_srt, src), (di_srt, dst)):
                sp.dma_start(to[0:FULL, :], frm[0:FULL * SF].rearrange("(p f) -> p f", f=SF)).then_inc(s_sl, 16)
                sp.dma_start(to[FULL:FULL + 1, 0:EDGES - FULL * SF], frm[FULL * SF:EDGES].unsqueeze(0)).then_inc(s_sl, 16)

        def sort_store_sp(sp):
            sp.wait_ge(s_sorted, 1)
            for n, frm in enumerate((ki_srt, di_srt)):
                sp.dma_start(SORTED[n].rearrange("(p f) -> p f", f=SF), frm[:, :]).then_inc(s_sst, 16)
            sp.wait_ge(s_sst, 32)

        def sort_fill_dve(dve):
            dve.memset(di_srt[:, :], 0)
            dve.memset(ki_srt[:, :], FAR).then_inc(s_sfill, 1)

        def sort_dve(dve):
            dve.wait_ge(s_sio, 1)
            v.link(dve.tensor_single_scalar(bits_i[:, :], gray_i[:, :], 1, ALU.logical_shift_right))
            v.link(dve.tensor_tensor(gray_i[:, :], gray_i[:, :], bits_i[:, :], ALU.bitwise_xor))
            dve.wait_ge(s_sl, 64)
            dve.tensor_copy(d_srt[0][:, :], di_srt[:, :])
            v.link(dve.tensor_copy(k_srt[0][:, :], ki_srt[:, :]))
            now, turns = 0, 0
            for n, (what, bit) in enumerate(STEPS):
                hand_over = n + 1 < len(STEPS) and STEPS[n + 1][0] == "turn"
                k0, k1, d0, d1 = (t[:, :] for t in (k_srt[now], k_srt[1 - now], d_srt[now], d_srt[1 - now]))
                if what == "direct":
                    if bit == 1:
                        v.link(dve.tensor_scalar(bits_i[:, :], bits_i[:, :], 1, None, ALU.bitwise_and))
                    else:
                        v.link(dve.tensor_scalar(bits_i[:, :], gray_i[:, :], bit - 1, 1, ALU.logical_shift_right, ALU.bitwise_and))
                    v.link(dve.tensor_scalar(s_srt[:, :], bits_i[:, :], -2.0, 1.0, ALU.mult, ALU.add))
                    done = dve.tensor_tensor(k0, k0, s_srt[:, :], ALU.mult)
                elif what == "turn":
                    turns += 1
                    dve.wait_ge(s_stout, turns)
                    dve.tensor_copy(k1, bank[0][:, 0:SF])
                    done = dve.tensor_copy(d1, bank[0][:, SF:2 * SF])
                    now = 1 - now
                else:
                    k0, k1, d0, d1 = (t.rearrange("p (n two d) -> p n two d", two=2, d=1 << bit) for t in (k0, k1, d0, d1))
                    swap = s_srt[:, 0:SF // 2].rearrange("p (n d) -> p n d", d=1 << bit)
                    diff = s_srt[:, SF // 2:SF].rearrange("p (n d) -> p n d", d=1 << bit)
                    dve.tensor_tensor(swap, k0[:, :, 0], k0[:, :, 1], ALU.is_gt)
                    v.link(dve.tensor_tensor(diff, d0[:, :, 1], d0[:, :, 0], ALU.subtract))
                    v.link(dve.tensor_tensor(diff, diff, swap, ALU.mult))
                    dve.tensor_tensor(k1[:, :, 0], k0[:, :, 0], k0[:, :, 1], ALU.min)
                    dve.tensor_tensor(k1[:, :, 1], k0[:, :, 0], k0[:, :, 1], ALU.max)
                    dve.tensor_tensor(d1[:, :, 0], d0[:, :, 0], diff, ALU.add)
                    done = dve.tensor_tensor(d1[:, :, 1], d0[:, :, 1], diff, ALU.subtract)
                    now = 1 - now
                if hand_over:
                    done.then_inc(s_stin, 1)
                else:
                    v.link(done)
            dve.tensor_copy(ki_srt[:, :], k_srt[now][:, :])
            dve.tensor_copy(di_srt[:, :], d_srt[now][:, :]).then_inc(s_sorted, 1)

        def sort_pe(pe):
            now, turns = 0, 0
            for what, _ in STEPS:
                if what == "turn":
                    turns += 1
                    pe.wait_ge(s_stin, turns)
                    for h in range(SF // 128):
                        part = slice(h * 128, h * 128 + 128)
                        pe.transpose(bank[0][:, part], k_srt[now][:, part], ident[:, :])
                        ins = pe.transpose(bank[0][:, SF + h * 128:SF + h * 128 + 128], d_srt[now][:, part], ident[:, :])
                    ins.then_inc(s_stout, 1)
                if what != "direct":
                    now = 1 - now
        s_idx, s_pre, s_deg, s_sd, s_ninit, s_fill = sems("s_idx s_pre s_deg s_sd s_ninit s_fill")
        xs, xd = rows_of(0, D), rows_of(J * D, D)
        fill = e_dup[0][:, :, :, :].rearrange("p c h f -> p (c h f)")[:, 0:NJ]

        def load_order(sp, keys, done):
            sp.dma_start(key_i[:, :], edges_of(keys)).then_inc(done, 16)
            sp.dma_start(prev_i[1:P, :], keys[J - 1:EDGES - 1].rearrange("(p j) -> p j", j=J)).then_inc(done, 16)
            sp.dma_start(prev_i[0:1, 1:J], keys[0:J - 1].unsqueeze(0)).then_inc(done, 16)
            sp.dma_start(next_i[0:P - 1, :], keys[1:EDGES - J + 1].rearrange("(p j) -> p j", j=J)).then_inc(done, 16)
            sp.dma_start(next_i[P - 1:P, 0:J - 1], keys[EDGES - J + 1:EDGES].unsqueeze(0)).then_inc(done, 16)

        def order_dve(dve):
            dve.tensor_copy(key[:, :], key_i[:, :])
            dve.tensor_copy(key_prev[:, :], prev_i[:, :])
            v.link(dve.tensor_copy(key_next[:, :], next_i[:, :]))
            segments_dve(dve)

        def last_only(dve, to, tmp):
            v.link(dve.tensor_scalar(tmp, more[:, :], float(FAR), None, ALU.mult))
            v.link(dve.tensor_tensor(tmp, key[:, :], tmp, ALU.add))
            v.link(dve.tensor_copy(to, tmp))

        with nc.Block() as block:
            @block.sync
            def _(sp):
                sp.wait_ge(s_pre, 1)
                load_order(sp, dst, s_idx)
                sp.dma_start(src_i[:, :], edges_of(src)).then_inc(s_idx, 16)
                sp.dma_start(dst_i[:, :], edges_of(dst)).then_inc(s_idx, 16)
                sp.wait_ge(s_fill, 1)
                sp.dma_start(NORM.rearrange("(p j) o -> p (j o)", p=P), fill).then_inc(s_ninit, 16)
                sp.wait_ge(s_ninit, 16)

            @block.vector
            def _(dve):
                dve.memset(prev_i[:, :], -1)
                dve.memset(next_i[:, :], -1).then_inc(s_pre, 1)
                dve.memset(fill, 1.0).then_inc(s_fill, 1)
                v.link(dve.memset(norm_d[:, :], 1.0))
                dve.wait_ge(s_idx, 7 * 16)
                order_dve(dve)
                over_segments(dve, "sum", [norm_d[:, :]])
                v.link(dve.tensor_scalar(norm_d[:, :], norm_d[:, :], 1.0, None, ALU.max))
                dve.tensor_copy(norm_s[:, :], norm_d[:, :]).then_inc(s_deg, 1)
                dve.wait_ge(s_sd, 1)
                v.link(dve.reciprocal(norm_d[:, :], norm_s[:, :]))
                over_segments(dve, "hold", [norm_d[:, :]])
                last_only(dve, scat_i[:, :], heads[0][:, :])

            @block.scalar
            def _(act):
                act.wait_ge(s_deg, 1)
                nc.scalar.activation(norm_s[:, :], norm_s[:, :], ACT.Sqrt).then_inc(s_sd, 1)

            @block.tensor
            def _(pe):
                segments_pe(pe)
                over_segments_pe(pe, "sum", 1)
                over_segments_pe(pe, "hold", 1)

        s_gx, s_gn, s_sn = sems("s_gx s_gn s_sn")
        with nc.Block() as block:
            @block.gpsimd
            def _(g):
                scatter(g, NORM, norm_d, scat_i, J, s_sn)
                gather(g, xs, x, src_i, s_gx)
                gather(g, xd, x, dst_i, s_gx)
                g.wait_ge(s_sn, ALL)
                gather(g, norm_s, NORM, src_i, s_gn)
                g.wait_ge(s_gx, 2 * ALL)
                g.wait_ge(s_gn, ALL)

            @block.sync
            def _(sp):
                nodes_sp(sp)

            @block.vector
            def _(dve):
                nodes_dve(dve)
                dve.wait_ge(s_gx, 2 * ALL)
                dots_dve(dve, ((n_sq[0], xd, gw[:, 0, :], heads[0]), (n_sq[1], xs, gw[:, 1, :], heads[1])), (0, ECH))

            @block.scalar
            def _(act):
                nodes_act(act)

            @block.tensor
            def _(pe):
                nodes_pe(pe)

        def edge_rows(t, i, u, width):
            return t.rearrange("(p j) f -> p (j f)", p=P)[:, bass.ds((2 * i + u) * NC * width, NC * width)]

        def centre_dve(dve, s, i, us):
            for u in us:
                v.link(dve.tensor_reduce(n_mean[u][:, :], n_in[u][:, :, :], AX, ALU.add))
                v.link(dve.tensor_scalar(n_mean[u][:, :], n_mean[u][:, :], -1.0 / D, None, ALU.mult))
                dve.tensor_tensor(n_c[u][:, :, :], n_in[u][:, :, :], wide(n_mean[u][:, :]), ALU.add).then_inc(s.centred, 1)

        def deviation_dve(dve, s, i, us, r=0, rounds=1):
            for u in us:
                dve.wait_ge(s.squares, turn(i, rounds, r, u, us))
                dve.tensor_reduce(n_var[u][:, :], n_sq[u][:, :, :], AX, ALU.add).then_inc(s.var, 1)

        def inverse_dve(dve, s, i, us, u, r=0, rounds=1):
            dve.wait_ge(s.dev, turn(i, rounds, r, u, us))
            v.link(dve.reciprocal(n_r[u][:, :], n_sd[u][:, :]))

        def deviation_act(act, s, i, us, r=0, rounds=1, frm=None):
            for u in us:
                if frm is None:
                    act.wait_ge(s.centred, turn(i, 1, 0, u, us))
                nc.scalar.activation(flat(n_sq[u][:, :, :]), flat(n_c[u][:, :, :]) if frm is None else frm(u), ACT.Square,
                                     scale=D ** -0.5).then_inc(s.squares, 1)
            for u in us:
                act.wait_ge(s.var, turn(i, rounds, r, u, us))
                nc.scalar.activation(n_sd[u][:, :], n_var[u][:, :], ACT.Sqrt, bias=eps[0:P, :]).then_inc(s.dev, 1)

        def transpose_pairs(pe, frm, to):
            for c in range(NC // 2):
                done = pe.transpose(to[:, c * P:(c + 1) * P], flat(frm[:, 2 * c:2 * c + 2, :]), ident[0:P, 0:P])
            return done

        def product_pairs(pe, u, w, to, alone=True):
            for c in range(NC // 2):
                done = pe.matmul(to[0:P, c * 128:(c + 1) * 128], n_t[u][:, c * P:(c + 1) * P], w[:, :], start=alone, stop=alone or c == NC // 2 - 1)
            return done

        def scatter_pass(s, parts):
            def program(g):
                def body(i, us):
                    for rows_ready, table, rows, idx, done in parts:
                        for u in us:
                            g.wait_ge(rows_ready, turn(i, 1, 0, u, us))
                            scatter(g, table, rows[u], idx[:, (2 * i + u) * NC:(2 * i + u + 1) * NC], NC, done[u])
                for i in range((ECH + 1) // 2):
                    body(i, range(min(U, ECH - 2 * i)))
                for _, _, _, _, done in parts:
                    for u in range(U):
                        g.wait_ge(done[u], 16 * NC * ((ECH + 1 - u) // 2))
            return program

        sp_ = phase("proj", "turned turned_sb y row", "loaded stored")

        def project_sp(sp):
            def body(i, us):
                for u in us:
                    if not is_first(i):
                        sp.wait_ge(sp_.turned, 2 * i - 1 + u)
                    sp.dma_start(flat(n_in[u][:, :, :]), edge_rows(edge_attr, i, u, D)).then_inc(sp_.loaded[u], 16)
                for u in us:
                    sp.wait_ge(sp_.row, turn(i, 1, 0, u, us))
                    sp.dma_start(edge_rows(EP, i, u, D), flat(n_out[u][:, :, :])).then_inc(sp_.stored[u], 16)
            pairs(nc.sync, ECH, body)

        def projected(eng):
            for u in range(U):
                eng.wait_ge(sp_.stored[u], 16 * ((ECH + 1 - u) // 2))

        def project_pe(pe):
            def body(i, us):
                for u in us:
                    pe.wait_ge(sp_.loaded[u], 16 * i + 16)
                    if not is_first(i):
                        pe.wait_ge(sp_.turned_sb, 2 * i - 1 + u)
                    transpose_pairs(pe, n_in[u], bank[4 + u]).then_inc(sp_.turned, 1)
                for u in us:
                    pe.wait_ge(sp_.turned_sb, turn(i, 1, 0, u, us))
                    if not is_first(i):
                        pe.wait_ge(sp_.row, 2 * i - 1 + u)
                    add_bias(pe, bank[2 + u], wl_bias)
                    product_pairs(pe, u, wl_diag, bank[2 + u], False).then_inc(sp_.y, 1)
            pairs(nc.tensor, ECH, body)

        def project_act(act):
            def body(i, us):
                for u in us:
                    act.wait_ge(sp_.turned, turn(i, 1, 0, u, us))
                    nc.scalar.copy(n_t[u][:, :], bank[4 + u][:, 0:NC // 2 * P]).then_inc(sp_.turned_sb, 1)
                for u in us:
                    act.wait_ge(sp_.y, turn(i, 1, 0, u, us))
                    if not is_first(i):
                        act.wait_ge(sp_.stored[u], 16 * i)
                    nc.scalar.copy(flat(n_out[u][:, :, :]), bank[2 + u][0:P, :]).then_inc(sp_.row, 1)
            pairs(nc.scalar, ECH, body)

        s0 = phase("gate", "tanh_in tanh centred squares var dev x1 turned turned_sb terms row", "stored scattered")
        with nc.Block() as block:
            @block.vector
            def _(dve):
                dve.tensor_tensor(heads[0][:, :], heads[0][:, :], heads[1][:, :], ALU.add).then_inc(s0.tanh_in, 1)
                dve.wait_ge(s0.tanh, 1)
                v.link(dve.scalar_tensor_tensor(heads[0][:, :], heads[0][:, :], 0.5, norm_d[:, :], ALU.mult, ALU.mult))
                v.link(dve.tensor_tensor(heads[0][:, :], heads[0][:, :], norm_s[:, :], ALU.mult))
                v.link(dve.tensor_tensor(xs, xs, wide(heads[0][:, :]), ALU.mult))
                sum_rows_dve(dve, xs, carry_rows[0])

                def body(i, us):
                    for u in us:
                        add_carry(dve, n_in[u][:, :, :], xs, carry_rows[0], i, u, n_out[u][:, :, :])
                        v.link(dve.tensor_tensor(n_in[u][:, :, :], n_in[u][:, :, :], chunk(xd, i, u), ALU.add))
                        if not is_first(i):
                            dve.wait_ge(s0.turned, 2 * i - 1 + u)
                    centre_dve(dve, s0, i, us)
                    deviation_dve(dve, s0, i, us)
                    for u in us:
                        inverse_dve(dve, s0, i, us, u)
                        if not is_first(i):
                            dve.wait_ge(s0.stored[u], 16 * i)
                            dve.wait_ge(s0.scattered[u], 16 * NC * i)
                        v.link(dve.tensor_tensor(n_c[u][:, :, :], n_c[u][:, :, :], wide(n_r[u][:, :]), ALU.mult))
                        dve.tensor_copy(r_x1[u][:, :, 0:D], n_c[u][:, :, :]).then_inc(s0.x1, 1)
                pairs(nc.vector, ECH, body, v)

            @block.scalar
            def _(act):
                act.wait_ge(s0.tanh_in, 1)
                nc.scalar.activation(heads[0][:, :], heads[0][:, :], ACT.Tanh, bias=gb[:, :]).then_inc(s0.tanh, 1)

                def body(i, us):
                    deviation_act(act, s0, i, us)
                    for u in us:
                        act.wait_ge(s0.turned, turn(i, 1, 0, u, us))
                        nc.scalar.copy(n_t[u][:, :], bank[u][:, 0:NC // 2 * P]).then_inc(s0.turned_sb, 1)
                    for u in us:
                        act.wait_ge(s0.terms, turn(i, 1, 0, u, us))
                        terms = bank[2 + u][0:P, 0:4 * NC].rearrange("p (c a) -> p c a", a=4)
                        nc.scalar.copy(chunk(own4[:, :, :], i, u), terms)
                        nc.scalar.copy(r_x1[u][:, :, D + 1:W1ROW], terms).then_inc(s0.row, 1)
                pairs(nc.scalar, ECH, body)

            @block.tensor
            def _(pe):
                carry_pe(pe, D, "sum")

                def body(i, us):
                    for u in us:
                        pe.wait_ge(s0.x1, turn(i, 1, 0, u, us))
                        transpose_pairs(pe, n_c[u], bank[u]).then_inc(s0.turned, 1)
                    for u in us:
                        pe.wait_ge(s0.turned_sb, turn(i, 1, 0, u, us))
                        if not is_first(i):
                            pe.wait_ge(s0.row, 2 * i - 1 + u)
                        for c in range(NC // 2):
                            done = pe.matmul(bank[2 + u][0:P, 8 * c:8 * c + 8], n_t[u][:, c * P:c * P + P], wa_pair[:, :], start=True, stop=True)
                        done.then_inc(s0.terms, 1)
                pairs(nc.tensor, ECH, body)

            def store_pass(sp, s, table, rows, width):
                def body(i, us):
                    for u in us:
                        sp.wait_ge(s.row, turn(i, 1, 0, u, us))
                        sp.dma_start(edge_rows(table, i, u, width), flat(rows[u][:, :, :])).then_inc(s.stored[u], 16)
                pairs(nc.sync, ECH, body)
                for u in range(U):
                    sp.wait_ge(s.stored[u], 16 * ((ECH + 1 - u) // 2))

            @block.sync
            def _(sp):
                store_pass(sp, s0, E1, r_x1, W1ROW)

            @block.gpsimd
            def _(g):
                scatter_pass(s0, [(s0.row, X1, r_x1, scat_i, s0.scattered)])(g)

        def attention_dve(dve, s, rows, at):
            for h in range(H):
                dve.tensor_copy(dens[h][:, :], own4[:, :, 2 + h])
                v.link(dve.tensor_tensor(selfs[h][:, :], own4[:, :, h], own4[:, :, 2 + h], ALU.add))
            for h in range(H):
                v.link(dve.scalar_tensor_tensor(selfs[h][:, :], selfs[h][:, :], 0.2, selfs[h][:, :], ALU.mult, ALU.max))
            over_segments(dve, "hold", [d[:, :] for d in dens])
            for h in range(H):
                v.link(dve.tensor_tensor(heads[h][:, :], rows[:, :, at + h], dens[h][:, :], ALU.add))
                v.link(dve.scalar_tensor_tensor(heads[h][:, :], heads[h][:, :], 0.2, heads[h][:, :], ALU.mult, ALU.max))
                v.link(dve.tensor_copy(tops[h][:, :], heads[h][:, :]))
            over_segments(dve, "max", [t[:, :] for t in tops])
            for h in range(H):
                v.link(dve.tensor_tensor(tops[h][:, :], tops[h][:, :], selfs[h][:, :], ALU.max))
            over_segments(dve, "hold", [t[:, :] for t in tops])
            for h in range(H):
                dve.tensor_tensor(heads[h][:, :], heads[h][:, :], tops[h][:, :], ALU.subtract)
                v.link(dve.tensor_tensor(selfs[h][:, :], selfs[h][:, :], tops[h][:, :], ALU.subtract))
                done = dve.tensor_scalar(selfs[h][:, :], selfs[h][:, :], 0.0, None, ALU.min)
            done.then_inc(s.logits, 1)
            dve.wait_ge(s.exps, 1)
            for h in range(H):
                v.link(dve.tensor_copy(dens[h][:, :], heads[h][:, :]))
            over_segments(dve, "sum", [d[:, :] for d in dens])
            for h in range(H):
                v.link(dve.tensor_tensor(dens[h][:, :], dens[h][:, :], selfs[h][:, :], ALU.add))
                v.link(dve.tensor_scalar(dens[h][:, :], dens[h][:, :], 0.5, None, ALU.max))
                v.link(dve.reciprocal(dens[h][:, :], dens[h][:, :]))

        def attention_act(act, s):
            act.wait_ge(s.logits, 1)
            for t in (*heads, *selfs):
                done = nc.scalar.activation(t[:, :], t[:, :], ACT.Exp)
            done.then_inc(s.exps, 1)

        def attention_pe(pe):
            over_segments_pe(pe, "hold", 2)
            over_segments_pe(pe, "max", 2)
            over_segments_pe(pe, "hold", 2)
            over_segments_pe(pe, "sum", 2)

        s1 = phase("att1", "gathered logits exps x turned turned_sb o1 o1_sb h2 row", "loaded stored scattered")
        xa, vb = rows_of(0, W1ROW), rows_of(J * W1ROW, D)
        with nc.Block() as block:
            @block.gpsimd
            def _(g):
                g.iota(gray_i[:, :], pattern=[[1, SF]], base=0, channel_multiplier=SF).then_inc(s_sio, 1)
                gather(g, xa, X1, src_i, s1.gathered)
                scatter_pass(s1, [(s1.row, H2, r_h2, scat_i, s1.scattered)])(g)

            @block.vector
            def _(dve):
                sort_fill_dve(dve)
                sort_dve(dve)
                dve.wait_ge(s1.gathered, ALL)
                attention_dve(dve, s1, xa, D + 1)
                dve.tensor_tensor(vb, xa[:, :, 0:D], wide(heads[1][:, :]), ALU.mult)
                v.link(dve.tensor_tensor(xa[:, :, 0:D], xa[:, :, 0:D], wide(heads[0][:, :]), ALU.mult))
                sums = (xa[:, :, 0:D], vb)
                for h in range(H):
                    sum_rows_dve(dve, sums[h], carry_rows[h])

                def body(i, us):
                    for u in us:
                        dve.wait_ge(s1.loaded[u], 16 * i + 16)
                        if not is_first(i):
                            dve.wait_ge(s1.turned, 2 * i - 1 + u)
                        for h in range(H):
                            tmp = (n_sq, n_in)[h][u][:, :, :]
                            v.link(dve.tensor_tensor(tmp, r_x1[u][:, :, 0:D], wide(chunk(selfs[h], i, u)), ALU.mult))
                            add_carry(dve, n_out[u][:, :, :], sums[h], carry_rows[h], i, u, n_c[u][:, :, :])
                            v.link(dve.tensor_tensor(tmp, tmp, n_out[u][:, :, :], ALU.add))
                            done = dve.tensor_tensor(e_dup[u][:, :, h, :], tmp, wide(chunk(dens[h], i, u)), ALU.mult)
                        done.then_inc(s1.x, 1)
                pairs(nc.vector, ECH, body, v)

            @block.tensor
            def _(pe):
                sort_pe(pe)
                attention_pe(pe)
                for _ in range(H):
                    carry_pe(pe, D, "sum")

                def body(i, us):
                    for u in us:
                        pe.wait_ge(s1.x, turn(i, 1, 0, u, us))
                        for c in range(NC):
                            done = pe.transpose(bank[c // 4][:, c % 4 * P:(c % 4 + 1) * P], e_dup[u][:, c, :, :].rearrange("p h f -> p (h f)"), ident[0:P, 0:P])
                        done.then_inc(s1.turned, 1)
                        pe.wait_ge(s1.turned_sb, turn(i, 1, 0, u, us))
                        for half in range(2):
                            done = pe.matmul(bank[2 + half][:, 0:NC // 2 * P], w1_heads[:, :], n_t[half][:, :], start=True, stop=True)
                        done.then_inc(s1.o1, 1)
                        pe.wait_ge(s1.o1_sb, turn(i, 1, 0, u, us))
                        if u or not is_first(i):
                            pe.wait_ge(s1.row, 2 * i + u)
                        for c in range(NC):
                            done = pe.matmul(h2_slot(c), o1_t[:, c // 4, c % 4 * P:c % 4 * P + P], w2_ext[:, :], start=True, stop=True)
                        done.then_inc(s1.h2, 1)
                pairs(nc.tensor, ECH, body)

            @block.scalar
            def _(act):
                attention_act(act, s1)

                def body(i, us):
                    for u in us:
                        act.wait_ge(s1.turned, turn(i, 1, 0, u, us))
                        nc.scalar.copy(n_t[0][:, :], bank[0][:, 0:NC // 2 * P])
                        nc.scalar.copy(n_t[1][:, :], bank[1][:, 0:NC // 2 * P]).then_inc(s1.turned_sb, 1)
                        act.wait_ge(s1.o1, turn(i, 1, 0, u, us))
                        for half in range(2):
                            done = nc.scalar.activation(o1_t[:, half, :], bank[2 + half][:, 0:NC // 2 * P], ACT.Identity, bias=b1_col[:, :])
                        done.then_inc(s1.o1_sb, 1)
                        act.wait_ge(s1.h2, turn(i, 1, 0, u, us))
                        if not is_first(i):
                            act.wait_ge(s1.stored[u], 16 * i)
                            act.wait_ge(s1.scattered[u], 16 * NC * i)
                        for b, cols in enumerate((3, 3, 2)):
                            at = bank[4 + b][0:P, 0:cols * W2ROW]
                            nc.scalar.copy(own4[:, bass.ds((2 * i + u) * NC + 3 * b, cols), :], at.rearrange("p (c w) -> p c w", w=W2ROW)[:, :, 2 * D:W2ROW])
                            done = nc.scalar.copy(flat(r_h2[u][:, 3 * b:3 * b + cols, :]), at)
                        done.then_inc(s1.row, 1)
                pairs(nc.scalar, ECH, body)

            @block.sync
            def _(sp):
                sort_sp(sp)
                sort_store_sp(sp)

                def load(i, u):
                    sp.dma_start(flat(r_x1[u][:, :, :]), edge_rows(E1, i, u, W1ROW)).then_inc(s1.loaded[u], 16)

                def body(i, us):
                    for u in us:
                        if not is_first(i):
                            sp.wait_ge(s1.x, 2 * i - 1 + u)
                        load(i, u)
                    for u in us:
                        sp.wait_ge(s1.row, turn(i, 1, 0, u, us))
                        sp.dma_start(edge_rows(E2, i, u, W2ROW), flat(r_h2[u][:, :, :])).then_inc(s1.stored[u], 16)
                pairs(nc.sync, ECH, body)
                for u in range(U):
                    sp.wait_ge(s1.stored[u], 16 * ((ECH + 1 - u) // 2))

        s2 = phase("att2", "gathered logits exps centred squares var dev row", "loaded scattered")
        ha = rows_of(0, W2ROW)
        with nc.Block() as block:
            @block.gpsimd
            def _(g):
                gather(g, ha, H2, src_i, s2.gathered)
                scatter_pass(s2, [(s2.row, X2, r_x2, scat_i, s2.scattered)])(g)

            @block.vector
            def _(dve):
                dve.wait_ge(s2.gathered, ALL)
                projected(dve)
                attention_dve(dve, s2, ha, 2 * D)
                for h in range(H):
                    v.link(dve.scalar_tensor_tensor(selfs[h][:, :], selfs[h][:, :], 1.0 / H, dens[h][:, :], ALU.mult, ALU.mult))
                over_segments(dve, "hold", [d[:, :] for d in dens])
                for h in range(H):
                    v.link(dve.scalar_tensor_tensor(heads[h][:, :], heads[h][:, :], 1.0 / H, dens[h][:, :], ALU.mult, ALU.mult))
                for h in range(H):
                    part = ha[:, :, h * D:h * D + D]
                    v.link(dve.tensor_tensor(part, part, wide(heads[h][:, :]), ALU.mult))
                v.link(dve.tensor_tensor(ha[:, :, 0:D], ha[:, :, 0:D], ha[:, :, D:2 * D], ALU.add))
                sum_rows_dve(dve, ha[:, :, 0:D], carry_rows[0])

                def body(i, us):
                    for u in us:
                        dve.wait_ge(s2.loaded[u], 32 * i + 32)
                        y = n_in[u][:, :, :]
                        v.link(dve.tensor_tensor(y, r_h2[u][:, :, 0:D], wide(chunk(selfs[0], i, u)), ALU.mult))
                        v.link(dve.tensor_tensor(n_c[u][:, :, :], r_h2[u][:, :, D:2 * D], wide(chunk(selfs[1], i, u)), ALU.mult))
                        v.link(dve.tensor_tensor(y, y, n_c[u][:, :, :], ALU.add))
                        add_carry(dve, n_out[u][:, :, :], ha[:, :, 0:D], carry_rows[0], i, u, n_sq[u][:, :, :])
                        v.link(dve.tensor_tensor(y, y, n_out[u][:, :, :], ALU.add))
                        v.link(dve.tensor_tensor(y, y, r_x1[u][:, :, 0:D], ALU.add))
                        v.link(dve.tensor_tensor(y, y, tall(b2_all), ALU.add))
                    centre_dve(dve, s2, i, us)
                    deviation_dve(dve, s2, i, us)
                    for u in us:
                        inverse_dve(dve, s2, i, us, u)
                        if not is_first(i):
                            dve.wait_ge(s2.scattered[u], 16 * NC * i)
                        dve.tensor_tensor(r_x2[u][:, :, :], n_c[u][:, :, :], wide(n_r[u][:, :]), ALU.mult).then_inc(s2.row, 1)
                pairs(nc.vector, ECH, body, v)

            @block.tensor
            def _(pe):
                project_pe(pe)
                attention_pe(pe)
                over_segments_pe(pe, "hold", 2)
                carry_pe(pe, D, "sum")

            @block.scalar
            def _(act):
                project_act(act)
                attention_act(act, s2)
                pairs(nc.scalar, ECH, lambda i, us: deviation_act(act, s2, i, us))

            @block.sync
            def _(sp):
                project_sp(sp)

                def body(i, us):
                    for u in us:
                        if not is_first(i):
                            sp.wait_ge(s2.centred, 2 * i - 1 + u)
                        sp.dma_start(flat(r_x1[u][:, :, :]), edge_rows(E1, i, u, W1ROW)).then_inc(s2.loaded[u], 16)
                        sp.dma_start(flat(r_h2[u][:, :, :]), edge_rows(E2, i, u, W2ROW)).then_inc(s2.loaded[u], 16)
                pairs(nc.sync, ECH, body)

        s3 = phase("cos", "ordered outside norms roots logits exps centred squares var dev x3", "scattered")
        s3_got = [sem(f"s_cos_got{n}") for n in range(GROUPS)]
        xr, xc = rows_of(0, D), rows_of(J * D, D)
        col_i = norm_s[:, :].bitcast(I32)
        with nc.Block() as block:
            @block.sync
            def _(sp):
                sp.wait_ge(s3.outside, 1)
                load_order(sp, SORTED[0, 0:EDGES], s3.ordered)
                sp.dma_start(col_i, edges_of(SORTED[1, 0:EDGES])).then_inc(s3.ordered, 16)
                x3_sp(sp)

            @block.gpsimd
            def _(g):
                g.wait_ge(s3.ordered, 6 * 16)
                for n in range(GROUPS):
                    cols = range(n * J // GROUPS, (n + 1) * J // GROUPS)
                    gather(g, xr, X2, key_i, s3_got[n], cols)
                    gather(g, xc, X2, col_i, s3_got[n], cols)
                x3_stored(g)
                scatter_pass(s3, [(s3.x3, X3, r_x3, src_scat_i, s3.scattered)])(g)

            @block.vector
            def _(dve):
                dve.memset(prev_i[:, :], -1)
                dve.memset(next_i[:, :], -1).then_inc(s3.outside, 1)
                dve.wait_ge(s3.ordered, 6 * 16)
                order_dve(dve)
                last_only(dve, src_scat_i[:, :], heads[0][:, :])
                x3_dve(dve)
                for n in range(GROUPS):
                    dve.wait_ge(s3_got[n], 2 * ALL // GROUPS)
                    dots_dve(dve, ((n_sq[0], xr, xr, tops[0]), (n_sq[1], xc, xc, tops[1]), (n_in[0], xr, xc, heads[0])),
                             (n * ECH // GROUPS, (n + 1) * ECH // GROUPS))
                dve.tensor_copy(dens[0][:, :], tops[0][:, :]).then_inc(s3.norms, 1)
                dve.wait_ge(s3.roots, 1)
                for t in tops:
                    v.link(dve.reciprocal(t[:, :], t[:, :]))
                    v.link(dve.tensor_tensor(heads[0][:, :], heads[0][:, :], t[:, :], ALU.mult))
                v.link(dve.tensor_scalar(heads[0][:, :], heads[0][:, :], beta_all[:, :], None, ALU.mult))
                v.link(dve.tensor_copy(tops[0][:, :], heads[0][:, :]))
                over_segments(dve, "max", [tops[0][:, :]])
                over_segments(dve, "hold", [tops[0][:, :]])
                dve.tensor_tensor(heads[0][:, :], heads[0][:, :], tops[0][:, :], ALU.subtract).then_inc(s3.logits, 1)
                dve.wait_ge(s3.exps, 1)
                v.link(dve.tensor_copy(dens[0][:, :], heads[0][:, :]))
                over_segments(dve, "sum", [dens[0][:, :]])
                v.link(dve.tensor_scalar(dens[0][:, :], dens[0][:, :], 1e-16, None, ALU.max))
                v.link(dve.reciprocal(dens[0][:, :], dens[0][:, :]))
                v.link(dve.tensor_tensor(xc, xc, wide(heads[0][:, :]), ALU.mult))
                sum_rows_dve(dve, xc, carry_rows[0])
                x3_stored(dve)

                def body(i, us):
                    for u in us:
                        add_carry(dve, n_in[u][:, :, :], xc, carry_rows[0], i, u, n_out[u][:, :, :])
                        v.link(dve.tensor_tensor(n_in[u][:, :, :], n_in[u][:, :, :], wide(chunk(dens[0], i, u)), ALU.mult))
                        v.link(dve.tensor_tensor(n_in[u][:, :, :], n_in[u][:, :, :], chunk(xr, i, u), ALU.add))
                    centre_dve(dve, s3, i, us)
                    deviation_dve(dve, s3, i, us)
                    for u in us:
                        inverse_dve(dve, s3, i, us, u)
                        if not is_first(i):
                            dve.wait_ge(s3.scattered[u], 16 * NC * i)
                        dve.tensor_tensor(r_x3[u][:, :, :], n_c[u][:, :, :], wide(n_r[u][:, :]), ALU.mult).then_inc(s3.x3, 1)
                pairs(nc.vector, ECH, body, v)

            @block.tensor
            def _(pe):
                segments_pe(pe)
                over_segments_pe(pe, "max", 1)
                over_segments_pe(pe, "hold", 1)
                over_segments_pe(pe, "sum", 1)
                carry_pe(pe, D, "sum")

            @block.scalar
            def _(act):
                x3_act(act)
                act.wait_ge(s3.norms, 1)
                for t in tops:
                    done = nc.scalar.activation(t[:, :], t[:, :], ACT.Sqrt, bias=eps8[0:P, :])
                done.then_inc(s3.roots, 1)
                act.wait_ge(s3.logits, 1)
                nc.scalar.activation(heads[0][:, :], heads[0][:, :], ACT.Exp).then_inc(s3.exps, 1)

                pairs(nc.scalar, ECH, lambda i, us: deviation_act(act, s3, i, us))

        s4 = phase("msg", "ordered outside gathered gathered_dst msg sum_turned sum_turned_sb y x centred squares var dev row", "loaded scattered")
        with nc.Block() as block:
            @block.sync
            def _(sp):
                sp.wait_ge(s4.outside, 1)
                load_order(sp, dst, s4.ordered)
                out_sp(sp)

                def body(i, us):
                    for u in us:
                        if not is_first(i):
                            sp.wait_ge(s4.msg, 2 * i - 1 + u)
                        sp.dma_start(flat(n_in[u][:, :, :]), edge_rows(EP, i, u, D)).then_inc(s4.loaded[u], 16)
                pairs(nc.sync, ECH, body)

            @block.gpsimd
            def _(g):
                gather(g, xs, X3, src_i, s4.gathered)
                gather(g, xd, X3, dst_i, s4.gathered_dst)
                out_stored(g)
                scatter_pass(s4, [(s4.row, out, n_out, scat_i, s4.scattered)])(g)

            @block.vector
            def _(dve):
                dve.memset(prev_i[:, :], -1)
                dve.memset(next_i[:, :], -1).then_inc(s4.outside, 1)
                dve.wait_ge(s4.ordered, 5 * 16)
                order_dve(dve)
                out_dve(dve)
                dve.wait_ge(s4.gathered, ALL)

                def message(i, us):
                    for u in us:
                        dve.wait_ge(s4.loaded[u], 16 * i + 16)
                        v.link(dve.tensor_tensor(n_sq[u][:, :, :], n_in[u][:, :, :], chunk(xs, i, u), ALU.add))
                        dve.tensor_scalar(chunk(xs, i, u), n_sq[u][:, :, :], 0.0, None, ALU.max).then_inc(s4.msg, 1)
                pairs(nc.vector, ECH, message, v)
                dve.wait_ge(s4.msg, ECH)
                sum_rows_dve(dve, xs, carry_rows[0])
                dve.wait_ge(s4.gathered_dst, ALL)
                out_stored(dve)

                def body(i, us):
                    for u in us:
                        add_carry(dve, n_c[u][:, :, :], xs, carry_rows[0], i, u, n_sq[u][:, :, :])
                        dve.tensor_tensor(n_in[u][:, :, :], n_c[u][:, :, :], chunk(xd, i, u), ALU.add).then_inc(s4.x, 1)
                    for u in us:
                        dve.wait_ge(s4.y, turn(i, 1, 0, u, us))
                        v.link(dve.tensor_tensor(n_in[u][:, :, :], cols3(bank[2 + u][0:P, :]), chunk(xd, i, u), ALU.add))
                        v.link(dve.tensor_tensor(n_in[u][:, :, :], n_in[u][:, :, :], tall(bn_all), ALU.add))
                    centre_dve(dve, s4, i, us)
                    deviation_dve(dve, s4, i, us)
                    for u in us:
                        inverse_dve(dve, s4, i, us, u)
                        if not is_first(i):
                            dve.wait_ge(s4.scattered[u], 16 * NC * i)
                        dve.tensor_tensor(n_out[u][:, :, :], n_c[u][:, :, :], wide(n_r[u][:, :]), ALU.mult).then_inc(s4.row, 1)
                pairs(nc.vector, ECH, body, v)

            @block.tensor
            def _(pe):
                segments_pe(pe)
                out_pe(pe)
                pe.wait_ge(so.row, NCH)
                carry_pe(pe, D, "sum")

                def body(i, us):
                    for u in us:
                        pe.wait_ge(s4.x, turn(i, 1, 0, u, us))
                        transpose_pairs(pe, n_in[u], bank[4 + u]).then_inc(s4.sum_turned, 1)
                    for u in us:
                        pe.wait_ge(s4.sum_turned_sb, turn(i, 1, 0, u, us))
                        product_pairs(pe, u, wn_diag, bank[2 + u]).then_inc(s4.y, 1)
                pairs(nc.tensor, ECH, body)

            @block.scalar
            def _(act):
                out_act(act)

                def body(i, us):
                    for u in us:
                        act.wait_ge(s4.sum_turned, turn(i, 1, 0, u, us))
                        nc.scalar.copy(n_t[u][:, :], bank[4 + u][:, 0:NC // 2 * P]).then_inc(s4.sum_turned_sb, 1)
                    deviation_act(act, s4, i, us)
                pairs(nc.scalar, ECH, body)

_INS = ['x', 'src', 'dst', 'edge_attr_64', 'L0_gnn_gate_w', 'L0_gnn_gate_b', 'L1_gnn_W1', 'L1_gnn_as1', 'L1_gnn_ad1', 'L1_gnn_b1', 'L1_gnn_W2', 'L1_gnn_as2', 'L1_gnn_ad2', 'L1_gnn_b2', 'L2_gnn_beta', 'L3_gnn_Wl', 'L3_gnn_bl', 'L3_gnn_Wn', 'L3_gnn_bn']


def kernel(**inputs):
    import numpy as np
    import concourse.bacc as bacc
    from concourse import mybir
    from concourse.bass_utils import run_bass_kernel_spmd

    nc = bacc.Bacc("TRN2", target_bir_lowering=False, num_devices=1)
    arrays, args = {}, []
    for name in _INS:
        a = np.ascontiguousarray(inputs[name])
        arrays[f"in_{name}_dram"] = a
        args.append(nc.dram_tensor(f"in_{name}_dram", a.shape, mybir.dt.from_np(a.dtype), kind="ExternalInput").ap())
    out = nc.dram_tensor("out_dram", (100000, 64), mybir.dt.float32, kind="ExternalOutput").ap()
    build(nc, *args, out)
    r = run_bass_kernel_spmd(nc, [arrays], core_ids=[0])
    return r.results[0]["out_dram"]
```

```python
from contextlib import ExitStack

import concourse.bass as bass
from concourse import mybir

F32 = mybir.dt.float32
I32 = mybir.dt.int32
BF16 = mybir.dt.bfloat16
ALU = mybir.AluOpType
ACT = mybir.ActivationFunctionType
AX = mybir.AxisListType.X

NODES, EDGES, D, H = 100000, 25000, 64, 2
P = 125
NJ = NODES // P
J = EDGES // P
NC = 8
U = 2
EPS = 1e-5
LINKS_OF_ALSO = 2
START = (20, 40)
GROUPS = (0, 10, 18, 22, 24, 25)
W1ROW, W2ROW = D + 5, 2 * D + 4
NW = W2ROW + 4 + D
SORT = 32768
FAR = 1 << 20
LOW = -1e38


class Chain:

    def __init__(self, eng, sem):
        self.eng, self.sem, self.base, self.n = eng, sem, 0, 0

    def link(self, ins):
        self.n += 1
        ins.then_inc(self.sem, 1)
        self.eng.wait_ge(self.sem, self.base + self.n)


def pairs(eng, chunks, body, chain=None):
    before = chain.n if chain else 0
    body(0, range(2))
    per = chain.n - before if chain else 0
    with eng.Fori(1, chunks // 2) as i:
        if chain:
            total = chain.n
            chain.base, chain.n = (i - 1) * per + total, 0
        body(i, range(2))
        if chain:
            assert chain.n == per
    if chain:
        chain.base, chain.n = 0, total + (chunks // 2 - 1) * per
    if chunks % 2:
        body(chunks // 2, range(1))


def turn(i, rounds, r, u, us):
    return i * 2 * rounds + r * len(us) + u + 1


def skewed(eng, pairs_n, body):
    body(0, True, False)
    body(1, True, True)
    with eng.Fori(2, pairs_n) as i:
        body(i, True, True)
    body(pairs_n, False, True)


def skewed3(eng, pairs_n, body, chain=None, late=0, also=None):
    body(0, True, False, False)
    body(1, True, True, False)
    before = chain.n if chain else 0
    body(2, True, True, True)
    per = chain.n - before if chain else 0
    for start, end, links in ((3, pairs_n - late, per), (pairs_n - late, pairs_n, per + LINKS_OF_ALSO)):
        if start == end:
            continue
        with eng.Fori(start, end) as i:
            if chain:
                total = chain.n
                chain.base, chain.n = (i - start) * links + total, 0
            body(i, True, True, True)
            if start > 3:
                also(i - start)
            if chain:
                assert chain.n == links
        if chain:
            chain.base, chain.n = 0, total + (end - start) * links
    body(pairs_n, False, True, True)
    body(pairs_n + 1, False, False, True)


def build(nc, x, src, dst, edge_attr, gate_w, gate_b, W1, as1, ad1, b1, W2, as2, ad2, b2, beta, Wl, bl, Wn, bn, out):
    ctx = ExitStack()
    with ctx:
        def sb(name, shape, dt=F32):
            return ctx.enter_context(nc.sbuf_tensor(name, shape, dt))

        def sem(name):
            return ctx.enter_context(nc.semaphore(name))

        def sems(names):
            return [sem(n) for n in names.split()]

        ident = sb("ident", [128, 128])
        eps = sb("eps", [128, 1])
        eps8 = sb("eps8", [128, 1])
        w1_dup = sb("w1_dup", [128, 128])
        w1_t = sb("w1_t", [128, D])
        w1_t_diag = sb("w1_t_diag", [128, 128])
        w2_ext = sb("w2_ext", [128, 132])
        w2_mean = sb("w2_mean", [128, D])
        heads_w = sb("heads_w", [128, W2ROW])
        wa = sb("wa", [128, 4])
        node_w = sb("node_w", [D + 1, NW])
        out_w = sb("out_w", [D, D])
        wn_pair = sb("wn_pair", [128, 128])
        wn_bias = sb("wn_bias", [3, NC * D], BF16)
        wl_bias = sb("wl_bias", [3, NC * D], BF16)
        h2_bias = sb("h2_bias", [3, 3 * W2ROW], BF16)
        ones3 = sb("ones3", [3, 128], BF16)
        bias_parts = [sb(f"bias_parts{n}", [1, 3, w], BF16) for n, w in enumerate((D, D, W2ROW))]
        piece = sb("bias_part", [1, W2ROW], BF16)
        rest = sb("bias_rest", [1, W2ROW])
        wa_pair = sb("wa_pair", [128, 8])
        att1 = sb("att1", [128, 4, D])
        att2 = sb("att2", [128, 4, D])
        att_tmp = sb("att_tmp", [128, 4, D])
        wn_diag = sb("wn_diag", [128, 128])
        wl_diag = sb("wl_diag", [128, 128])
        bias_row = sb("bias_row", [1, NW])
        r_x1 = [sb(f"r_x1{u}", [P, NC, W1ROW]) for u in range(U)]
        x_t = [sb(f"x_t{u}", [D + 1, NC * P]) for u in range(U)]
        row_mean = sb("row_mean", [128, 1])
        b1_col = sb("b1_col", [128, 1])
        b2_row = sb("b2_row", [1, D])
        b2_all = sb("b2_all", [P, D])
        bn_row = sb("bn_row", [1, D])
        bn_all = sb("bn_all", [P, D])
        bl_row = sb("bl_row", [1, D])
        gw = sb("gw", [P, 2, D])
        gb = sb("gb", [P, 1])
        beta_all = sb("beta_all", [P, 1])

        banks = ctx.enter_context(nc.psum_tensor("banks", [128, 8, 512], F32))
        bank = [banks[:, i, :] for i in range(8)]

        s_v, s_g = sems("s_v s_g")
        v = Chain(nc.vector, s_v)
        pool = Chain(nc.gpsimd, s_g)

        X1 = nc.dram_tensor("x1_rows", [NODES, W1ROW], F32).ap()
        H2 = nc.dram_tensor("h2_rows", [NODES, W2ROW], F32).ap()
        X2 = nc.dram_tensor("x2_rows", [NODES, D], F32).ap()
        X3 = nc.dram_tensor("x3_rows", [NODES, D], F32).ap()
        NORM = nc.dram_tensor("norm_rows", [NODES, 1], F32).ap()
        E1 = nc.dram_tensor("x1_edge_rows", [EDGES, W1ROW], F32).ap()
        E2 = nc.dram_tensor("h2_edge_rows", [EDGES, W2ROW], F32).ap()
        EP = nc.dram_tensor("edge_projections", [EDGES, D], F32).ap()
        SORTED = nc.dram_tensor("sorted_pairs", [2, SORT], I32).ap()

        def plane(name, dt=F32):
            return sb(name, [P, J], dt)

        A = sb("edge_rows", [P, J * (W1ROW + D)])

        def rows_of(at, width):
            return A[:, at:at + J * width].rearrange("p (j w) -> p j w", w=width)

        src_i, dst_i, scat_i, src_scat_i = plane("src_i", I32), plane("dst_i", I32), plane("scat_i", I32), plane("src_scat_i", I32)
        xs, xd = rows_of(0, D), rows_of(J * D, D)
        own4 = sb("own4", [P, J, 4])
        x1_in = [t[:, 0:NC * (D + 1)].rearrange("p (c f) -> p c f", f=D + 1)
                 for t in (own4[:, :, :].rearrange("p j a -> p (j a)"), A[:, 2 * J * D:])]

        def edges_of(t):
            return t.rearrange("(p j) -> p j", p=P)

        def gather(g, to, table, idx, done, cols=range(J)):
            for j in cols:
                g.indirect_dma_start(out=to[:, j, :] if len(to.shape) == 3 else to[:, j:j + 1], out_offset=None, in_=table,
                                     in_offset=bass.IndirectOffsetOnAxis(ap=idx[:, j:j + 1], axis=0),
                                     bounds_check=NODES - 1, oob_is_err=False).then_inc(done, 16)

        def scatter(g, table, frm, idx, cols, done):
            for j in range(cols):
                g.indirect_dma_start(out=table, out_offset=bass.IndirectOffsetOnAxis(ap=idx[:, j:j + 1], axis=0),
                                     in_=frm[:, j, :] if len(frm.shape) == 3 else frm[:, j:j + 1], in_offset=None,
                                     bounds_check=NODES - 1, oob_is_err=False).then_inc(done, 16)

        ALL = 16 * J


        s_ends, s_gx = sems("s_ends s_gx")
        s_made, s_const, s_w, s_wd, s_w1sb, s_mixp = sems("s_made s_const s_w s_wd s_w1sb s_mixp")
        loads = [
            (w1_dup[0:D, :], W1), (w1_dup[D:128, :], W1),
            (w2_ext[:, 0:128], W2), (out_w[0:D, :], Wn),
            (att1[:, 0:2, :], as1.unsqueeze(0).to_broadcast([128, H, D])),
            (att1[:, 2:4, :], ad1.unsqueeze(0).to_broadcast([128, H, D])),
            (att2[:, 0:2, :], as2.unsqueeze(0).to_broadcast([128, H, D])),
            (att2[:, 2:4, :], ad2.unsqueeze(0).to_broadcast([128, H, D])),
            (b1_col[:, :], b1.unsqueeze(1)), (b2_row[:, :], b2.unsqueeze(0)), (bn_row[:, :], bn.unsqueeze(0)),
            (b2_all[:, :], b2.unsqueeze(0).to_broadcast([P, D])), (bn_all[:, :], bn.unsqueeze(0).to_broadcast([P, D])),
            (bl_row[:, :], bl.unsqueeze(0)),
            (gw[:, :, :], gate_w.rearrange("(s f) o -> o s f", s=2).to_broadcast([P, 2, D])),
            (gb[:, :], gate_b.unsqueeze(0).to_broadcast([P, 1])),
            (beta_all[:, :], beta.unsqueeze(0).to_broadcast([P, 1])),
        ]
        with nc.Block() as block:
            @block.sync
            def _(sp):
                sp.dma_start(src_i[:, :], edges_of(src)).then_inc(s_ends, 16)
                sp.dma_start(dst_i[:, :], edges_of(dst)).then_inc(s_ends, 16)
                for to, frm in loads:
                    sp.dma_start(to, frm).then_inc(s_w, 16)
                sp.wait_ge(s_made, 1)
                for h in range(2):
                    half = slice(h * D, h * D + D)
                    sp.dma_start(wl_diag[half, half], Wl).then_inc(s_wd, 16)
                    sp.dma_start(wn_diag[half, half], Wn).then_inc(s_wd, 16)
                sp.wait_ge(s_made, 2)
                sp.dma_start(node_w[D:D + 1, :], bias_row[:, :]).then_inc(s_wd, 16)
                for h in range(2):
                    half = slice(h * D, h * D + D)
                    sp.dma_start(wn_pair[half, half], out_w[:, :]).then_inc(s_wd, 16)
                for to, frm, times, width in ((wn_bias, bias_parts[0], NC, D), (wl_bias, bias_parts[1], NC, D), (h2_bias, bias_parts[2], 3, W2ROW)):
                    for k in range(3):
                        sp.dma_start(to[k:k + 1, :].rearrange("o (c f) -> o c f", f=width),
                                     frm[:, k].unsqueeze(1).to_broadcast([1, times, width])).then_inc(s_wd, 16)
                sp.wait_ge(s_wd, (4 + 1 + 2 + 9) * 16)

            @block.gpsimd
            def _(g):
                pool.link(g.memset(ident[:, :], 0.0))
                pool.link(g.affine_select(out=ident[:, :], in_=ident[:, :], compare_op=ALU.not_equal, fill=1.0,
                                          base=0, pattern=[[-1, 128]], channel_multiplier=1))
                g.memset(eps[:, :], EPS)
                g.memset(eps8[:, :], 1e-8).then_inc(s_const, 1)
                g.wait_ge(s_ends, 2 * 16)
                gather(g, xs, x, src_i, s_gx, range(START[0]))

            @block.vector
            def _(dve):
                for t in (w1_t_diag, wl_diag, wa_pair, wn_pair):
                    dve.memset(t[:, :], 0.0)
                dve.memset(wn_diag[:, :], 0.0).then_inc(s_made, 1)
                dve.wait_ge(s_w, 16 * len(loads))
                for k in range(4):
                    part = slice((k % H) * D, (k % H) * D + D)
                    v.link(dve.tensor_tensor(att_tmp[:, k, :], w1_dup[:, part], att1[:, k, :], ALU.mult))
                v.link(dve.tensor_reduce(wa[:, :], att_tmp[:, :, :], AX, ALU.add))
                for h in range(2):
                    half = slice(h * D, h * D + D)
                    dve.tensor_copy(wa_pair[half, 4 * h:4 * h + 4], wa[half, :])
                for k in range(4):
                    part = slice((k % H) * D, (k % H) * D + D)
                    v.link(dve.tensor_tensor(att_tmp[:, k, :], w2_ext[:, part], att2[:, k, :], ALU.mult))
                v.link(dve.tensor_reduce(w2_ext[:, 128:132], att_tmp[:, :, :], AX, ALU.add))
                v.link(dve.tensor_tensor(w2_mean[:, :], w2_ext[:, 0:D], w2_ext[:, D:128], ALU.add))
                v.link(dve.tensor_scalar(w2_mean[:, :], w2_mean[:, :], 0.5, None, ALU.mult))
                dve.wait_ge(s_mixp, 1)
                v.link(dve.tensor_copy(w1_t[:, :], bank[0][:, 0:D]))
                for h in range(H):
                    half = slice(h * D, h * D + D)
                    done = dve.tensor_copy(w1_t_diag[half, half], w1_t[half, :])
                done.then_inc(s_w1sb, 1)
                dve.wait_ge(s_mixp, 2)

                def centre(rows, m):
                    v.link(dve.tensor_reduce(row_mean[0:rows, :], m, AX, ALU.add))
                    v.link(dve.tensor_scalar(row_mean[0:rows, :], row_mean[0:rows, :], 1.0 / D, None, ALU.mult))
                    v.link(dve.tensor_scalar(m, m, row_mean[0:rows, :], None, ALU.subtract))

                y_cols = slice(W2ROW + 4, NW)
                v.link(dve.tensor_copy(heads_w[:, :], bank[3][:, 0:W2ROW]))
                v.link(dve.tensor_copy(node_w[0:D, 0:W2ROW], bank[1][0:D, 0:W2ROW]))
                v.link(dve.tensor_copy(node_w[0:D, W2ROW:W2ROW + 4], wa[0:D, :]))
                v.link(dve.tensor_tensor(node_w[0:D, y_cols], bank[1][0:D, W2ROW:W2ROW + D], ident[0:D, 0:D], ALU.add))
                centre(D, node_w[0:D, y_cols])
                v.link(dve.tensor_tensor(out_w[0:D, :], out_w[0:D, :], ident[0:D, 0:D], ALU.add))
                centre(D, out_w[0:D, :])
                v.link(dve.memset(bias_row[:, :], 0.0))
                v.link(dve.tensor_copy(bias_row[:, 0:W2ROW], bank[2][0:1, 0:W2ROW]))
                v.link(dve.tensor_tensor(bias_row[:, y_cols], bank[2][0:1, W2ROW:W2ROW + D], b2_row[:, :], ALU.add))
                centre(1, bias_row[:, y_cols])
                centre(1, bn_row[:, :])
                v.link(dve.memset(ones3[:, :], 1.0))
                for row, to, w in ((bn_row, bias_parts[0], D), (bl_row, bias_parts[1], D), (bias_row, bias_parts[2], W2ROW)):
                    v.link(dve.tensor_copy(rest[:, 0:w], row[:, 0:w]))
                    for k in range(3):
                        v.link(dve.tensor_copy(piece[:, 0:w], rest[:, 0:w]))
                        v.link(dve.tensor_copy(to[:, k], piece[:, 0:w]))
                        v.link(dve.tensor_tensor(rest[:, 0:w], rest[:, 0:w], piece[:, 0:w], ALU.subtract))
                for u in range(U):
                    dve.memset(x1_in[u][:, :, D:D + 1], 1.0)
                    done = dve.memset(r_x1[u][:, :, D:D + 1], 1.0)
                done.then_inc(s_made, 1)

            @block.tensor
            def _(pe):
                pe.wait_ge(s_w, 16 * len(loads))
                pe.wait_ge(s_const, 1)
                pe.transpose(bank[0][:, 0:D], w1_dup[0:D, :], ident[0:D, 0:D]).then_inc(s_mixp, 1)
                pe.wait_ge(s_w1sb, 1)
                pe.matmul(bank[3][:, 0:W2ROW], w1_t_diag[:, :], w2_ext[:, :], start=True, stop=True)
                for rows, w in ((bank[1][0:D, :], w1_t[:, :]), (bank[2][0:1, :], b1_col[:, :])):
                    pe.matmul(rows[:, 0:W2ROW], w, w2_ext[:, :], start=True, stop=True)
                    done = pe.matmul(rows[:, W2ROW:W2ROW + D], w, w2_mean[:, :], start=True, stop=True)
                done.then_inc(s_mixp, 1)

        def rowbuf(name, width, n=U):
            return [sb(f"{name}{u}", [P, NC, width]) for u in range(n)]

        n_in, n_c, n_sq, n_out = rowbuf("n_in", D), rowbuf("n_c", D), rowbuf("n_sq", D), rowbuf("n_out", D)
        r_h2, r_x2 = rowbuf("r_h2", W2ROW), rowbuf("r_x2", D)
        r_x3 = r_x2
        n_t = [sb(f"n_t{u}", [128, NC // 2 * P]) for u in range(U)]
        o1_t = sb("o1_t", [128, 2, NC // 2 * P])
        n_mean, n_var, n_sd, n_r = ([sb(f"n_{n}{u}", [P, NC]) for u in range(U)] for n in ("mean", "var", "sd", "r"))
        n_var2, n_sd2, n_r2 = ([sb(f"n_{n}{u}", [P, NC]) for u in range(U)] for n in ("var2", "sd2", "r2"))
        e_dup = [sb(f"e_dup{u}", [P, NC, 2, D]) for u in range(U)]
        NCH = NJ // NC

        def phase(name, names, double=""):
            made = {n: sem(f"s_{name}_{n}") for n in names.split()}
            made.update({n: [sem(f"s_{name}_{n}{u}") for u in range(U)] for n in double.split()})
            return type(name, (), made)

        def flat(t):
            return t.rearrange("p c f -> p (c f)")

        def wide(t, width=D):
            return t.unsqueeze(2).to_broadcast([P, t.shape[1], width])

        def cols3(t):
            return t.rearrange("p (c f) -> p c f", f=D)

        def is_first(i):
            return isinstance(i, int) and i == 0

        def is_at(i, n):
            return isinstance(i, int) and i == n

        def h2_slot(c):
            return bank[4 + c // 3][0:P, c % 3 * W2ROW:c % 3 * W2ROW + W2ROW]

        def node_rows(t, i, u, width):
            return t.rearrange("(p j) f -> p (j f)", p=P)[:, bass.ds((2 * i + u) * NC * width, NC * width)]

        def transposed_rows(pe, rows, u):
            for c in range(NC):
                done = pe.transpose(bank[4 + 2 * u + c // 4][0:D + 1, c % 4 * P:c % 4 * P + P], rows[:, c, :], ident[0:P, 0:P])
            return done

        def transposed_act(u):
            return nc.scalar.copy(x_t[u][:, :].rearrange("f (b n) -> f b n", b=2), banks[0:D + 1, 4 + 2 * u:6 + 2 * u, 0:NC // 2 * P])

        def add_bias(pe, to, bias):
            pe.matmul(to, ones3[:, 0:P], bias, start=True, stop=False)

        sn = phase("node", "centred squares squares2 var var2 dev dev2 x1 turned turned_sb x1_rows product terms row x2", "loaded x1_out h2_out x2_out")
        product = [banks[0:P, 2 * h:2 * h + 2, 0:2 * NW].rearrange("p b (c w) -> p b c w", w=NW) for h in range(2)]
        NPAIRS = NCH // 2

        def half(t, h):
            return t[:, h * NC // 2:(h + 1) * NC // 2, :].rearrange("p (b c) w -> p b c w", c=2)

        def nodes_sp(sp):
            def load(i, u):
                sp.dma_start(flat(n_in[u][:, :, :]), node_rows(x, i, u, D)).then_inc(sn.loaded[u], 16)

            def store(i):
                for u in range(U):
                    sp.wait_ge(sn.terms, 4 * i + 2 * u + 2)
                    sp.dma_start(node_rows(X1, i, u, W1ROW), flat(r_x1[u][:, :, :])).then_inc(sn.x1_out[u], 16)
                    sp.wait_ge(sn.row, 4 * i + 2 * u + 2)
                    sp.dma_start(node_rows(H2, i, u, W2ROW), flat(r_h2[u][:, :, :])).then_inc(sn.h2_out[u], 16)

            def store_x2(i):
                for u in range(U):
                    sp.wait_ge(sn.x2, 2 * i + u + 1)
                    sp.dma_start(node_rows(X2, i, u, D), flat(r_x2[u][:, :, :])).then_inc(sn.x2_out[u], 16)

            def load_next(i):
                for u in range(U):
                    sp.wait_ge(sn.centred, 2 * i + u + 1)
                    load(i + 1, u)

            for u in range(U):
                load(0, u)
            load_next(0)
            load_next(1)
            with nc.sync.Fori(2, NPAIRS - 1) as i:
                store(i - 2)
                load_next(i)
                store_x2(i - 2)
            for i in range(NPAIRS - 3, NPAIRS):
                store(i)
                store_x2(i)
            for u in range(U):
                for s in (sn.x1_out, sn.h2_out, sn.x2_out):
                    sp.wait_ge(s[u], 16 * NPAIRS)

        def nodes_dve(dve, gate_dots):
            def body(i, a, b, c):
                j, k = i - 1, i - 2
                if b:
                    for u in range(U):
                        dve.wait_ge(sn.squares, 2 * j + u + 1)
                        dve.tensor_reduce(n_var[u][:, :], n_sq[u][:, :, :], AX, ALU.add).then_inc(sn.var, 1)
                if c:
                    for u in range(U):
                        if not is_at(i, 2):
                            dve.wait_ge(sn.x1_out[u], 16 * k)
                        dve.tensor_copy(r_x1[u][:, :, 0:D], x1_in[u][:, :, 0:D]).then_inc(sn.x1_rows, 1)
                if b:
                    for u in range(U):
                        dve.wait_ge(sn.dev, 2 * j + u + 1)
                        v.link(dve.reciprocal(n_r[u][:, :], n_sd[u][:, :]))
                        if not is_at(i, 1):
                            dve.wait_ge(sn.turned, 2 * j - 1 + u)
                            dve.wait_ge(sn.x1_rows, 2 * j - 1 + u)
                        dve.tensor_tensor(x1_in[u][:, :, 0:D], n_c[u][:, :, :], wide(n_r[u][:, :]), ALU.mult).then_inc(sn.x1, 1)
                if a:
                    for u in range(U):
                        dve.wait_ge(sn.loaded[u], 16 * i + 16)
                        v.link(dve.tensor_reduce(n_mean[u][:, :], n_in[u][:, :, :], AX, ALU.add))
                        v.link(dve.tensor_scalar(n_mean[u][:, :], n_mean[u][:, :], -1.0 / D, None, ALU.mult))
                        dve.tensor_tensor(n_c[u][:, :, :], n_in[u][:, :, :], wide(n_mean[u][:, :]), ALU.add).then_inc(sn.centred, 1)
                if c:
                    for u in range(U):
                        dve.wait_ge(sn.squares2, 4 * k + 2 * u + 2)
                        dve.tensor_reduce(n_var2[u][:, :], n_out[u][:, :, :], AX, ALU.add).then_inc(sn.var2, 1)
                    for u in range(U):
                        dve.wait_ge(sn.dev2, 2 * k + u + 1)
                        v.link(dve.reciprocal(n_r2[u][:, :], n_sd2[u][:, :]))
                        if not is_at(i, 2):
                            dve.wait_ge(sn.x2_out[u], 16 * k)
                        dve.wait_ge(sn.row, 4 * k + 2 * u + 2)
                        dve.tensor_tensor(r_x2[u][:, :, :], e_dup[u][:, :, 0, :], wide(n_r2[u][:, :]), ALU.mult).then_inc(sn.x2, 1)
            skewed3(nc.vector, NPAIRS, body, v, J // NC, lambda i: gate_dots(dve, i))

        def nodes_act(act):
            def body(i, a, b, c):
                j, k = i - 1, i - 2
                if b:
                    for u in range(U):
                        act.wait_ge(sn.var, 2 * j + u + 1)
                        nc.scalar.activation(n_sd[u][:, :], n_var[u][:, :], ACT.Sqrt, bias=eps[0:P, :]).then_inc(sn.dev, 1)
                for u in range(U):
                    if c:
                        act.wait_ge(sn.x1_rows, 2 * k + u + 1)
                        for h in range(2):
                            act.wait_ge(sn.product, 4 * k + 2 * u + h + 1)
                            y = product[h][:, :, :, W2ROW + 4:NW]
                            nc.scalar.copy(half(r_x1[u][:, :, D + 1:W1ROW], h), product[h][:, :, :, W2ROW:W2ROW + 4]).then_inc(sn.terms, 1)
                            nc.scalar.activation(half(n_out[u][:, :, :], h), y, ACT.Square, scale=D ** -0.5).then_inc(sn.squares2, 1)
                            if h == 0 and not is_at(i, 2):
                                act.wait_ge(sn.x2, 2 * k - 1 + u)
                                act.wait_ge(sn.h2_out[u], 16 * k)
                            nc.scalar.copy(half(e_dup[u][:, :, 0, :], h), y)
                            nc.scalar.copy(half(r_h2[u][:, :, :], h), product[h][:, :, :, 0:W2ROW]).then_inc(sn.row, 1)
                    if b:
                        act.wait_ge(sn.turned, 2 * j + u + 1)
                        transposed_act(u).then_inc(sn.turned_sb, 1)
                if a:
                    for u in range(U):
                        act.wait_ge(sn.centred, 2 * i + u + 1)
                        nc.scalar.activation(flat(n_sq[u][:, :, :]), flat(n_c[u][:, :, :]), ACT.Square, scale=D ** -0.5).then_inc(sn.squares, 1)
                if c:
                    for u in range(U):
                        act.wait_ge(sn.var2, 2 * k + u + 1)
                        nc.scalar.activation(n_sd2[u][:, :], n_var2[u][:, :], ACT.Sqrt, bias=eps[0:P, :]).then_inc(sn.dev2, 1)
            skewed3(nc.scalar, NPAIRS, body)

        def nodes_pe(pe):
            def body(i, a, b, c):
                j, k = i - 1, i - 2
                for u in range(U):
                    if c:
                        pe.wait_ge(sn.turned_sb, 2 * k + u + 1)
                        for h in range(2):
                            if u or not is_at(i, 2):
                                pe.wait_ge(sn.row, 4 * k - 1 + 2 * u + h)
                            for n in range(NC // 2):
                                at = (h * NC // 2 + n) * P
                                done = pe.matmul(product[h][:, n // 2, n % 2, :], x_t[u][:, at:at + P], node_w[:, :], start=True, stop=True)
                            done.then_inc(sn.product, 1)
                    if b:
                        pe.wait_ge(sn.x1, 2 * j + u + 1)
                        transposed_rows(pe, x1_in[u], u).then_inc(sn.turned, 1)
            skewed3(nc.tensor, NPAIRS, body)

        sx3 = phase("x3", "squares var dev x3", "loaded stored")

        def x3_sp(sp):
            def body(i, a, b):
                for u in range(U):
                    if a:
                        if b:
                            sp.wait_ge(sx3.x3, 2 * i - 1 + u)
                        sp.dma_start(flat(r_x2[u][:, :, :]), node_rows(X2, i, u, D)).then_inc(sx3.loaded[u], 16)
                    if b:
                        if not a:
                            sp.wait_ge(sx3.x3, 2 * i - 1 + u)
                        sp.dma_start(node_rows(X3, i - 1, u, D), flat(n_out[u][:, :, :])).then_inc(sx3.stored[u], 16)
            skewed(nc.sync, NPAIRS, body)

        def x3_stored(eng):
            for u in range(U):
                eng.wait_ge(sx3.stored[u], 16 * NPAIRS)

        def x3_dve(dve):
            def body(i, us):
                for u in us:
                    dve.wait_ge(sx3.squares, turn(i, 1, 0, u, us))
                    dve.tensor_reduce(n_var[u][:, :], n_sq[u][:, :, :], AX, ALU.add).then_inc(sx3.var, 1)
                for u in us:
                    dve.wait_ge(sx3.dev, turn(i, 1, 0, u, us))
                    v.link(dve.reciprocal(n_r[u][:, :], n_sd[u][:, :]))
                    if not is_first(i):
                        dve.wait_ge(sx3.stored[u], 16 * i)
                    dve.tensor_tensor(n_out[u][:, :, :], r_x2[u][:, :, :], wide(n_r[u][:, :]), ALU.mult).then_inc(sx3.x3, 1)
            pairs(nc.vector, NCH, body, v)

        def x3_act(act):
            def body(i, us):
                for u in us:
                    act.wait_ge(sx3.loaded[u], 16 * i + 16)
                    nc.scalar.activation(flat(n_sq[u][:, :, :]), flat(r_x2[u][:, :, :]), ACT.Square, scale=D ** -0.5).then_inc(sx3.squares, 1)
                for u in us:
                    act.wait_ge(sx3.var, turn(i, 1, 0, u, us))
                    nc.scalar.activation(n_sd[u][:, :], n_var[u][:, :], ACT.Sqrt, bias=eps[0:P, :]).then_inc(sx3.dev, 1)
            pairs(nc.scalar, NCH, body)

        OUT_SPLIT = NPAIRS * 3 // 5
        outs = ((0, OUT_SPLIT), (OUT_SPLIT, NPAIRS))
        so = phase("out", "turned turned_sb y squares copied var dev row", "loaded stored")

        def out_sp(sp, part):
            start, end = part

            def load(i, u):
                sp.dma_start(flat(n_c[u][:, :, :]), node_rows(X3, i, u, D)).then_inc(so.loaded[u], 16)

            def store(i, u):
                sp.wait_ge(so.row, 2 * i + u + 1)
                sp.dma_start(node_rows(out, i, u, D), flat(n_out[u][:, :, :])).then_inc(so.stored[u], 16)

            for u in range(U):
                if start:
                    sp.wait_ge(so.turned, 2 * start - 1 + u)
                load(start, u)
            for u in range(U):
                sp.wait_ge(so.turned, 2 * start + u + 1)
                load(start + 1, u)
            with nc.sync.Fori(start + 2, end) as i:
                for u in range(U):
                    sp.wait_ge(so.turned, 2 * i - 1 + u)
                    load(i, u)
                for u in range(U):
                    store(i - 2, u)
            for i in (end - 2, end - 1):
                for u in range(U):
                    store(i, u)

        def out_stored(eng, part):
            for u in range(U):
                eng.wait_ge(so.stored[u], 16 * part[1])

        def out_pe(pe, part):
            start, end = part

            def body(i, a, b):
                if b:
                    for u in range(U):
                        pe.wait_ge(so.turned_sb, 2 * i - 1 + u)
                        if not is_at(i, 1):
                            pe.wait_ge(so.copied, 2 * i - 3 + u)
                        add_bias(pe, bank[2 + u][0:P, :], wn_bias[:, :])
                        for c in range(NC // 2):
                            done = pe.matmul(bank[2 + u][0:P, c * 128:(c + 1) * 128], n_t[u][:, c * P:(c + 1) * P], wn_pair[:, :],
                                             start=False, stop=c == NC // 2 - 1)
                        done.then_inc(so.y, 1)
                if a:
                    for u in range(U):
                        pe.wait_ge(so.loaded[u], 16 * i + 16)
                        for c in range(NC // 2):
                            done = pe.transpose(bank[6 + u][:, c * P:(c + 1) * P], flat(n_c[u][:, 2 * c:2 * c + 2, :]), ident[0:P, 0:P])
                        done.then_inc(so.turned, 1)
            skewed(nc.tensor, end - start, lambda i, a, b: body(i + start, a, b))

        def out_act(act, part):
            start, end = part

            def body(i, a, b):
                if a:
                    for u in range(U):
                        act.wait_ge(so.turned, 2 * i + u + 1)
                        if b:
                            act.wait_ge(so.y, 2 * i - 1 + u)
                        nc.scalar.copy(n_t[u][:, :], bank[6 + u][:, 0:NC // 2 * P]).then_inc(so.turned_sb, 1)
                if b:
                    for u in range(U):
                        act.wait_ge(so.y, 2 * i - 1 + u)
                        nc.scalar.activation(flat(n_sq[u][:, :, :]), bank[2 + u][0:P, :], ACT.Square, scale=D ** -0.5).then_inc(so.squares, 1)
                        if not is_at(i, 1):
                            act.wait_ge(so.row, 2 * i - 3 + u)
                        nc.scalar.copy(e_dup[u][:, :, 0, :], cols3(bank[2 + u][0:P, :])).then_inc(so.copied, 1)
                    for u in range(U):
                        act.wait_ge(so.var, 2 * i - 1 + u)
                        nc.scalar.activation(n_sd[u][:, :], n_var[u][:, :], ACT.Sqrt, bias=eps[0:P, :]).then_inc(so.dev, 1)
            skewed(nc.scalar, end - start, lambda i, a, b: body(i + start, a, b))

        def out_dve(dve, part):
            start, end = part

            def body(i, us):
                for u in us:
                    dve.wait_ge(so.squares, turn(i, 1, 0, u, us))
                    dve.tensor_reduce(n_var[u][:, :], n_sq[u][:, :, :], AX, ALU.add).then_inc(so.var, 1)
                for u in us:
                    dve.wait_ge(so.dev, turn(i, 1, 0, u, us))
                    v.link(dve.reciprocal(n_r[u][:, :], n_sd[u][:, :]))
                    if not is_first(i):
                        dve.wait_ge(so.stored[u], 16 * i)
                    dve.wait_ge(so.copied, turn(i, 1, 0, u, us))
                    dve.tensor_tensor(n_out[u][:, :, :], e_dup[u][:, :, 0, :], wide(n_r[u][:, :]), ALU.mult).then_inc(so.row, 1)
            pairs(nc.vector, 2 * (end - start), lambda i, us: body(i + start, us), v)

        key, key_prev, key_next = plane("key"), plane("key_prev"), plane("key_next")
        key_i, prev_i, next_i = plane("key_i", I32), plane("prev_i", I32), plane("next_i", I32)
        cont, last, more = plane("cont"), plane("last"), plane("more")
        reach_f, reach_r = plane("reach_f"), plane("reach_r")
        pen_f, pen_reach = plane("pen_f"), plane("pen_reach")
        norm_d, norm_s = plane("norm_d"), plane("norm_s")
        heads = [plane(f"head{h}") for h in range(2)]
        tops = [plane(f"top{h}") for h in range(2)]
        dens = [plane(f"den{h}") for h in range(2)]
        selfs = [plane(f"self{h}") for h in range(2)]
        pass_f_t, pen_f_t, pass_r_t = (sb(n, [128, P]) for n in ("pass_f_t", "pen_f_t", "pass_r_t"))
        cross_in = sb("cross_in", [128, 128])
        crossed = sb("crossed", [128, P + 1])
        carry_in, ends = sb("carry_in", [P, 2]), sb("ends", [P, 2])
        carry_rows = [sb(f"carry_rows{h}", [P, D]) for h in range(2)]
        s_tin, s_tout = sems("s_tin s_tout")
        crossings = {"dve": 0, "pe": 0}

        ECH = J // NC

        def chunk(t, i, u):
            return t[:, bass.ds((2 * i + u) * NC, NC)] if len(t.shape) == 2 else t[:, bass.ds((2 * i + u) * NC, NC), :]

        def tall(row):
            return row[:, :].unsqueeze(1).to_broadcast([P, NC, D])

        def dots_dve(dve, products, chunks):
            start = v.n
            with nc.vector.Fori(chunks[0], chunks[1]) as i:
                v.base, v.n = (i - chunks[0]) * 2 + start, 0
                for tmp, a, b, _ in products:
                    other = tall(b) if len(b.shape) == 2 else b[:, bass.ds(i * NC, NC), :]
                    done = dve.tensor_tensor(tmp[:, :, :], a[:, bass.ds(i * NC, NC), :], other, ALU.mult)
                v.link(done)
                for tmp, _, _, to in products:
                    done = dve.tensor_reduce(to[:, bass.ds(i * NC, NC)], tmp[:, :, :], AX, ALU.add)
                v.link(done)
            v.base, v.n = 0, start + 2 * (chunks[1] - chunks[0])

        def transpose_dve(dve, ins):
            ins.then_inc(s_tin, 1)
            crossings["dve"] += 1
            dve.wait_ge(s_tout, crossings["dve"])

        def transpose_pe(pe, frm, rows, cols):
            crossings["pe"] += 1
            pe.wait_ge(s_tin, crossings["pe"])
            pe.transpose(bank[0][0:cols, 0:rows], frm, ident[0:rows, 0:rows]).then_inc(s_tout, 1)

        def segments_dve(dve):
            dve.tensor_tensor(cont[:, :], key[:, :], key_prev[:, :], ALU.is_equal)
            dve.tensor_tensor(last[:, :], key[:, :], key_next[:, :], ALU.not_equal)
            v.link(dve.tensor_tensor(more[:, :], key[:, :], key_next[:, :], ALU.is_equal))
            dve.tensor_scalar(pen_f[:, :], cont[:, :], 1.0, -LOW, ALU.subtract, ALU.mult)
            dve.tensor_tensor_scan(reach_f[:, :], cont[:, :], cont[:, :], 1.0, ALU.mult, ALU.mult)
            v.link(dve.tensor_tensor_scan(reach_r[:, ::-1], more[:, ::-1], more[:, ::-1], 1.0, ALU.mult, ALU.mult))
            dve.tensor_scalar(pen_reach[:, :], reach_f[:, :], 1.0, -LOW, ALU.subtract, ALU.mult)
            transpose_dve(dve, dve.tensor_copy(cross_in[0:P, :], reach_f[:, J - 1:J].to_broadcast([P, 128])))
            v.link(dve.tensor_copy(pass_f_t[:, :], bank[0][:, 0:P]))
            dve.tensor_scalar(pen_f_t[:, :], pass_f_t[:, :], 1.0, -LOW, ALU.subtract, ALU.mult)
            transpose_dve(dve, dve.tensor_copy(cross_in[0:P, :], reach_r[:, 0:1].to_broadcast([P, 128])))
            v.link(dve.tensor_copy(pass_r_t[:, :], bank[0][:, 0:P]))

        def segments_pe(pe):
            for _ in range(2):
                transpose_pe(pe, cross_in[0:P, :], P, 128)

        def carry_dve(dve, ends, n, kind, to):
            transpose_dve(dve, dve.tensor_copy(cross_in[0:P, 0:n], ends))
            if kind == "hold":
                v.link(dve.memset(crossed[0:n, P:P + 1], 0.0))
                transpose_dve(dve, dve.tensor_tensor_scan(crossed[0:n, P - 1::-1], pass_r_t[0:n, ::-1], bank[0][0:n, P - 1::-1], 0.0, ALU.mult, ALU.add))
            else:
                first = LOW if kind == "max" else 0.0
                v.link(dve.memset(crossed[0:n, 0:1], first))
                transpose_dve(dve, dve.tensor_tensor_scan(
                    crossed[0:n, 1:P + 1], (pen_f_t if kind == "max" else pass_f_t)[0:n, :], bank[0][0:n, 0:P], first,
                    ALU.add if kind == "max" else ALU.mult, ALU.max if kind == "max" else ALU.add))
            v.link(dve.tensor_copy(to, bank[0][0:P, 0:n]))

        def carry_pe(pe, n, kind):
            transpose_pe(pe, cross_in[0:P, 0:n], P, n)
            transpose_pe(pe, crossed[0:n, 1:P + 1] if kind == "hold" else crossed[0:n, 0:P], n, P)

        def over_segments(dve, kind, ws):
            if kind == "hold":
                for w in ws:
                    done = dve.tensor_tensor(w, w, last[:, :], ALU.mult)
                v.link(done)
                for w in ws:
                    done = dve.tensor_tensor_scan(w[:, ::-1], more[:, ::-1], w[:, ::-1], 0.0, ALU.mult, ALU.add)
            elif kind == "max":
                for w in ws:
                    done = dve.tensor_tensor_scan(w, pen_f[:, :], w, LOW, ALU.add, ALU.max)
            else:
                for w in ws:
                    done = dve.tensor_tensor_scan(w, cont[:, :], w, 0.0, ALU.mult, ALU.add)
            v.link(done)
            at, n = 0 if kind == "hold" else J - 1, len(ws)
            for k, w in enumerate(ws):
                done = dve.tensor_copy(ends[:, k:k + 1], w[:, at:at + 1])
            v.link(done)
            carry_dve(dve, ends[:, 0:n], n, kind, carry_in[:, 0:n])
            for k, w in enumerate(ws):
                if kind == "max":
                    done = dve.scalar_tensor_tensor(w, pen_reach[:, :], carry_in[:, k:k + 1], w, ALU.add, ALU.max)
                else:
                    reach = reach_r if kind == "hold" else reach_f
                    done = dve.scalar_tensor_tensor(w, reach[:, :], carry_in[:, k:k + 1], w, ALU.mult, ALU.add)
            v.link(done)

        def over_segments_pe(pe, kind, n):
            carry_pe(pe, n, kind)

        def sum_rows_dve(dve, rows, carry):
            for f in range(D):
                done = dve.tensor_tensor_scan(rows[:, :, f], cont[:, :], rows[:, :, f], 0.0, ALU.mult, ALU.add)
            v.link(done)
            carry_dve(dve, rows[:, J - 1, :], D, "sum", carry[:, :])

        def add_carry(dve, to, rows, carry, i, u, tmp):
            v.link(dve.tensor_tensor(tmp, wide(chunk(reach_f, i, u)), tall(carry), ALU.mult))
            v.link(dve.tensor_tensor(to, chunk(rows, i, u), tmp, ALU.add))


        SF, SLOT_BITS = SORT // 128, SORT.bit_length() - 1
        F_BITS = SF.bit_length() - 1
        k_srt = [n_t[n][:, 0:SF] for n in range(2)]
        d_srt = [o1_t[:, n, 0:SF] for n in range(2)]
        s_srt, ki_srt, di_srt = (t[:, :, :].rearrange("p k f -> p (k f)") for t in (att_tmp, att1, att2))
        ki_srt, di_srt = ki_srt.bitcast(I32), di_srt.bitcast(I32)
        gray_i, bits_i = sb("gray_i", [128, SF], I32), sb("bits_i", [128, SF], I32)
        s_sl, s_sio, s_sfill, s_sst, s_sorted = sems("s_sl s_sio s_sfill s_sst s_sorted")
        s_stin, s_stout = sems("s_stin s_stout")
        FULL = EDGES // SF

        def sort_steps():
            for merge in range(1, SLOT_BITS + 1):
                yield "direct", merge
                if merge > F_BITS:
                    yield "turn", 0
                    for bit in range(merge - 1, F_BITS - 1, -1):
                        yield "exchange", bit - F_BITS
                    yield "turn", 0
                for bit in range(min(merge, F_BITS) - 1, -1, -1):
                    yield "exchange", bit

        STEPS = list(sort_steps())
        CUT = STEPS.index(("direct", SLOT_BITS - 1))
        PARTS = ((0, CUT), (CUT, len(STEPS)))
        held = [t[:, :, :].rearrange("p k f -> p (k f)") for t in (att1, att2)]

        def turns_before(step):
            return sum(what == "turn" for what, _ in STEPS[:step])

        def sort_sp(sp):
            sp.wait_ge(s_sfill, 1)
            for to, frm in ((ki_srt, src), (di_srt, dst)):
                sp.dma_start(to[0:FULL, :], frm[0:FULL * SF].rearrange("(p f) -> p f", f=SF)).then_inc(s_sl, 16)
                sp.dma_start(to[FULL:FULL + 1, 0:EDGES - FULL * SF], frm[FULL * SF:EDGES].unsqueeze(0)).then_inc(s_sl, 16)

        def sort_store_sp(sp):
            sp.wait_ge(s_sorted, 2)
            for n, frm in enumerate((ki_srt, di_srt)):
                sp.dma_start(SORTED[n].rearrange("(p f) -> p f", f=SF), frm[:, :]).then_inc(s_sst, 16)
            sp.wait_ge(s_sst, 32)

        def sort_fill_dve(dve):
            dve.memset(di_srt[:, :], 0)
            dve.memset(ki_srt[:, :], FAR).then_inc(s_sfill, 1)

        def sort_start_dve(dve):
            dve.wait_ge(s_sio, 1)
            v.link(dve.tensor_single_scalar(bits_i[:, :], gray_i[:, :], 1, ALU.logical_shift_right))
            v.link(dve.tensor_tensor(gray_i[:, :], gray_i[:, :], bits_i[:, :], ALU.bitwise_xor))
            dve.wait_ge(s_sl, 64)
            dve.tensor_copy(d_srt[0][:, :], di_srt[:, :])
            v.link(dve.tensor_copy(k_srt[0][:, :], ki_srt[:, :]))

        def sort_resume_dve(dve):
            dve.tensor_copy(d_srt[0][:, :], held[1])
            v.link(dve.tensor_copy(k_srt[0][:, :], held[0]))

        def sort_dve(dve, part, to_k, to_d):
            now, turns = 0, turns_before(part[0])
            for n in range(*part):
                what, bit = STEPS[n]
                hand_over = n + 1 < len(STEPS) and STEPS[n + 1][0] == "turn"
                k0, k1, d0, d1 = (t[:, :] for t in (k_srt[now], k_srt[1 - now], d_srt[now], d_srt[1 - now]))
                if what == "direct":
                    if bit == 1:
                        v.link(dve.tensor_scalar(bits_i[:, :], bits_i[:, :], 1, None, ALU.bitwise_and))
                    else:
                        v.link(dve.tensor_scalar(bits_i[:, :], gray_i[:, :], bit - 1, 1, ALU.logical_shift_right, ALU.bitwise_and))
                    v.link(dve.tensor_scalar(s_srt[:, :], bits_i[:, :], -2.0, 1.0, ALU.mult, ALU.add))
                    done = dve.tensor_tensor(k0, k0, s_srt[:, :], ALU.mult)
                elif what == "turn":
                    turns += 1
                    dve.wait_ge(s_stout, turns)
                    dve.tensor_copy(k1, bank[0][:, 0:SF])
                    done = dve.tensor_copy(d1, bank[0][:, SF:2 * SF])
                    now = 1 - now
                else:
                    k0, k1, d0, d1 = (t.rearrange("p (n two d) -> p n two d", two=2, d=1 << bit) for t in (k0, k1, d0, d1))
                    swap = s_srt[:, 0:SF // 2].rearrange("p (n d) -> p n d", d=1 << bit)
                    diff = s_srt[:, SF // 2:SF].rearrange("p (n d) -> p n d", d=1 << bit)
                    dve.tensor_tensor(swap, k0[:, :, 0], k0[:, :, 1], ALU.is_gt)
                    v.link(dve.tensor_tensor(diff, d0[:, :, 1], d0[:, :, 0], ALU.subtract))
                    v.link(dve.tensor_tensor(diff, diff, swap, ALU.mult))
                    dve.tensor_tensor(k1[:, :, 0], k0[:, :, 0], k0[:, :, 1], ALU.min)
                    dve.tensor_tensor(k1[:, :, 1], k0[:, :, 0], k0[:, :, 1], ALU.max)
                    dve.tensor_tensor(d1[:, :, 0], d0[:, :, 0], diff, ALU.add)
                    done = dve.tensor_tensor(d1[:, :, 1], d0[:, :, 1], diff, ALU.subtract)
                    now = 1 - now
                if hand_over:
                    done.then_inc(s_stin, 1)
                else:
                    v.link(done)
            dve.tensor_copy(to_k, k_srt[now][:, :])
            dve.tensor_copy(to_d, d_srt[now][:, :]).then_inc(s_sorted, 1)

        def sort_pe(pe, part):
            now, turns = 0, turns_before(part[0])
            for what, _ in STEPS[part[0]:part[1]]:
                if what == "turn":
                    turns += 1
                    pe.wait_ge(s_stin, turns)
                    for h in range(SF // 128):
                        part = slice(h * 128, h * 128 + 128)
                        pe.transpose(bank[0][:, part], k_srt[now][:, part], ident[:, :])
                        ins = pe.transpose(bank[0][:, SF + h * 128:SF + h * 128 + 128], d_srt[now][:, part], ident[:, :])
                    ins.then_inc(s_stout, 1)
                if what != "direct":
                    now = 1 - now
        s_idx, s_pre, s_deg, s_sd, s_ninit = sems("s_idx s_pre s_deg s_sd s_ninit")
        fill = e_dup[0][:, :, :, :].rearrange("p c h f -> p (c h f)")[:, 0:NJ]

        def load_order(sp, keys, done):
            sp.dma_start(key_i[:, :], edges_of(keys)).then_inc(done, 16)
            sp.dma_start(prev_i[1:P, :], keys[J - 1:EDGES - 1].rearrange("(p j) -> p j", j=J)).then_inc(done, 16)
            sp.dma_start(prev_i[0:1, 1:J], keys[0:J - 1].unsqueeze(0)).then_inc(done, 16)
            sp.dma_start(next_i[0:P - 1, :], keys[1:EDGES - J + 1].rearrange("(p j) -> p j", j=J)).then_inc(done, 16)
            sp.dma_start(next_i[P - 1:P, 0:J - 1], keys[EDGES - J + 1:EDGES].unsqueeze(0)).then_inc(done, 16)

        def order_dve(dve):
            dve.tensor_copy(key[:, :], key_i[:, :])
            dve.tensor_copy(key_prev[:, :], prev_i[:, :])
            v.link(dve.tensor_copy(key_next[:, :], next_i[:, :]))
            segments_dve(dve)

        def last_only(dve, to, tmp):
            v.link(dve.tensor_scalar(tmp, more[:, :], float(FAR), None, ALU.mult))
            v.link(dve.tensor_tensor(tmp, key[:, :], tmp, ALU.add))
            v.link(dve.tensor_copy(to, tmp))

        with nc.Block() as block:
            @block.gpsimd
            def _(g):
                gather(g, xs, x, src_i, s_gx, range(START[0], START[1]))

            @block.sync
            def _(sp):
                sp.wait_ge(s_pre, 1)
                load_order(sp, dst, s_idx)
                sp.wait_ge(s_pre, 2)
                sp.dma_start(NORM.rearrange("(p j) o -> p (j o)", p=P), fill).then_inc(s_ninit, 16)
                sp.wait_ge(s_ninit, 16)

            @block.vector
            def _(dve):
                dve.memset(prev_i[:, :], -1)
                dve.memset(next_i[:, :], -1).then_inc(s_pre, 1)
                dve.memset(fill, 1.0).then_inc(s_pre, 1)
                v.link(dve.memset(norm_d[:, :], 1.0))
                dve.wait_ge(s_idx, 5 * 16)
                order_dve(dve)
                over_segments(dve, "sum", [norm_d[:, :]])
                v.link(dve.tensor_scalar(norm_d[:, :], norm_d[:, :], 1.0, None, ALU.max))
                dve.tensor_copy(norm_s[:, :], norm_d[:, :]).then_inc(s_deg, 1)
                dve.wait_ge(s_sd, 1)
                v.link(dve.reciprocal(norm_d[:, :], norm_s[:, :]))
                over_segments(dve, "hold", [norm_d[:, :]])
                last_only(dve, scat_i[:, :], heads[0][:, :])

            @block.scalar
            def _(act):
                act.wait_ge(s_deg, 1)
                nc.scalar.activation(norm_s[:, :], norm_s[:, :], ACT.Sqrt).then_inc(s_sd, 1)

            @block.tensor
            def _(pe):
                segments_pe(pe)
                over_segments_pe(pe, "sum", 1)
                over_segments_pe(pe, "hold", 1)

        s_gn, s_sn = sems("s_gn s_sn")

        def gate_dots(dve, i):
            dve.wait_ge(s_gx, 2 * ALL)
            products = ((e_dup[0], xd, 0, heads[0]), (e_dup[1], xs, 1, heads[1]))
            cols = bass.ds(i * NC, NC)
            for tmp, rows, k, _ in products:
                done = dve.tensor_tensor(tmp[:, :, 1, :], rows[:, cols, :], gw[:, k, :].unsqueeze(1).to_broadcast([P, NC, D]), ALU.mult)
            v.link(done)
            for tmp, _, _, to in products:
                done = dve.tensor_reduce(to[:, cols], tmp[:, :, 1, :], AX, ALU.add)
            v.link(done)

        with nc.Block() as block:
            @block.gpsimd
            def _(g):
                gather(g, xs, x, src_i, s_gx, range(START[1], J))
                gather(g, xd, x, dst_i, s_gx)
                scatter(g, NORM, norm_d, scat_i, J, s_sn)
                g.wait_ge(s_sn, ALL)
                gather(g, norm_s, NORM, src_i, s_gn)
                g.wait_ge(s_gx, 2 * ALL)
                g.wait_ge(s_gn, ALL)

            @block.sync
            def _(sp):
                nodes_sp(sp)

            @block.vector
            def _(dve):
                nodes_dve(dve, gate_dots)

            @block.scalar
            def _(act):
                nodes_act(act)

            @block.tensor
            def _(pe):
                nodes_pe(pe)

        def edge_rows(t, i, u, width):
            return t.rearrange("(p j) f -> p (j f)", p=P)[:, bass.ds((2 * i + u) * NC * width, NC * width)]

        def centre_dve(dve, s, i, us):
            for u in us:
                v.link(dve.tensor_reduce(n_mean[u][:, :], n_in[u][:, :, :], AX, ALU.add))
                v.link(dve.tensor_scalar(n_mean[u][:, :], n_mean[u][:, :], -1.0 / D, None, ALU.mult))
                dve.tensor_tensor(n_c[u][:, :, :], n_in[u][:, :, :], wide(n_mean[u][:, :]), ALU.add).then_inc(s.centred, 1)

        def deviation_dve(dve, s, i, us, r=0, rounds=1):
            for u in us:
                dve.wait_ge(s.squares, turn(i, rounds, r, u, us))
                dve.tensor_reduce(n_var[u][:, :], n_sq[u][:, :, :], AX, ALU.add).then_inc(s.var, 1)

        def inverse_dve(dve, s, i, us, u, r=0, rounds=1):
            dve.wait_ge(s.dev, turn(i, rounds, r, u, us))
            v.link(dve.reciprocal(n_r[u][:, :], n_sd[u][:, :]))

        def deviation_act(act, s, i, us, r=0, rounds=1, frm=None):
            for u in us:
                if frm is None:
                    act.wait_ge(s.centred, turn(i, 1, 0, u, us))
                nc.scalar.activation(flat(n_sq[u][:, :, :]), flat(n_c[u][:, :, :]) if frm is None else frm(u), ACT.Square,
                                     scale=D ** -0.5).then_inc(s.squares, 1)
            for u in us:
                act.wait_ge(s.var, turn(i, rounds, r, u, us))
                nc.scalar.activation(n_sd[u][:, :], n_var[u][:, :], ACT.Sqrt, bias=eps[0:P, :]).then_inc(s.dev, 1)

        def transpose_pairs(pe, frm, to):
            for c in range(NC // 2):
                done = pe.transpose(to[:, c * P:(c + 1) * P], flat(frm[:, 2 * c:2 * c + 2, :]), ident[0:P, 0:P])
            return done

        def product_pairs(pe, u, w, to, alone=True):
            for c in range(NC // 2):
                done = pe.matmul(to[0:P, c * 128:(c + 1) * 128], n_t[u][:, c * P:(c + 1) * P], w[:, :], start=alone, stop=alone or c == NC // 2 - 1)
            return done

        def scatter_pass(s, parts):
            def program(g):
                def body(i, us):
                    for rows_ready, table, rows, idx, done in parts:
                        for u in us:
                            g.wait_ge(rows_ready, turn(i, 1, 0, u, us))
                            scatter(g, table, rows[u], idx[:, (2 * i + u) * NC:(2 * i + u + 1) * NC], NC, done[u])
                for i in range((ECH + 1) // 2):
                    body(i, range(min(U, ECH - 2 * i)))
                for _, _, _, _, done in parts:
                    for u in range(U):
                        g.wait_ge(done[u], 16 * NC * ((ECH + 1 - u) // 2))
            return program

        sp_ = phase("proj", "turned turned_sb y row", "loaded stored")

        def project_sp(sp):
            def body(i, us):
                for u in us:
                    if not is_first(i):
                        sp.wait_ge(sp_.turned, 2 * i - 1 + u)
                    sp.dma_start(flat(n_in[u][:, :, :]), edge_rows(edge_attr, i, u, D)).then_inc(sp_.loaded[u], 16)
                for u in us:
                    sp.wait_ge(sp_.row, turn(i, 1, 0, u, us))
                    sp.dma_start(edge_rows(EP, i, u, D), flat(n_out[u][:, :, :])).then_inc(sp_.stored[u], 16)
            pairs(nc.sync, ECH, body)

        def projected(eng):
            for u in range(U):
                eng.wait_ge(sp_.stored[u], 16 * ((ECH + 1 - u) // 2))

        def project_pe(pe):
            def body(i, us):
                for u in us:
                    pe.wait_ge(sp_.loaded[u], 16 * i + 16)
                    if not is_first(i):
                        pe.wait_ge(sp_.turned_sb, 2 * i - 1 + u)
                    transpose_pairs(pe, n_in[u], bank[4 + u]).then_inc(sp_.turned, 1)
                for u in us:
                    pe.wait_ge(sp_.turned_sb, turn(i, 1, 0, u, us))
                    if not is_first(i):
                        pe.wait_ge(sp_.row, 2 * i - 1 + u)
                    add_bias(pe, bank[2 + u][0:P, :], wl_bias[:, :])
                    product_pairs(pe, u, wl_diag, bank[2 + u], False).then_inc(sp_.y, 1)
            pairs(nc.tensor, ECH, body)

        def project_act(act):
            def body(i, us):
                for u in us:
                    act.wait_ge(sp_.turned, turn(i, 1, 0, u, us))
                    nc.scalar.copy(n_t[u][:, :], bank[4 + u][:, 0:NC // 2 * P]).then_inc(sp_.turned_sb, 1)
                for u in us:
                    act.wait_ge(sp_.y, turn(i, 1, 0, u, us))
                    if not is_first(i):
                        act.wait_ge(sp_.stored[u], 16 * i)
                    nc.scalar.copy(flat(n_out[u][:, :, :]), bank[2 + u][0:P, :]).then_inc(sp_.row, 1)
            pairs(nc.scalar, ECH, body)

        s0 = phase("gate", "tanh_in tanh centred squares var dev x1 turned turned_sb terms row", "stored scattered")
        with nc.Block() as block:
            @block.vector
            def _(dve):
                dve.tensor_tensor(heads[0][:, :], heads[0][:, :], heads[1][:, :], ALU.add).then_inc(s0.tanh_in, 1)
                dve.wait_ge(s0.tanh, 1)
                v.link(dve.scalar_tensor_tensor(heads[0][:, :], heads[0][:, :], 0.5, norm_d[:, :], ALU.mult, ALU.mult))
                v.link(dve.tensor_tensor(heads[0][:, :], heads[0][:, :], norm_s[:, :], ALU.mult))
                v.link(dve.tensor_tensor(xs, xs, wide(heads[0][:, :]), ALU.mult))
                sum_rows_dve(dve, xs, carry_rows[0])

                def body(i, us):
                    for u in us:
                        add_carry(dve, n_in[u][:, :, :], xs, carry_rows[0], i, u, n_out[u][:, :, :])
                        v.link(dve.tensor_tensor(n_in[u][:, :, :], n_in[u][:, :, :], chunk(xd, i, u), ALU.add))
                        if not is_first(i):
                            dve.wait_ge(s0.turned, 2 * i - 1 + u)
                    centre_dve(dve, s0, i, us)
                    deviation_dve(dve, s0, i, us)
                    for u in us:
                        inverse_dve(dve, s0, i, us, u)
                        if not is_first(i):
                            dve.wait_ge(s0.stored[u], 16 * i)
                            dve.wait_ge(s0.scattered[u], 16 * NC * i)
                        v.link(dve.tensor_tensor(n_c[u][:, :, :], n_c[u][:, :, :], wide(n_r[u][:, :]), ALU.mult))
                        dve.tensor_copy(r_x1[u][:, :, 0:D], n_c[u][:, :, :]).then_inc(s0.x1, 1)
                pairs(nc.vector, ECH, body, v)

            @block.scalar
            def _(act):
                act.wait_ge(s0.tanh_in, 1)
                nc.scalar.activation(heads[0][:, :], heads[0][:, :], ACT.Tanh, bias=gb[:, :]).then_inc(s0.tanh, 1)

                def body(i, us):
                    deviation_act(act, s0, i, us)
                    for u in us:
                        act.wait_ge(s0.turned, turn(i, 1, 0, u, us))
                        nc.scalar.copy(n_t[u][:, :], bank[u][:, 0:NC // 2 * P]).then_inc(s0.turned_sb, 1)
                    for u in us:
                        act.wait_ge(s0.terms, turn(i, 1, 0, u, us))
                        terms = bank[2 + u][0:P, 0:4 * NC].rearrange("p (c a) -> p c a", a=4)
                        nc.scalar.copy(chunk(own4[:, :, :], i, u), terms)
                        nc.scalar.copy(r_x1[u][:, :, D + 1:W1ROW], terms).then_inc(s0.row, 1)
                pairs(nc.scalar, ECH, body)

            @block.tensor
            def _(pe):
                carry_pe(pe, D, "sum")

                def body(i, us):
                    for u in us:
                        pe.wait_ge(s0.x1, turn(i, 1, 0, u, us))
                        transpose_pairs(pe, n_c[u], bank[u]).then_inc(s0.turned, 1)
                    for u in us:
                        pe.wait_ge(s0.turned_sb, turn(i, 1, 0, u, us))
                        if not is_first(i):
                            pe.wait_ge(s0.row, 2 * i - 1 + u)
                        for c in range(NC // 2):
                            done = pe.matmul(bank[2 + u][0:P, 8 * c:8 * c + 8], n_t[u][:, c * P:c * P + P], wa_pair[:, :], start=True, stop=True)
                        done.then_inc(s0.terms, 1)
                pairs(nc.tensor, ECH, body)

            def store_pass(sp, s, table, rows, width):
                def body(i, us):
                    for u in us:
                        sp.wait_ge(s.row, turn(i, 1, 0, u, us))
                        sp.dma_start(edge_rows(table, i, u, width), flat(rows[u][:, :, :])).then_inc(s.stored[u], 16)
                pairs(nc.sync, ECH, body)
                for u in range(U):
                    sp.wait_ge(s.stored[u], 16 * ((ECH + 1 - u) // 2))

            @block.sync
            def _(sp):
                store_pass(sp, s0, E1, r_x1, W1ROW)

            @block.gpsimd
            def _(g):
                scatter_pass(s0, [(s0.row, X1, r_x1, scat_i, s0.scattered)])(g)

        def attention_dve(dve, s, rows, at):
            for h in range(H):
                dve.tensor_copy(dens[h][:, :], own4[:, :, 2 + h])
                v.link(dve.tensor_tensor(selfs[h][:, :], own4[:, :, h], own4[:, :, 2 + h], ALU.add))
            for h in range(H):
                v.link(dve.scalar_tensor_tensor(selfs[h][:, :], selfs[h][:, :], 0.2, selfs[h][:, :], ALU.mult, ALU.max))
            over_segments(dve, "hold", [d[:, :] for d in dens])
            dve.wait_ge(s.gathered, ALL)
            for h in range(H):
                v.link(dve.tensor_tensor(heads[h][:, :], rows[:, :, at + h], dens[h][:, :], ALU.add))
                v.link(dve.scalar_tensor_tensor(heads[h][:, :], heads[h][:, :], 0.2, heads[h][:, :], ALU.mult, ALU.max))
                v.link(dve.tensor_copy(tops[h][:, :], heads[h][:, :]))
            over_segments(dve, "max", [t[:, :] for t in tops])
            for h in range(H):
                v.link(dve.tensor_tensor(tops[h][:, :], tops[h][:, :], selfs[h][:, :], ALU.max))
            over_segments(dve, "hold", [t[:, :] for t in tops])
            for h in range(H):
                dve.tensor_tensor(heads[h][:, :], heads[h][:, :], tops[h][:, :], ALU.subtract)
                v.link(dve.tensor_tensor(selfs[h][:, :], selfs[h][:, :], tops[h][:, :], ALU.subtract))
                done = dve.tensor_scalar(selfs[h][:, :], selfs[h][:, :], 0.0, None, ALU.min)
            done.then_inc(s.logits, 1)
            dve.wait_ge(s.exps, 1)
            for h in range(H):
                v.link(dve.tensor_copy(dens[h][:, :], heads[h][:, :]))
            over_segments(dve, "sum", [d[:, :] for d in dens])
            for h in range(H):
                v.link(dve.tensor_tensor(dens[h][:, :], dens[h][:, :], selfs[h][:, :], ALU.add))
                v.link(dve.tensor_scalar(dens[h][:, :], dens[h][:, :], 0.5, None, ALU.max))
                v.link(dve.reciprocal(dens[h][:, :], dens[h][:, :]))

        def attention_act(act, s):
            act.wait_ge(s.logits, 1)
            for t in (*heads, *selfs):
                done = nc.scalar.activation(t[:, :], t[:, :], ACT.Exp)
            done.then_inc(s.exps, 1)

        def attention_pe(pe):
            over_segments_pe(pe, "hold", 2)
            over_segments_pe(pe, "max", 2)
            over_segments_pe(pe, "hold", 2)
            over_segments_pe(pe, "sum", 2)

        s1 = phase("att1", "gathered logits exps x turned turned_sb h2 row", "loaded stored scattered")
        xa, vb = rows_of(0, W1ROW), rows_of(J * W1ROW, D)
        turned_pair = [[t[:, :] for t in n_t], [o1_t[:, b, :] for b in range(2)]]
        SHARE = 2 * J // 5
        GPSIMD_COLS, VECTOR_COLS = slice(0, SHARE), slice(SHARE, J)
        s_shared = sem("s_shared")

        def weigh1(eng, chain, at):
            chain.link(eng.tensor_tensor(vb[:, at, :], xa[:, at, 0:D], wide(heads[1][:, at]), ALU.mult))
            return eng.tensor_tensor(xa[:, at, 0:D], xa[:, at, 0:D], wide(heads[0][:, at]), ALU.mult)

        def weigh2(eng, chain, at):
            for h in range(H):
                part = ha[:, at, h * D:h * D + D]
                chain.link(eng.tensor_tensor(part, part, wide(heads[h][:, at]), ALU.mult))
            return eng.tensor_tensor(ha[:, at, 0:D], ha[:, at, 0:D], ha[:, at, D:2 * D], ALU.add)

        def weigh3(eng, chain, at):
            return eng.tensor_tensor(xc[:, at, :], xc[:, at, :], wide(heads[0][:, at]), ALU.mult)

        with nc.Block() as block:
            @block.gpsimd
            def _(g):
                g.iota(gray_i[:, :], pattern=[[1, SF]], base=0, channel_multiplier=SF).then_inc(s_sio, 1)
                gather(g, xa, X1, src_i, s1.gathered)
                g.wait_ge(s1.gathered, ALL)
                g.wait_ge(s1.exps, 1)
                weigh1(g, pool, GPSIMD_COLS).then_inc(s_shared, 1)
                scatter_pass(s1, [(s1.row, H2, r_h2, scat_i, s1.scattered)])(g)

            @block.vector
            def _(dve):
                sort_fill_dve(dve)
                sort_start_dve(dve)
                sort_dve(dve, PARTS[0], held[0], held[1])
                attention_dve(dve, s1, xa, D + 1)
                v.link(weigh1(dve, v, VECTOR_COLS))
                dve.wait_ge(s_shared, 1)
                sums = (xa[:, :, 0:D], vb)
                for h in range(H):
                    sum_rows_dve(dve, sums[h], carry_rows[h])

                def body(i, us):
                    for u in us:
                        dve.wait_ge(s1.loaded[u], 16 * i + 16)
                        if not is_first(i):
                            dve.wait_ge(s1.turned, 2 * i - 1 + u)
                        for h in range(H):
                            tmp = (n_sq, n_in)[h][u][:, :, :]
                            v.link(dve.tensor_tensor(tmp, r_x1[u][:, :, 0:D], wide(chunk(selfs[h], i, u)), ALU.mult))
                            add_carry(dve, n_out[u][:, :, :], sums[h], carry_rows[h], i, u, n_c[u][:, :, :])
                            v.link(dve.tensor_tensor(tmp, tmp, n_out[u][:, :, :], ALU.add))
                            done = dve.tensor_tensor(e_dup[u][:, :, h, :], tmp, wide(chunk(dens[h], i, u)), ALU.mult)
                        done.then_inc(s1.x, 1)
                pairs(nc.vector, ECH, body, v)

            @block.tensor
            def _(pe):
                sort_pe(pe, PARTS[0])
                attention_pe(pe)
                for _ in range(H):
                    carry_pe(pe, D, "sum")

                def body(i, us):
                    for u in us:
                        pe.wait_ge(s1.x, turn(i, 1, 0, u, us))
                        if not is_first(i):
                            pe.wait_ge(s1.turned_sb, 2 * i - 1 + u)
                        for c in range(NC):
                            done = pe.transpose(bank[2 * u + c // 4][:, c % 4 * P:(c % 4 + 1) * P], e_dup[u][:, c, :, :].rearrange("p h f -> p (h f)"), ident[0:P, 0:P])
                        done.then_inc(s1.turned, 1)
                    for u in us:
                        pe.wait_ge(s1.turned_sb, turn(i, 1, 0, u, us))
                        if u or not is_first(i):
                            pe.wait_ge(s1.row, 2 * i + u)
                        for c in range(NC):
                            if c % 3 == 0:
                                cols = min(3, NC - c) * W2ROW
                                add_bias(pe, bank[4 + c // 3][0:P, 0:cols], h2_bias[:, 0:cols])
                            done = pe.matmul(h2_slot(c), turned_pair[u][c // 4][:, c % 4 * P:c % 4 * P + P], heads_w[:, :],
                                             start=False, stop=c % 3 == 2 or c == NC - 1)
                        done.then_inc(s1.h2, 1)
                pairs(nc.tensor, ECH, body)

            @block.scalar
            def _(act):
                attention_act(act, s1)

                def body(i, us):
                    for u in us:
                        act.wait_ge(s1.turned, turn(i, 1, 0, u, us))
                        for b in range(2):
                            done = nc.scalar.copy(turned_pair[u][b], bank[2 * u + b][:, 0:NC // 2 * P])
                        done.then_inc(s1.turned_sb, 1)
                    for u in us:
                        act.wait_ge(s1.h2, turn(i, 1, 0, u, us))
                        if not is_first(i):
                            act.wait_ge(s1.stored[u], 16 * i)
                            act.wait_ge(s1.scattered[u], 16 * NC * i)
                        for b, cols in enumerate((3, 3, 2)):
                            at = bank[4 + b][0:P, 0:cols * W2ROW]
                            nc.scalar.copy(own4[:, bass.ds((2 * i + u) * NC + 3 * b, cols), :], at.rearrange("p (c w) -> p c w", w=W2ROW)[:, :, 2 * D:W2ROW])
                            done = nc.scalar.copy(flat(r_h2[u][:, 3 * b:3 * b + cols, :]), at)
                        done.then_inc(s1.row, 1)
                pairs(nc.scalar, ECH, body)

            @block.sync
            def _(sp):
                sort_sp(sp)

                def load(i, u):
                    sp.dma_start(flat(r_x1[u][:, :, :]), edge_rows(E1, i, u, W1ROW)).then_inc(s1.loaded[u], 16)

                def store(i, u):
                    sp.wait_ge(s1.row, 2 * i + u + 1)
                    sp.dma_start(edge_rows(E2, i, u, W2ROW), flat(r_h2[u][:, :, :])).then_inc(s1.stored[u], 16)

                def body(i, ahead):
                    for u in range(ahead):
                        sp.wait_ge(s1.x, 2 * i + u + 1)
                        load(i + 1, u)
                    for u in range(U):
                        store(i, u)
                for u in range(U):
                    load(0, u)
                with nc.sync.Fori(0, ECH // 2 - 1) as i:
                    body(i, U)
                body(ECH // 2 - 1, ECH % 2)
                if ECH % 2:
                    store(ECH // 2, 0)
                for u in range(U):
                    sp.wait_ge(s1.stored[u], 16 * ((ECH + 1 - u) // 2))

        s2 = phase("att2", "gathered logits exps weights centred squares var dev row", "loaded scattered")
        ha = rows_of(0, W2ROW)
        with nc.Block() as block:
            @block.gpsimd
            def _(g):
                gather(g, ha, H2, src_i, s2.gathered)
                g.wait_ge(s2.gathered, ALL)
                g.wait_ge(s2.weights, H)
                weigh2(g, pool, GPSIMD_COLS).then_inc(s_shared, 1)
                scatter_pass(s2, [(s2.row, X2, r_x2, scat_i, s2.scattered)])(g)

            @block.vector
            def _(dve):
                sort_resume_dve(dve)
                sort_dve(dve, PARTS[1], ki_srt, di_srt)
                attention_dve(dve, s2, ha, 2 * D)
                projected(dve)
                for h in range(H):
                    v.link(dve.scalar_tensor_tensor(selfs[h][:, :], selfs[h][:, :], 1.0 / H, dens[h][:, :], ALU.mult, ALU.mult))
                over_segments(dve, "hold", [d[:, :] for d in dens])
                for h in range(H):
                    dve.scalar_tensor_tensor(heads[h][:, :], heads[h][:, :], 1.0 / H, dens[h][:, :], ALU.mult, ALU.mult).then_inc(s2.weights, 1)
                dve.wait_ge(s2.weights, H)
                v.link(weigh2(dve, v, VECTOR_COLS))
                dve.wait_ge(s_shared, 2)
                sum_rows_dve(dve, ha[:, :, 0:D], carry_rows[0])

                def body(i, us):
                    for u in us:
                        dve.wait_ge(s2.loaded[u], 32 * i + 32)
                        y = n_in[u][:, :, :]
                        v.link(dve.tensor_tensor(y, r_h2[u][:, :, 0:D], wide(chunk(selfs[0], i, u)), ALU.mult))
                        v.link(dve.tensor_tensor(n_c[u][:, :, :], r_h2[u][:, :, D:2 * D], wide(chunk(selfs[1], i, u)), ALU.mult))
                        v.link(dve.tensor_tensor(y, y, n_c[u][:, :, :], ALU.add))
                        add_carry(dve, n_out[u][:, :, :], ha[:, :, 0:D], carry_rows[0], i, u, n_sq[u][:, :, :])
                        v.link(dve.tensor_tensor(y, y, n_out[u][:, :, :], ALU.add))
                        v.link(dve.tensor_tensor(y, y, r_x1[u][:, :, 0:D], ALU.add))
                        v.link(dve.tensor_tensor(y, y, tall(b2_all), ALU.add))
                    centre_dve(dve, s2, i, us)
                    deviation_dve(dve, s2, i, us)
                    for u in us:
                        inverse_dve(dve, s2, i, us, u)
                        if not is_first(i):
                            dve.wait_ge(s2.scattered[u], 16 * NC * i)
                        dve.tensor_tensor(r_x2[u][:, :, :], n_c[u][:, :, :], wide(n_r[u][:, :]), ALU.mult).then_inc(s2.row, 1)
                pairs(nc.vector, ECH, body, v)

            @block.tensor
            def _(pe):
                sort_pe(pe, PARTS[1])
                project_pe(pe)
                attention_pe(pe)
                over_segments_pe(pe, "hold", 2)
                carry_pe(pe, D, "sum")

            @block.scalar
            def _(act):
                act.wait_ge(s_sorted, 2)
                project_act(act)
                attention_act(act, s2)
                pairs(nc.scalar, ECH, lambda i, us: deviation_act(act, s2, i, us))

            @block.sync
            def _(sp):
                sort_store_sp(sp)
                project_sp(sp)

                def body(i, us):
                    for u in us:
                        if not is_first(i):
                            sp.wait_ge(s2.centred, 2 * i - 1 + u)
                        sp.dma_start(flat(r_x1[u][:, :, :]), edge_rows(E1, i, u, W1ROW)).then_inc(s2.loaded[u], 16)
                        sp.dma_start(flat(r_h2[u][:, :, :]), edge_rows(E2, i, u, W2ROW)).then_inc(s2.loaded[u], 16)
                pairs(nc.sync, ECH, body)

        s3 = phase("cos", "ordered outside norms roots logits exps centred squares var dev x3", "scattered")
        groups = list(zip(GROUPS, GROUPS[1:]))
        s3_got = [sem(f"s_cos_got{n}") for n in range(len(groups))]
        xr, xc = rows_of(0, D), rows_of(J * D, D)
        col_i = norm_s[:, :].bitcast(I32)
        with nc.Block() as block:
            @block.sync
            def _(sp):
                sp.wait_ge(s3.outside, 1)
                load_order(sp, SORTED[0, 0:EDGES], s3.ordered)
                sp.dma_start(col_i, edges_of(SORTED[1, 0:EDGES])).then_inc(s3.ordered, 16)
                x3_sp(sp)

            @block.gpsimd
            def _(g):
                g.wait_ge(s3.ordered, 6 * 16)
                for n, (start, end) in enumerate(groups):
                    cols = range(start * NC, end * NC)
                    gather(g, xr, X2, key_i, s3_got[n], cols)
                    gather(g, xc, X2, col_i, s3_got[n], cols)
                for n, (start, end) in enumerate(groups):
                    g.wait_ge(s3_got[n], 2 * 16 * NC * (end - start))
                g.wait_ge(s3.exps, 1)
                weigh3(g, pool, GPSIMD_COLS).then_inc(s_shared, 1)
                x3_stored(g)
                scatter_pass(s3, [(s3.x3, X3, r_x3, src_scat_i, s3.scattered)])(g)

            @block.vector
            def _(dve):
                dve.memset(prev_i[:, :], -1)
                dve.memset(next_i[:, :], -1).then_inc(s3.outside, 1)
                dve.wait_ge(s3.ordered, 6 * 16)
                order_dve(dve)
                last_only(dve, src_scat_i[:, :], heads[0][:, :])
                x3_dve(dve)
                for n, (start, end) in enumerate(groups):
                    dve.wait_ge(s3_got[n], 2 * 16 * NC * (end - start))
                    dots_dve(dve, ((n_sq[0], xr, xr, tops[0]), (n_sq[1], xc, xc, tops[1]), (n_in[0], xr, xc, heads[0])),
                             (start, end))
                dve.tensor_copy(dens[0][:, :], tops[0][:, :]).then_inc(s3.norms, 1)
                dve.wait_ge(s3.roots, 1)
                for t in tops:
                    v.link(dve.reciprocal(t[:, :], t[:, :]))
                    v.link(dve.tensor_tensor(heads[0][:, :], heads[0][:, :], t[:, :], ALU.mult))
                v.link(dve.tensor_scalar(heads[0][:, :], heads[0][:, :], beta_all[:, :], None, ALU.mult))
                v.link(dve.tensor_copy(tops[0][:, :], heads[0][:, :]))
                over_segments(dve, "max", [tops[0][:, :]])
                over_segments(dve, "hold", [tops[0][:, :]])
                dve.tensor_tensor(heads[0][:, :], heads[0][:, :], tops[0][:, :], ALU.subtract).then_inc(s3.logits, 1)
                dve.wait_ge(s3.exps, 1)
                v.link(dve.tensor_copy(dens[0][:, :], heads[0][:, :]))
                over_segments(dve, "sum", [dens[0][:, :]])
                v.link(dve.tensor_scalar(dens[0][:, :], dens[0][:, :], 1e-16, None, ALU.max))
                v.link(dve.reciprocal(dens[0][:, :], dens[0][:, :]))
                v.link(weigh3(dve, v, VECTOR_COLS))
                dve.wait_ge(s_shared, 3)
                sum_rows_dve(dve, xc, carry_rows[0])
                x3_stored(dve)

                def body(i, us):
                    for u in us:
                        add_carry(dve, n_in[u][:, :, :], xc, carry_rows[0], i, u, n_out[u][:, :, :])
                        v.link(dve.tensor_tensor(n_in[u][:, :, :], n_in[u][:, :, :], wide(chunk(dens[0], i, u)), ALU.mult))
                        v.link(dve.tensor_tensor(n_in[u][:, :, :], n_in[u][:, :, :], chunk(xr, i, u), ALU.add))
                    centre_dve(dve, s3, i, us)
                    deviation_dve(dve, s3, i, us)
                    for u in us:
                        inverse_dve(dve, s3, i, us, u)
                        if not is_first(i):
                            dve.wait_ge(s3.scattered[u], 16 * NC * i)
                        dve.tensor_tensor(r_x3[u][:, :, :], n_c[u][:, :, :], wide(n_r[u][:, :]), ALU.mult).then_inc(s3.x3, 1)
                pairs(nc.vector, ECH, body, v)

            @block.tensor
            def _(pe):
                segments_pe(pe)
                over_segments_pe(pe, "max", 1)
                over_segments_pe(pe, "hold", 1)
                over_segments_pe(pe, "sum", 1)
                carry_pe(pe, D, "sum")

            @block.scalar
            def _(act):
                x3_act(act)
                act.wait_ge(s3.norms, 1)
                for t in tops:
                    done = nc.scalar.activation(t[:, :], t[:, :], ACT.Sqrt, bias=eps8[0:P, :])
                done.then_inc(s3.roots, 1)
                act.wait_ge(s3.logits, 1)
                nc.scalar.activation(heads[0][:, :], heads[0][:, :], ACT.Exp).then_inc(s3.exps, 1)

                pairs(nc.scalar, ECH, lambda i, us: deviation_act(act, s3, i, us))

        s4 = phase("msg", "ordered outside gathered gathered_dst msg sum_turned sum_turned_sb y x centred squares var dev row", "loaded scattered")
        with nc.Block() as block:
            @block.sync
            def _(sp):
                sp.wait_ge(s4.outside, 1)
                load_order(sp, dst, s4.ordered)
                out_sp(sp, outs[0])

                def body(i, us):
                    for u in us:
                        if not is_first(i):
                            sp.wait_ge(s4.msg, 2 * i - 1 + u)
                        sp.dma_start(flat(n_in[u][:, :, :]), edge_rows(EP, i, u, D)).then_inc(s4.loaded[u], 16)
                pairs(nc.sync, ECH, body)
                out_sp(sp, outs[1])

            @block.gpsimd
            def _(g):
                gather(g, xs, X3, src_i, s4.gathered)
                gather(g, xd, X3, dst_i, s4.gathered_dst)
                for part in outs:
                    out_stored(g, part)
                scatter_pass(s4, [(s4.row, out, n_out, scat_i, s4.scattered)])(g)

            @block.vector
            def _(dve):
                dve.memset(prev_i[:, :], -1)
                dve.memset(next_i[:, :], -1).then_inc(s4.outside, 1)
                dve.wait_ge(s4.ordered, 5 * 16)
                order_dve(dve)
                out_dve(dve, outs[0])
                dve.wait_ge(s4.gathered, ALL)

                def message(i, us):
                    for u in us:
                        dve.wait_ge(s4.loaded[u], 16 * i + 16)
                        v.link(dve.tensor_tensor(n_sq[u][:, :, :], n_in[u][:, :, :], chunk(xs, i, u), ALU.add))
                        dve.tensor_scalar(chunk(xs, i, u), n_sq[u][:, :, :], 0.0, None, ALU.max).then_inc(s4.msg, 1)
                pairs(nc.vector, ECH, message, v)
                dve.wait_ge(s4.msg, ECH)
                sum_rows_dve(dve, xs, carry_rows[0])
                out_stored(dve, outs[0])
                out_dve(dve, outs[1])
                dve.wait_ge(s4.gathered_dst, ALL)
                out_stored(dve, outs[1])

                def body(i, us):
                    for u in us:
                        add_carry(dve, n_c[u][:, :, :], xs, carry_rows[0], i, u, n_sq[u][:, :, :])
                        dve.tensor_tensor(n_in[u][:, :, :], n_c[u][:, :, :], chunk(xd, i, u), ALU.add).then_inc(s4.x, 1)
                    for u in us:
                        dve.wait_ge(s4.y, turn(i, 1, 0, u, us))
                        v.link(dve.tensor_tensor(n_in[u][:, :, :], cols3(bank[2 + u][0:P, :]), chunk(xd, i, u), ALU.add))
                        v.link(dve.tensor_tensor(n_in[u][:, :, :], n_in[u][:, :, :], tall(bn_all), ALU.add))
                    centre_dve(dve, s4, i, us)
                    deviation_dve(dve, s4, i, us)
                    for u in us:
                        inverse_dve(dve, s4, i, us, u)
                        if not is_first(i):
                            dve.wait_ge(s4.scattered[u], 16 * NC * i)
                        dve.tensor_tensor(n_out[u][:, :, :], n_c[u][:, :, :], wide(n_r[u][:, :]), ALU.mult).then_inc(s4.row, 1)
                pairs(nc.vector, ECH, body, v)

            @block.tensor
            def _(pe):
                segments_pe(pe)
                out_pe(pe, outs[0])
                carry_pe(pe, D, "sum")
                pe.wait_ge(so.copied, 2 * OUT_SPLIT)
                out_pe(pe, outs[1])
                pe.wait_ge(so.copied, NCH)

                def body(i, us):
                    for u in us:
                        pe.wait_ge(s4.x, turn(i, 1, 0, u, us))
                        transpose_pairs(pe, n_in[u], bank[4 + u]).then_inc(s4.sum_turned, 1)
                    for u in us:
                        pe.wait_ge(s4.sum_turned_sb, turn(i, 1, 0, u, us))
                        product_pairs(pe, u, wn_diag, bank[2 + u]).then_inc(s4.y, 1)
                pairs(nc.tensor, ECH, body)

            @block.scalar
            def _(act):
                out_act(act, outs[0])
                act.wait_ge(s4.msg, ECH)
                out_act(act, outs[1])

                def body(i, us):
                    for u in us:
                        act.wait_ge(s4.sum_turned, turn(i, 1, 0, u, us))
                        nc.scalar.copy(n_t[u][:, :], bank[4 + u][:, 0:NC // 2 * P]).then_inc(s4.sum_turned_sb, 1)
                    deviation_act(act, s4, i, us)
                pairs(nc.scalar, ECH, body)

_INS = ['x', 'src', 'dst', 'edge_attr_64', 'L0_gnn_gate_w', 'L0_gnn_gate_b', 'L1_gnn_W1', 'L1_gnn_as1', 'L1_gnn_ad1', 'L1_gnn_b1', 'L1_gnn_W2', 'L1_gnn_as2', 'L1_gnn_ad2', 'L1_gnn_b2', 'L2_gnn_beta', 'L3_gnn_Wl', 'L3_gnn_bl', 'L3_gnn_Wn', 'L3_gnn_bn']


def kernel(**inputs):
    import numpy as np
    import concourse.bacc as bacc
    from concourse import mybir
    from concourse.bass_utils import run_bass_kernel_spmd

    nc = bacc.Bacc("TRN2", target_bir_lowering=False, num_devices=1)
    arrays, args = {}, []
    for name in _INS:
        a = np.ascontiguousarray(inputs[name])
        arrays[f"in_{name}_dram"] = a
        args.append(nc.dram_tensor(f"in_{name}_dram", a.shape, mybir.dt.from_np(a.dtype), kind="ExternalInput").ap())
    out = nc.dram_tensor("out_dram", (100000, 64), mybir.dt.float32, kind="ExternalOutput").ap()
    build(nc, *args, out)
    r = run_bass_kernel_spmd(nc, [arrays], core_ids=[0])
    return r.results[0]["out_dram"]
```
